# Optimizing a Trainium2 kernel written in Bass

```python
import numpy as np
import jax
import jax.numpy as jnp

def _softmax(x, axis=-1):
    return jax.nn.softmax(x, axis=axis)

def _gelu(x):
    return jax.nn.gelu(x, approximate=True)

def _silu(x):
    return jax.nn.silu(x)

def _sigmoid(x):
    return jax.nn.sigmoid(x)

def _layernorm(x, axis=-1, eps=1e-05):
    m = jnp.mean(x, axis=axis, keepdims=True)
    v = jnp.var(x, axis=axis, keepdims=True)
    return (x - m) / jnp.sqrt(v + eps)

def _scatter_add(tgt, idx, src, axis=0):
    return tgt.at[idx].add(src)

def _segment_sum(src, seg, n):
    return jax.ops.segment_sum(src, seg, n)
kernel_name = 'mk_xattn_ffn_d1_seqx_r4_750c02'

def setup_inputs(seed: int=0):
    np.random.seed(seed)
    _w = jnp.asarray

    def _rec_inputs():
        import jax
        import jax.numpy as jnp
        _rk = jax.random.key(seed)
        x = 7.22e-05 + 1 * jax.random.normal(jax.random.fold_in(_rk, 1), (16, 128, 512), jnp.float32)
        _lenS = 128 - jax.random.randint(jax.random.fold_in(_rk, 7), (16,), 0, max(1, 128 // 4) + 1, jnp.int32)
        _lenS2 = 128 - jax.random.randint(jax.random.fold_in(_rk, 8), (16,), 0, max(1, 128 // 4) + 1, jnp.int32)
        _ctx_2048P = jax.random.normal(jax.random.fold_in(_rk, 11), (16, 16, 512), jnp.float32)
        _ctx_2048c = jax.random.dirichlet(jax.random.fold_in(_rk, 511), 0.3 * jnp.ones((16,), jnp.float32), (16, 128))
        _ctx_2048t = jnp.einsum('bsk,bkd->bsd', _ctx_2048c, _ctx_2048P)
        _ctx_2048t = _ctx_2048t * jax.lax.rsqrt(jnp.mean(jnp.square(_ctx_2048t)) + 1e-12) * 0.953939
        ctx_2048 = 4.13588e-05 + 0.999923 * (_ctx_2048t + 0.3 * jax.random.normal(jax.random.fold_in(_rk, 611), (16, 128, 512), jnp.float32))
        return (x, ctx_2048)
    x, ctx_2048 = _rec_inputs()

    def _L0_xattn_setup():
        import jax, jax.numpy as jnp
        import numpy as np
        N, E, T, H = (8, 128, 512, 8)
        key = jax.random.key(seed)
        ks = jax.random.split(key, 6)
        s = 1.0 / np.sqrt(E)
        return {'mask': jax.random.normal(ks[0], (N, E, T), jnp.float32), 'encodings': jax.random.normal(ks[1], (N, E, T), jnp.float32), 'w_in': jax.random.normal(ks[2], (3 * E, E), jnp.float32) * s, 'b_in': jnp.zeros((3 * E,), jnp.float32), 'w_out': jax.random.normal(ks[3], (E, E), jnp.float32) * s, 'b_out': jnp.zeros((E,), jnp.float32), 'w_ct': jax.random.normal(ks[4], (E, E), jnp.float32) * s, 'b_ct': jnp.zeros((E,), jnp.float32), 'local_size': 64}
    _L0_xattn_all = _L0_xattn_setup()
    _L0_xattn_in = {k: v for k, v in _L0_xattn_all.items() if k in ('w_in', 'b_in', 'w_out', 'b_out', 'w_ct', 'b_ct')}
    del _L0_xattn_all

    def _L0_ffn_setup():
        import jax, jax.numpy as jnp
        import numpy as np
        TOPK = 2
        NORM_TOPK = True
        SCALE = 1.0
        EPS = 1e-09
        key = jax.random.key(seed)
        ks = jax.random.split(key, 9)
        h, i, E = (512, 256, 16)
        std = 0.02
        return {'x': jax.random.normal(ks[0], (1, 512, h), jnp.float32), 'Wr': jax.random.normal(ks[1], (E, h), jnp.float32) * std, 'bias': jnp.zeros((E,), jnp.float32), 'Wg': jax.random.normal(ks[2], (E, h, i), jnp.float32) * std, 'Wu': jax.random.normal(ks[3], (E, h, i), jnp.float32) * std, 'Wd': jax.random.normal(ks[4], (E, i, h), jnp.float32) * std, 'sWg': jax.random.normal(ks[5], (h, i), jnp.float32) * std, 'sWu': jax.random.normal(ks[6], (h, i), jnp.float32) * std, 'sWd': jax.random.normal(ks[7], (i, h), jnp.float32) * std}
    _L0_ffn_all = _L0_ffn_setup()
    _L0_ffn_in = {k: v for k, v in _L0_ffn_all.items() if k in ('Wr', 'bias', 'Wg', 'Wu', 'Wd', 'sWg', 'sWu', 'sWd')}
    del _L0_ffn_all
    return {'x': x, 'ctx_2048': ctx_2048, 'L0_xattn_w_in': _L0_xattn_in['w_in'], 'L0_xattn_b_in': _L0_xattn_in['b_in'], 'L0_xattn_w_out': _L0_xattn_in['w_out'], 'L0_xattn_b_out': _L0_xattn_in['b_out'], 'L0_xattn_w_ct': _L0_xattn_in['w_ct'], 'L0_xattn_b_ct': _L0_xattn_in['b_ct'], 'L0_ffn_Wr': _L0_ffn_in['Wr'], 'L0_ffn_bias': _L0_ffn_in['bias'], 'L0_ffn_Wg': _L0_ffn_in['Wg'], 'L0_ffn_Wu': _L0_ffn_in['Wu'], 'L0_ffn_Wd': _L0_ffn_in['Wd'], 'L0_ffn_sWg': _L0_ffn_in['sWg'], 'L0_ffn_sWu': _L0_ffn_in['sWu'], 'L0_ffn_sWd': _L0_ffn_in['sWd']}

def reference(x, ctx_2048, L0_xattn_w_in, L0_xattn_b_in, L0_xattn_w_out, L0_xattn_b_out, L0_xattn_w_ct, L0_xattn_b_ct, L0_ffn_Wr, L0_ffn_bias, L0_ffn_Wg, L0_ffn_Wu, L0_ffn_Wd, L0_ffn_sWg, L0_ffn_sWu, L0_ffn_sWd):
    import jax
    import jax.numpy as jnp

    def _L0_xattn_ref(mask, encodings, w_in, b_in, w_out, b_out, w_ct, b_ct, local_size):
        import jax, jax.numpy as jnp
        import numpy as np
        N, E, T, H = (8, 128, 512, 8)
        n, e, t = mask.shape
        d = e // H
        x = jnp.transpose(mask, (0, 2, 1))
        qkv = x @ w_in.T + b_in
        q, k, v = jnp.split(qkv, 3, axis=-1)
        q = q.reshape(n, t, H, d)
        k = k.reshape(n, t, H, d)
        v = v.reshape(n, t, H, d)
        scores = jnp.einsum('bqhd,bkhd->bhqk', q, k) / jnp.sqrt(jnp.asarray(d, q.dtype))
        idx = jnp.arange(t)
        band = jnp.abs(idx[:, None] - idx[None, :]) <= local_size
        neg = jnp.asarray(jnp.finfo(scores.dtype).min, scores.dtype)
        scores = jnp.where(band[None, None], scores, neg)
        attn = jax.nn.softmax(scores, axis=-1)
        o = jnp.einsum('bhqk,bkhd->bqhd', attn, v).reshape(n, t, e)
        o = o @ w_out.T + b_out
        o = jnp.transpose(o, (0, 2, 1))
        y = jax.nn.relu(o) * encodings
        out = jnp.einsum('nit,io->not', y, w_ct) + b_ct[None, :, None]
        return out

    def _L0_ffn_ref(x, Wr, bias, Wg, Wu, Wd, sWg, sWu, sWd):
        import jax, jax.numpy as jnp
        import numpy as np
        TOPK = 2
        NORM_TOPK = True
        SCALE = 1.0
        EPS = 1e-09
        b, s, h = x.shape
        E = Wr.shape[0]
        xt = x.reshape(b * s, h)
        logits = xt @ Wr.T + bias
        probs = jax.nn.softmax(logits, axis=-1)
        topk_val, topk_idx = jax.lax.top_k(probs, TOPK)
        if NORM_TOPK:
            w = topk_val / (jnp.sum(topk_val, axis=-1, keepdims=True) + EPS)
        else:
            w = topk_val
        w = w * SCALE
        g = jnp.einsum('th,ehi->tei', xt, Wg)
        u = jnp.einsum('th,ehi->tei', xt, Wu)
        y = jnp.einsum('tei,eih->teh', jax.nn.silu(g) * u, Wd)
        oh = jax.nn.one_hot(topk_idx, E, dtype=x.dtype)
        routed = jnp.einsum('tke,tk,teh->th', oh, w, y)
        shared = jax.nn.silu(xt @ sWg) * (xt @ sWu) @ sWd
        return (routed + shared).reshape(b, s, h)
    x = x + _L0_xattn_ref(_layernorm(x, axis=-1), ctx_2048, L0_xattn_w_in, L0_xattn_b_in, L0_xattn_w_out, L0_xattn_b_out, L0_xattn_w_ct, L0_xattn_b_ct, 64)
    x = x + _L0_ffn_ref(_layernorm(x, axis=-1), L0_ffn_Wr, L0_ffn_bias, L0_ffn_Wg, L0_ffn_Wu, L0_ffn_Wd, L0_ffn_sWg, L0_ffn_sWu, L0_ffn_sWd)
    return x

_drawn_inputs = setup_inputs


def setup_inputs(seed=0):
    import zlib

    import numpy as np

    out = dict(_drawn_inputs(seed))
    spreads = {'L0_xattn_b_in': (0.0, 0.1),
     'L0_xattn_b_out': (0.0, 0.1),
     'L0_xattn_b_ct': (0.0, 0.1),
     'L0_ffn_bias': (0.0, 0.1)}
    factors = {}
    for name, (base, spread) in spreads.items():
        noise = np.random.default_rng([zlib.crc32(name.encode()), seed]).standard_normal(out[name].shape)
        drawn = base * np.exp(spread * noise) if base else spread * noise
        out[name] = jnp.asarray(drawn.astype(out[name].dtype))
    for name, factor in factors.items():
        out[name] = (out[name] * factor).astype(out[name].dtype)
    return out
```

```python
from contextlib import ExitStack

import concourse.bass as bass
from concourse import mybir

F32 = mybir.dt.float32
BF16 = mybir.dt.bfloat16
I32 = mybir.dt.int32
ALU = mybir.AluOpType
ACT = mybir.ActivationFunctionType
AX = mybir.AxisListType

P = 128
SEQS, T = 16, 512
HEADS, D = 8, 16
LOCAL = 64
QB = T // P
EPS = 1e-5
EXPERTS, INNER = 16, 256
TOKENS = SEQS * P
BLOCKS = 2 * TOKENS // P + EXPERTS - 1
Q_PARTS = (0, 0, 1, 0, 1, 2)
K_PARTS = (0, 1, 0, 2, 1, 0)
STACK = 6 * D
UNITS = 2 * QB
MASKED = -1e38

C_ID, C_SEL, C_IOTA, C_REV, C_TILE, C_ONE, C_ROW1, C_SPARE, C_HALF, C_END = 0, 128, 384, 512, 528, 560, 576, 577, 578, 579
B_ID, B_MASK, B_TRI, B_ONES, B_ZERO, B_END = 0, 128, 384, 512, 640, 896
W_Q, W_K, W_V, W_O, W_CT, W_R, W_BIAS, W_END = 0, 128, 256, 384, 640, 768, 832, 840
BQ, BK, BV0, BV1, BO, BCT, BR = range(W_BIAS, W_BIAS + 7)
TABLE = 5 * BLOCKS


class Turn:

    def __init__(self, first, trip, step):
        self.first, self.trip, self.step = first, trip, step
        self.n = first if isinstance(trip, int) and trip == 0 else trip * step + first
        self.buf = first % step
        self.round = trip + first // step

    def plus(self, d):
        return Turn(self.first + d, self.trip, self.step)


def after(eng, sem, count):
    if isinstance(count, int) and count <= 0:
        return
    eng.wait_ge(sem, count)


def window(block):
    lo, hi = max(0, P * block - LOCAL), min(T, P * block + P + LOCAL)
    return lo, hi - lo, lo - (P * block - LOCAL)


def xattn_moe_kernel(nc, x, ctx_in, const_f, const_b, w_small, w_gu, w_d, sw_gu, sw_d, out):
    es = ExitStack()
    with es:
        def sb(name, shape, dt=F32):
            return es.enter_context(nc.sbuf_tensor(name, shape, dt))

        def sem(name):
            return es.enter_context(nc.semaphore(name))

        xn_rows = nc.dram_tensor("xn_rows", (TOKENS, T), F32).ap()
        out_rows = out.rearrange("a p t -> (a p) t")

        wgu = sb("wgu", [P, EXPERTS * 4 * 512])
        X = sb("X", [P, SEQS, T])
        cf = sb("cf", [P, C_END])
        cb = sb("cb", [P, B_END], BF16)
        logits = sb("logits", [P, SEQS, EXPERTS])
        swgu = sb("swgu", [P, 4, 512])
        swd = sb("swd", [P, 2, T])
        wd = sb("wd", [P, 2, 2, T])
        rows = sb("rows", [P, 2, T])
        rowsT = sb("rowsT", [P, 2, 4, P])
        act_in = sb("act_in", [P, 2, INNER])
        actT = sb("actT", [P, 2, 2, P])
        y_out = sb("y_out", [P, 2, T])

        used = [0]

        def over(shape, dt=F32):
            cols = 1
            for s in shape:
                cols *= s
            words = cols if dt is F32 else (cols + 1) // 2
            ap = wgu[:, used[0]:used[0] + words]
            used[0] += words
            assert used[0] <= EXPERTS * 4 * 512
            if dt is not F32:
                ap = ap.bitcast(dt)
            if len(shape) == 1:
                return ap
            names = " ".join("abc"[:len(shape)])
            return ap.rearrange(f"p ({names}) -> p {names}", **{"abc"[i]: s for i, s in enumerate(shape)})

        qstack = [over([HEADS, T], BF16) for _ in range(3)]
        kstack = [over([HEADS, T], BF16) for _ in range(3)]
        vaug = [over([QB, HEADS, 32]) for _ in range(3)]
        enc = [over([T]) for _ in range(3)]
        xn1 = over([T])
        qparts = over([3, T], BF16)
        kparts = over([3, T], BF16)
        qres = over([T])
        kres = over([T])
        probs = [over([4, 2 * P]) for _ in range(2)]
        ounorm = [over([T]) for _ in range(2)]
        onorm = [over([T]) for _ in range(2)]
        dens = over([HEADS * T // P])
        recips = over([HEADS * T // P])
        recip_rows = over([T])
        relu_o = over([T])
        gated = over([T])
        xn2 = over([T])
        xn2T = over([4, P])
        logitT = over([P])
        negmax = over([HEADS, QB])
        mres = over([HEADS * QB])
        mparts = over([3, HEADS * QB], BF16)
        mrows = over([P], BF16)
        wsm = over([W_END])
        beff = over([1])
        cb_f = over([B_END])
        stats = over([2, 6])
        moments = over([2, 2])
        rstd = over([2])
        epsd = over([2])

        top = sb("top", [P, 2, SEQS])
        pick = sb("pick", [P, 2, SEQS])
        hot = sb("hot", [P, 2, SEQS, EXPERTS], BF16)
        tmp = sb("tmp", [P, SEQS, EXPERTS])
        member = sb("member", [P, SEQS, EXPERTS], BF16)
        count = sb("count", [P, 4, EXPERTS])
        count_i = sb("count_i", [P, EXPERTS], I32)
        small = sb("small", [P, 6, SEQS * 2])
        small_i = sb("small_i", [P, 2, SEQS * 2], I32)
        gate_parts = sb("gate_parts", [P, 3, SEQS * 2], BF16)
        gate_res = sb("gate_res", [P, SEQS * 2])
        expert_of = sb("expert_of", [P, BLOCKS])
        expert_i = sb("expert_i", [P, BLOCKS], I32)
        slot = sb("slot", [P, 4, BLOCKS])
        gather_i = sb("gather_i", [P, BLOCKS], I32)
        scatter_i = sb("scatter_i", [P, BLOCKS], I32)
        gate_of = sb("gate_of", [P, BLOCKS])
        gather_now = sb("gather_now", [P, 2], I32)
        scatter_now = sb("scatter_now", [P, 2], I32)
        vals = sb("vals", [P, 2 * SEQS, 5])
        wd_flat = wd[:].rearrange("p a b c -> p (a b c)")
        hot_row = wd_flat[:, 0:512].bitcast(BF16).rearrange("p (q r) -> p q r", q=8)
        hot_col = wd_flat[:, 512:512 + 4 * TABLE].bitcast(BF16).rearrange("p (q g b) -> p q g b", q=8, g=5)
        before = wd_flat[:, 0:BLOCKS * EXPERTS].rearrange("p (b e) -> p b e", b=BLOCKS)
        table = wd_flat[:, 1500:1500 + TABLE]
        hot_block = wd_flat[:, 1750:1750 + 4 * BLOCKS].bitcast(BF16).rearrange("p (q b) -> p q b", q=8)

        bank = [es.enter_context(nc.psum_tensor(f"bank{i}", [P, 512], F32)) for i in range(8)]
        s1, s2, oacc, misc = bank[0:2], bank[2:4], bank[4:6], bank[6:8]

        consts_in, weights_in, shared_in = sem("consts_in"), sem("weights_in"), sem("shared_in")
        x_in = [sem(f"x_in{i}") for i in range(3)]
        enc_in = [sem(f"enc_in{i}") for i in range(3)]
        stack_in = [sem(f"stack_in{i}") for i in range(3)]
        max_in = [sem(f"max_in{i}") for i in range(3)]
        xn_stored = [sem(f"xn_stored{i}") for i in range(3)]
        experts_in = sem("experts_in")
        rows_in = [sem(f"rows_in{i}") for i in range(2)]
        wd_in = [sem(f"wd_in{i}") for i in range(2)]
        y_stored = [sem(f"y_stored{i}") for i in range(2)]
        gathered = [sem(f"gathered{i}") for i in range(2)]
        added = [sem(f"added{i}") for i in range(2)]
        spare_stored = sem("spare_stored")
        setup = sem("setup")
        beff_mm, beff_ready = sem("beff_mm"), sem("beff_ready")
        stats1, mom1, eps1, rstd1, xn1_ready = (sem(s) for s in ("stats1", "mom1", "eps1", "rstd1", "xn1_ready"))
        stats2, mom2, eps2, rstd2, xn2_ready = (sem(s) for s in ("stats2", "mom2", "eps2", "rstd2", "xn2_ready"))
        q_mm, k_mm, v_mm = sem("q_mm"), sem("k_mm"), sem("v_mm")
        q_p1, q_res, q_p2, q_p3 = sem("q_p1"), sem("q_res"), sem("q_p2"), sem("q_p3")
        k_p1, k_res, k_p2, k_p3 = sem("k_p1"), sem("k_res"), sem("k_p2"), sem("k_p3")
        v_ready = sem("v_ready")
        s1_ready, rowmax = sem("s1_ready"), sem("rowmax")
        m_step, m_mm, m_rows = sem("m_step"), sem("m_mm"), sem("m_rows")
        s2_ready, exp_ready, pv_done = sem("s2_ready"), sem("exp_ready"), sem("pv_done")
        o_copied = [sem(f"o_copied{i}") for i in range(2)]
        dens_in = [sem(f"dens_in{i}") for i in range(3)]
        recips_in = [sem(f"recips_in{i}") for i in range(3)]
        den_mm, recip_ready, o_ready = sem("den_mm"), sem("recip_ready"), sem("o_ready")
        proj_mm, relu_ready, gated_ready = sem("proj_mm"), sem("relu_ready"), sem("gated_ready")
        ct_mm, x2_ready = sem("ct_mm"), sem("x2_ready")
        xt_mm, xt_ready, router_mm, lt_ready, l_mm, l_ready = (
            sem(s) for s in ("xt_mm", "xt_ready", "router_mm", "lt_ready", "l_mm", "l_ready"))
        t_mm, t_ready, gu_mm, silu_ready, act_ready, at_mm, at_ready, dn_mm, y_ready = (
            sem(s) for s in ("t_mm", "t_ready", "gu_mm", "silu_ready", "act_ready", "at_mm", "at_ready",
                             "dn_mm", "y_ready"))
        route, shifted, exp_done = sem("route"), sem("shifted"), sem("exp_done")
        ranks_read, counts_read = sem("ranks_read"), sem("counts_read")
        gather_set, scatter_set = sem("gather_set"), sem("scatter_set")
        member_ready, rank_mm, hot_blocks, hot_ready, table_mm, tables_ready = (
            sem(s) for s in ("member_ready", "rank_mm", "hot_blocks", "hot_ready", "table_mm", "tables_ready"))

        ident = cf[:, C_ID:C_ID + P]
        identb = cb[:, B_ID:B_ID + P]

        def mask(blk):
            lo, w, off = window(blk)
            return cb[:, B_MASK + off:B_MASK + off + w]

        STACK_DMAS = 12 * 16

        DVE, PE, POOL, SP = (sem(f"passed_{e}") for e in ("dve", "pe", "pool", "sp"))

        def stand(eng, own, sem, count):
            after(eng, sem, count)
            if not isinstance(count, int):
                eng.sem_inc(own, 1)

        def attention_steps(eng, step):
            for i in range(-2, 4):
                step(Turn(i, 0, 3))
            with eng.Fori(0, 3) as trip:
                for k in range(3):
                    step(Turn(4 + k, trip, 3))
            for i in range(13, 19):
                step(Turn(i, 0, 3))

        def rowmax_unit(i, u):
            e = i if u < UNITS - 2 else i.plus(1)
            return (e, (u + 2) % UNITS) if has(e, 0) else None

        def has(i, d):
            return not isinstance(i.n, int) or 0 <= i.n + d < SEQS

        block = es.enter_context(nc.Block())

        @block.sync
        def _(sp):
            sp.dma_start(wsm, w_small).then_inc(weights_in, 16)
            sp.dma_start(X[:, 0, :], x[0]).then_inc(x_in[0], 16)
            sp.dma_start(cf[:], const_f).then_inc(consts_in, 16)
            sp.dma_start(cb_f, const_b).then_inc(consts_in, 16)
            sp.dma_start(X[:, 1:4, :], x[1:4].rearrange("n p t -> p n t")).then_inc(x_in[1], 16)
            sp.dma_start(X[:, 4:, :], x[4:].rearrange("n p t -> p n t")).then_inc(x_in[2], 16)
            sp.dma_start(swgu[:], sw_gu).then_inc(shared_in, 16)
            sp.dma_start(swd[:], sw_d).then_inc(shared_in, 16)

            def send(stack, parts, groups, sem):
                for g in groups:
                    which = (Q_PARTS if stack is qstack else K_PARTS)[g]
                    sp.dma_start(stack[sem[1]][D * g:D * g + D, :, :], parts[:, which, :]).then_inc(sem[0], 16)

            def step(i):
                d = i.plus(1)
                if has(i, -2):
                    c = i.plus(-2)
                    for g in range(2):
                        sp.wait_ge(o_copied[g], c.n + 1)
                        sp.dma_start(dens[64 * g:64 * g + 64, :], ounorm[g][D:P:32, :]).then_inc(dens_in[c.buf], 16)
                if has(i, 1):
                    stand(sp, SP, s2_ready, 2 * UNITS * (i.n - 1))
                    to = (stack_in[d.buf], d.buf)
                    sp.wait_ge(q_p1, d.n + 1)
                    send(qstack, qparts, (0, 1, 3), to)
                    sp.wait_ge(q_p2, d.n + 1)
                    send(qstack, qparts, (2, 4), to)
                    sp.wait_ge(q_p3, d.n + 1)
                    send(qstack, qparts, (5,), to)
                if has(i, -2):
                    sp.wait_ge(recip_ready, c.n + 1)
                    sp.dma_start(recip_rows[0:HEADS, :], recips).then_inc(recips_in[c.buf], 16)
                if has(i, 1):
                    sp.wait_ge(k_p1, d.n + 1)
                    send(kstack, kparts, (0, 2, 5), to)
                    sp.wait_ge(k_p2, d.n + 1)
                    send(kstack, kparts, (1, 4), to)
                    sp.wait_ge(k_p3, d.n + 1)
                    send(kstack, kparts, (3,), to)
                if has(i, 0):
                    after(sp, gated_ready, i.n - 2)
                    sp.dma_start(enc[i.buf], ctx_in[bass.ds(i.n, 1), :, :].rearrange("a p t -> (a p) t")
                                 ).then_inc(enc_in[i.buf], 16)
                    sp.wait_ge(m_rows, i.n + 1)
                    sp.dma_start(qstack[i.buf][STACK:STACK + 3, :, :], mrows[0:96, :]).then_inc(max_in[i.buf], 16)
                if has(i, -2):
                    sp.wait_ge(xn2_ready, c.n + 1)
                    sp.dma_start(xn_rows[bass.ds(c.n * P, P), :], xn2).then_inc(xn_stored[c.buf], 16)

            attention_steps(sp, step)

            sp.wait_ge(l_ready, SEQS)
            for b in range(3):
                sp.wait_ge(xn_stored[b], 16 * len(range(b, SEQS, 3)))
            for e in range(EXPERTS):
                sp.wait_ge(t_mm, e + 1)
                sp.dma_start(wgu[:, e * 2048:(e + 1) * 2048], w_gu[:, e, :]).then_inc(experts_in, 16)

            sp.wait_ge(tables_ready, 1)

            def load_wd(k):
                stand(sp, SP, dn_mm, k.n - 1)
                e = sp.value_load(expert_i[0:1, bass.ds(k.n - SEQS, 1)], min_val=0, max_val=EXPERTS - 1)
                sp.dma_start(wd[:, k.buf, :, :].rearrange("p c n -> p (c n)"),
                             w_d[bass.ds(e, 1), :, :].rearrange("a p n -> (a p) n")).then_inc(wd_in[k.buf], 16)

            with sp.Fori(0, BLOCKS // 2) as trip:
                for k in range(2):
                    load_wd(Turn(SEQS + k, trip, 2))
            load_wd(Turn(SEQS + BLOCKS - 1, 0, 2))

        @block.gpsimd
        def _(pool):
            pool.wait_ge(consts_in, 32)

            def inverse_deviation(which, n, mom, eps, out_sem):
                stand(pool, POOL, mom, n + 1)
                nc.gpsimd.tensor_scalar(epsd[:, which:which + 1], moments[:, which, 1:2], EPS, None,
                                        ALU.add).then_inc(eps, 1)
                pool.wait_ge(eps, n + 1)
                nc.gpsimd.tensor_tensor(rstd[:, which:which + 1], epsd[:, which:which + 1],
                                        cf[:, C_HALF:C_HALF + 1], ALU.pow).then_inc(out_sem, 1)

            def parts(n, res, to, res_sem, p2_sem, p3_sem):
                stand(pool, POOL, res_sem, n + 1)
                nc.gpsimd.tensor_copy(to[:, 1, :], res).then_inc(p2_sem, 1)
                pool.wait_ge(p2_sem, n + 1)
                nc.gpsimd.tensor_tensor(to[:, 2, :], res, to[:, 1, :], ALU.subtract).then_inc(p3_sem, 1)

            def step(i):
                if has(i, 1):
                    d = i.plus(1)
                    parts(d.n, qres, qparts, q_res, q_p2, q_p3)
                    parts(d.n, kres, kparts, k_res, k_p2, k_p3)
                if has(i, 2):
                    inverse_deviation(0, i.n + 2, mom1, eps1, rstd1)
                if has(i, -2):
                    inverse_deviation(1, i.n - 2, mom2, eps2, rstd2)

            attention_steps(pool, step)

            pool.wait_ge(tables_ready, 1)

            def gather(k):
                stand(pool, POOL, gathered[k.buf], 16 * (k.round - SEQS // 2))
                nc.gpsimd.tensor_copy(gather_now[:, k.buf:k.buf + 1],
                                      gather_i[:, bass.ds(k.n - SEQS, 1)]).then_inc(gather_set, 1)
                pool.wait_ge(gather_set, k.n - SEQS + 1)
                stand(pool, POOL, t_mm, k.n - 1)
                nc.gpsimd.indirect_dma_start(
                    rows[:, k.buf, :], None, xn_rows[:, :],
                    bass.IndirectOffsetOnAxis(ap=gather_now[:, k.buf:k.buf + 1], axis=0),
                    bounds_check=TOKENS - 1, oob_is_err=True).then_inc(gathered[k.buf], 16)

            def add_rows(k):
                for b in range(2):
                    stand(pool, POOL, added[b], 16 * ((k.round if b or not k.buf else k.round + 1) - SEQS // 2))
                nc.gpsimd.tensor_copy(scatter_now[:, k.buf:k.buf + 1],
                                      scatter_i[:, bass.ds(k.n - SEQS, 1)]).then_inc(scatter_set, 1)
                stand(pool, POOL, scatter_set, k.n - SEQS + 1)
                stand(pool, POOL, y_ready, k.n + 1)
                nc.gpsimd.indirect_dma_start(
                    out_rows[:, :], bass.IndirectOffsetOnAxis(ap=scatter_now[:, k.buf:k.buf + 1], axis=0),
                    y_out[:, k.buf, :], None, bounds_check=TOKENS + P - 1, oob_is_err=True,
                    compute_op=ALU.add).then_inc(added[k.buf], 16)

            AHEAD = 4
            for k in range(AHEAD):
                gather(Turn(SEQS + k, 0, 2))
            pool.wait_ge(spare_stored, 16)
            for b in range(2):
                pool.wait_ge(y_stored[b], 16 * (SEQS // 2))
            for k in range(2):
                add_rows(Turn(SEQS + k, 0, 2))
                gather(Turn(SEQS + AHEAD + k, 0, 2))
            with pool.Fori(0, (BLOCKS - AHEAD) // 2 - 1) as trip:
                for k in range(2):
                    add_rows(Turn(SEQS + 2 + k, trip, 2))
                    gather(Turn(SEQS + 2 + AHEAD + k, trip, 2))
            for k in range((BLOCKS - AHEAD) // 2 * 2, BLOCKS):
                add_rows(Turn(SEQS + k, 0, 2))
                if k + AHEAD < BLOCKS:
                    gather(Turn(SEQS + AHEAD + k, 0, 2))
            for b in range(2):
                pool.wait_ge(added[b], 16 * len(range(b, BLOCKS, 2)))

        @block.tensor
        def _(pe):
            mm = nc.tensor.matmul

            pe.wait_ge(weights_in, 16)
            for g in range(2):
                last = mm(misc[0][:, 0:1], wsm[:, W_O + P * g:W_O + P * g + P], wsm[:, BV0 + g:BV0 + g + 1],
                          start=(g == 0), stop=(g == 1))
            last.then_inc(beff_mm, 1)
            pe.wait_ge(consts_in, 32)
            pe.wait_ge(setup, 7)

            def step(i):
                b, c, d, e = i.plus(-1), i.plus(-2), i.plus(1), i.plus(-3)
                for u in range(UNITS):
                    if rowmax_unit(i, u):
                        a, au = rowmax_unit(i, u)
                        blk, hg = au // 2, au % 2
                        lo, w, _ = window(blk)
                        if au == 0:
                            pe.wait_ge(stack_in[a.buf], STACK_DMAS * (a.round + 1))
                        for half in range(2):
                            r = 2 * UNITS * a.n + 2 * au + half
                            after(pe, rowmax, r - 1)
                            for j in range(2):
                                h = 4 * hg + 2 * half + j
                                o = s1[half][:, 256 * j:256 * j + w]
                                mm(o, qstack[a.buf][0:STACK, h, P * blk:P * blk + P],
                                   kstack[a.buf][0:STACK, h, lo:lo + w], start=True, stop=False)
                                last = mm(o, identb, mask(blk), start=False, stop=True)
                            last.then_inc(s1_ready, 1)
                    if has(i, -1):
                        blk, hg = u // 2, u % 2
                        lo, w, _ = window(blk)
                        if u == 0:
                            pe.wait_ge(max_in[b.buf], 16 * (b.round + 1))
                        for half in range(2):
                            r = 2 * UNITS * b.n + 2 * u + half
                            after(pe, exp_ready, r - 1)
                            for j in range(2):
                                h = 4 * hg + 2 * half + j
                                o = s2[half][:, 256 * j:256 * j + w]
                                mm(o, kstack[b.buf][0:STACK + 3, h, P * blk:P * blk + P],
                                   qstack[b.buf][0:STACK + 3, h, lo:lo + w], start=True, stop=False)
                                last = mm(o, identb, mask(blk), start=False, stop=True)
                            last.then_inc(s2_ready, 1)
                        if u >= 1:
                            attend_values(b, u - 1)
                    between(i, u)
                if has(i, -1):
                    attend_values(b, UNITS - 1)
                if has(i, -3):
                    stand(pe, PE, lt_ready, e.n + 1)
                    nc.tensor.transpose(misc[1][:, 0:EXPERTS], logitT[0:EXPERTS, :],
                                        cf[0:EXPERTS, C_ID:C_ID + EXPERTS]).then_inc(l_mm, 1)

            def between(i, u):
                a, b, c, d, e = i, i.plus(-1), i.plus(-2), i.plus(1), i.plus(-3)
                if u == 0 and has(i, 1):
                    pe.wait_ge(xn1_ready, d.n + 1)
                    if d.n if isinstance(d.n, int) else True:
                        after(pe, k_res, d.n)
                    after(pe, m_rows, d.n - 1)
                    after(pe, l_ready, d.n - 4)
                    mm(misc[1][:], wsm[:, W_Q:W_Q + P], xn1, start=True, stop=True).then_inc(q_mm, 1)
                if u == 1 and has(i, 1):
                    after(pe, v_ready, d.n)
                    after(pe, lt_ready, d.n - 4)
                    if isinstance(d.n, int) and d.n == 0:
                        pe.wait_ge(beff_ready, 1)
                    for k in range(QB):
                        last = mm(misc[0][:, P * k:P * k + P], xn1[:, P * k:P * k + P], wsm[:, W_V:W_V + P],
                                  start=True, stop=True)
                    last.then_inc(v_mm, 1)
                if u == 2 and has(i, 1):
                    pe.wait_ge(q_res, d.n + 1)
                    mm(misc[1][:], wsm[:, W_K:W_K + P], xn1, start=True, stop=True).then_inc(k_mm, 1)
                if u == 3 and has(i, -2):
                    pe.wait_ge(recips_in[c.buf], 16 * (c.round + 1))
                    if has(i, 1):
                        pe.wait_ge(v_ready, d.n + 1)
                        pe.wait_ge(k_res, d.n + 1)
                    else:
                        after(pe, l_ready, c.n - 1)
                    for g in range(2):
                        mm(misc[g][:], cf[0:HEADS, C_SEL + P * g:C_SEL + P * g + P], recip_rows[0:HEADS, :],
                           start=True, stop=True).then_inc(den_mm, 1)
                if u == 4 and has(i, -2):
                    pe.wait_ge(o_ready, 2 * c.n + 2)
                    for g in range(2):
                        last = mm(misc[0][:], wsm[:, W_O + P * g:W_O + P * g + P], onorm[g],
                                  start=(g == 0), stop=(g == 1))
                    last.then_inc(proj_mm, 1)
                if u == 5 and has(i, -3):
                    pe.wait_ge(xn2_ready, e.n + 1)
                    after(pe, l_ready, e.n)
                    for k in range(4):
                        last = nc.tensor.transpose(misc[1][:, P * k:P * k + P], xn2[:, P * k:P * k + P], ident)
                    last.then_inc(xt_mm, 1)
                if u == 6 and has(i, -2):
                    pe.wait_ge(gated_ready, c.n + 1)
                    mm(misc[0][:], wsm[:, W_CT:W_CT + P], gated, start=True, stop=True).then_inc(ct_mm, 1)
                if u == 6 and has(i, 0):
                    if has(i, -3):
                        pe.wait_ge(xt_ready, e.n + 1)
                    elif has(i, 1):
                        pe.wait_ge(k_res, d.n + 1)
                    pe.wait_ge(m_step, 4 * (a.n + 1))
                    nc.tensor.transpose(misc[1][:].bitcast(BF16)[0:96, 0:P],
                                        mparts.rearrange("p a b -> p (a b)"), identb).then_inc(m_mm, 1)
                if u == 7 and has(i, -3):
                    pe.wait_ge(xt_ready, e.n + 1)
                    if has(i, -2):
                        pe.wait_ge(x2_ready, c.n + 1)
                    if has(i, 0):
                        pe.wait_ge(m_rows, a.n + 1)
                    for k in range(4):
                        last = mm(misc[0][0:EXPERTS, 0:P], wsm[:, W_R + 16 * k:W_R + 16 * k + 16], xn2T[:, k, :],
                                  start=(k == 0), stop=(k == 3))
                    last.then_inc(router_mm, 1)

            def attend_values(b, u):
                blk, hg = u // 2, u % 2
                lo, w, _ = window(blk)
                pe.wait_ge(exp_ready, 2 * UNITS * b.n + 2 * u + 2)
                if u == 0:
                    pe.wait_ge(v_ready, b.n + 1)
                if blk == 0:
                    after(pe, o_copied[hg], b.n)
                for j in range(4):
                    last = mm(oacc[hg][32 * j:32 * j + 32, lo:lo + w], vaug[b.buf][:, blk, 4 * hg + j, :],
                              probs[u % 2][:, j, 0:w], start=(blk == 0), stop=(blk == QB - 1),
                              skip_group_check=True)
                last.then_inc(pv_done, 1)

            attention_steps(pe, step)

            tb, gb, ab, yb, rb = bank[0:2], bank[2:4], bank[4], bank[5:7], bank[7]
            pe.wait_ge(l_ready, SEQS)

            def turn_rows(k, shared):
                if shared:
                    pe.wait_ge(rows_in[k.buf], 16 * (k.round + 1))
                else:
                    pe.wait_ge(gathered[k.buf], 16 * (k.round - SEQS // 2 + 1))
                after(pe, t_ready, k.n - 1)
                for c in range(4):
                    last = nc.tensor.transpose(tb[k.buf][:, P * c:P * c + P], rows[:, k.buf, P * c:P * c + P], ident)
                last.then_inc(t_mm, 1)

            def gate_up(k, shared):
                pe.wait_ge(t_ready, k.n + 1)
                after(pe, act_ready, k.n - 1)
                if not shared:
                    e = pe.value_load(expert_i[0:1, bass.ds(k.n - SEQS, 1)], min_val=0, max_val=EXPERTS - 1)
                for c in range(4):
                    w = swgu[:, c, :] if shared else wgu[:, bass.ds(e * 2048 + 512 * c, 512)]
                    last = mm(gb[k.buf][:], rowsT[:, k.buf, c, :], w, start=(c == 0), stop=(c == 3))
                last.then_inc(gu_mm, 1)

            def turn_act(k):
                pe.wait_ge(act_ready, k.n + 1)
                after(pe, at_ready, k.n - 1)
                for c in range(2):
                    o = INNER * k.buf + P * c
                    last = nc.tensor.transpose(ab[:, o:o + P], act_in[:, k.buf, P * c:P * c + P], ident)
                last.then_inc(at_mm, 1)

            def down(k, shared):
                pe.wait_ge(at_ready, k.n + 1)
                after(pe, y_ready, k.n - 1)
                if not shared:
                    pe.wait_ge(wd_in[k.buf], 16 * (k.round - SEQS // 2 + 1))
                for c in range(2):
                    w = swd[:, c, :] if shared else wd[:, k.buf, c, :]
                    last = mm(yb[k.buf][:], actT[:, k.buf, c, :], w, start=(c == 0), stop=(c == 1))
                last.then_inc(dn_mm, 1)

            def ranks():
                pe.wait_ge(member_ready, 1)
                tri, ones = cb[:, B_TRI:B_TRI + P], cb[:, B_ONES:B_ONES + P]
                m = member[:].rearrange("p n e -> p (n e)")
                mm(rb[:, 0:256], tri, m, start=True, stop=False)
                for t in range(SEQS - 1):
                    later = SEQS - 1 - t
                    last = mm(rb[:, 16 * (t + 1):256].rearrange("p (n e) -> p n e", e=EXPERTS), ones,
                              member[:, t:t + 1, :].to_broadcast([P, later, EXPERTS]),
                              start=False, stop=(later == 1))
                last.then_inc(rank_mm, 1)
                pe.wait_ge(ranks_read, 1)
                for t in range(SEQS):
                    last = mm(rb[:, 0:EXPERTS], ones, member[:, t, :], start=(t == 0), stop=(t == SEQS - 1))
                last.then_inc(rank_mm, 1)
                pe.wait_ge(counts_read, 1)
                mm(rb[:, 0:TABLE], ones, cb[:, B_ZERO:B_ZERO + TABLE], start=True,
                   stop=False).then_inc(table_mm, 1)

            def chunk(trip):
                pe.wait_ge(hot_ready, trip + 1)
                for q in range(8):
                    last = mm(rb[:, 0:TABLE], hot_row[:, q, :], hot_col[:, q, :, :].rearrange("p g b -> p (g b)"),
                              start=False, stop=False)
                last.then_inc(table_mm, 1)

            def tables():
                mm(rb[:, 0:TABLE], cb[:, B_ONES:B_ONES + P], cb[:, B_ZERO:B_ZERO + TABLE], start=False,
                   stop=True).then_inc(table_mm, 1)

            pe.wait_ge(shared_in, 32)
            turn_rows(Turn(0, 0, 2), True)

            def pe_step(k, shared):
                if not shared and k.first == SEQS:
                    pe.wait_ge(experts_in, 16 * EXPERTS)
                gate_up(k, shared)
                prev = k.plus(-1)
                prev_shared = shared or (k.first == SEQS and isinstance(k.trip, int))
                turn_act(prev)
                if not (isinstance(k.n, int) and k.n == SEQS + BLOCKS - 1):
                    turn_rows(k.plus(1), shared and not (isinstance(k.n, int) and k.n == SEQS - 1))
                down(prev, prev_shared)

            gate_up(Turn(0, 0, 2), True)
            turn_rows(Turn(1, 0, 2), True)
            pe_step(Turn(1, 0, 2), True)
            for k in range(2, 6):
                pe_step(Turn(k, 0, 2), True)
            ranks()
            with pe.Fori(0, 4) as trip:
                for k in range(2):
                    pe_step(Turn(6 + k, trip, 2), True)
                chunk(trip)
            tables()
            pe_step(Turn(14, 0, 2), True)
            pe_step(Turn(15, 0, 2), True)
            pe_step(Turn(16, 0, 2), False)
            pe_step(Turn(17, 0, 2), False)
            with pe.Fori(0, (BLOCKS - 3) // 2) as trip:
                for k in range(2):
                    pe_step(Turn(SEQS + 2 + k, trip, 2), False)
            pe_step(Turn(SEQS + BLOCKS - 1, 0, 2), False)
            turn_act(Turn(SEQS + BLOCKS - 1, 0, 2))
            down(Turn(SEQS + BLOCKS - 1, 0, 2), False)

        @block.scalar
        def _(act):
            act.wait_ge(weights_in, 16)
            act.wait_ge(beff_mm, 1)
            nc.scalar.activation(beff, misc[0][:, 0:1], ACT.Identity, bias=wsm[:, BO:BO + 1]).then_inc(beff_ready, 1)
            act.wait_ge(beff_ready, 1)

            def step(i):
                b, c, d, e = i.plus(-1), i.plus(-2), i.plus(1), i.plus(-3)
                for u in range(UNITS):
                    if has(i, -1):
                        blk = u // 2
                        _, w, _ = window(blk)
                        after(act, pv_done, UNITS * b.n + u - 1)
                        for half in range(2):
                            act.wait_ge(s2_ready, 2 * UNITS * b.n + 2 * u + half + 1)
                            nc.scalar.activation(
                                probs[u % 2][:, 2 * half:2 * half + 2, 0:w],
                                s2[half][:].rearrange("p (j c) -> p j c", j=2)[:, :, 0:w],
                                ACT.Exp, scale=D ** -0.5).then_inc(exp_ready, 1)
                    if u == 0 and has(i, 1):
                        act.wait_ge(q_mm, d.n + 1)
                        first_part_free(d)
                        nc.scalar.activation(qparts[:, 0, :], misc[1][:], ACT.Identity,
                                             bias=wsm[:, BQ:BQ + 1]).then_inc(q_p1, 1)
                    if u == 2 and has(i, 1):
                        act.wait_ge(k_mm, d.n + 1)
                        nc.scalar.activation(kparts[:, 0, :], misc[1][:], ACT.Identity,
                                             bias=wsm[:, BK:BK + 1]).then_inc(k_p1, 1)
                    if u == 4 and has(i, -2):
                        act.wait_ge(proj_mm, c.n + 1)
                        after(act, gated_ready, c.n)
                        nc.scalar.activation(relu_o, misc[0][:], ACT.Relu, bias=beff).then_inc(relu_ready, 1)
                    if u == 5 and has(i, -3):
                        act.wait_ge(xt_mm, e.n + 1)
                        nc.scalar.copy(xn2T.rearrange("p a b -> p (a b)"), misc[1][:]).then_inc(xt_ready, 1)
                if has(i, -3):
                    act.wait_ge(router_mm, e.n + 1)
                    nc.scalar.activation(logitT[0:EXPERTS, :], misc[0][0:EXPERTS, 0:P], ACT.Identity,
                                         bias=wsm[0:EXPERTS, BR:BR + 1]).then_inc(lt_ready, 1)
                if has(i, -1):
                    for hg in range(2):
                        act.wait_ge(pv_done, UNITS * b.n + UNITS - 1 + hg)
                        after(act, o_ready, 2 * b.n)
                        nc.scalar.copy(ounorm[hg], oacc[hg][:]).then_inc(o_copied[hg], 1)

            def first_part_free(d):
                prev = d.plus(-1)
                if not isinstance(d.n, int) or d.n >= 1:
                    act.wait_ge(stack_in[prev.buf], STACK_DMAS * (prev.round + 1))

            attention_steps(act, step)

            tb, gb, ab = bank[0:2], bank[2:4], bank[4]
            act.wait_ge(setup, 8)
            act.dma_start(out_rows[TOKENS:TOKENS + P, :], y_out[:, 1, :]).then_inc(spare_stored, 16)
            for b in range(3):
                act.wait_ge(xn_stored[b], 16 * len(range(b, SEQS, 3)))

            def load_rows(k):
                after(act, t_mm, k.n - 1)
                act.dma_start(rows[:, k.buf, :], xn_rows[bass.ds(k.n * P, P), :]).then_inc(rows_in[k.buf], 16)

            def rows_copy(k):
                act.wait_ge(t_mm, k.n + 1)
                after(act, gu_mm, k.n - 1)
                nc.scalar.copy(rowsT[:, k.buf, :, :].rearrange("p a b -> p (a b)"), tb[k.buf][:]).then_inc(t_ready, 1)

            def act_copy(k):
                act.wait_ge(at_mm, k.n + 1)
                after(act, dn_mm, k.n - 1)
                nc.scalar.copy(actT[:, k.buf, :, :].rearrange("p a b -> p (a b)"),
                               ab[:, INNER * k.buf:INNER * k.buf + INNER]).then_inc(at_ready, 1)

            def silu(k):
                act.wait_ge(gu_mm, k.n + 1)
                after(act, at_mm, k.n - 1)
                nc.scalar.activation(act_in[:, k.buf, :], gb[k.buf][:, 0:INNER], ACT.Silu).then_inc(silu_ready, 1)

            def store_shared(k):
                act.wait_ge(y_ready, k.n + 1)
                act.dma_start(out_rows[bass.ds(k.n * P, P), :], y_out[:, k.buf, :]).then_inc(y_stored[k.buf], 16)

            load_rows(Turn(0, 0, 2))
            load_rows(Turn(1, 0, 2))
            act.wait_ge(shifted, 1)
            nc.scalar.activation(logits[:], logits[:], ACT.Exp).then_inc(exp_done, 1)
            rows_copy(Turn(0, 0, 2))

            def step_experts(k, load, store):
                act_copy(k.plus(-1))
                rows_copy(k.plus(1))
                if load:
                    load_rows(k.plus(2))
                silu(k)
                if store:
                    store_shared(k.plus(-1))

            rows_copy(Turn(1, 0, 2))
            load_rows(Turn(2, 0, 2))
            silu(Turn(0, 0, 2))
            step_experts(Turn(1, 0, 2), True, True)
            for k in range(2, 4):
                step_experts(Turn(k, 0, 2), True, True)
            with act.Fori(0, 5) as trip:
                for k in range(2):
                    step_experts(Turn(4 + k, trip, 2), True, True)
            for k in range(14, 17):
                step_experts(Turn(k, 0, 2), False, True)
            with act.Fori(0, (BLOCKS - 3) // 2) as trip:
                for k in range(2):
                    step_experts(Turn(SEQS + 1 + k, trip, 2), False, False)
            step_experts(Turn(SEQS + BLOCKS - 2, 0, 2), False, False)
            last = Turn(SEQS + BLOCKS - 1, 0, 2)
            act_copy(last.plus(-1))
            silu(last)
            act_copy(last)

        @block.vector
        def _(dve):
            v = nc.vector
            for b in range(3):
                v.memset(kstack[b][STACK:STACK + 3, :, :], 1.0).then_inc(setup, 1)
                v.memset(vaug[b][:, :, :, D:2 * D], 1.0).then_inc(setup, 1)
            dve.wait_ge(consts_in, 32)
            v.tensor_copy(cb[:], cb_f).then_inc(setup, 1)
            v.memset(y_out[:, 1, :], 0.0).then_inc(setup, 1)
            dve.wait_ge(weights_in, 16)

            def normalise(which, n, src, dst, rstd_sem, ready):
                dve.wait_ge(rstd_sem, n + 1)
                v.tensor_scalar(dst, src, moments[:, which, 0:1], rstd[:, which:which + 1],
                                ALU.subtract, ALU.mult).then_inc(ready, 1)

            def moments_of(which, n, src, st, mom, before):
                stand(dve, DVE, before, n)
                v.bn_stats(stats[:, which, :], src).then_inc(st, 1)
                stand(dve, DVE, st, n + 1)
                v.bn_aggr(moments[:, which, :], stats[:, which, :]).then_inc(mom, 1)

            def seq(n):
                return X[:, bass.ds(n, 1), :].rearrange("p a t -> p (a t)")

            def step(i):
                a, c, d, e, f = i, i.plus(-2), i.plus(1), i.plus(-3), i.plus(2)
                for u in range(UNITS):
                    if rowmax_unit(i, u):
                        s, su = rowmax_unit(i, u)
                        blk, hg = su // 2, su % 2
                        _, w, _ = window(blk)
                        for half in range(2):
                            h = 4 * hg + 2 * half
                            dve.wait_ge(s1_ready, 2 * UNITS * s.n + 2 * su + half + 1)
                            v.tensor_reduce(negmax[:, h:h + 2, blk:blk + 1],
                                            s1[half][:].rearrange("p (j c) -> p j c", j=2)[:, :, 0:w],
                                            AX.X, ALU.max, negate=True).then_inc(rowmax, 1)
                    if u == 0 and has(i, 1):
                        dve.wait_ge(q_p1, d.n + 1)
                        after(dve, q_p3, d.n)
                        v.scalar_tensor_tensor(qres, misc[1][:], wsm[:, BQ:BQ + 1], qparts[:, 0, :],
                                               ALU.add, ALU.subtract).then_inc(q_res, 1)
                    if u == 1 and has(i, 1):
                        dve.wait_ge(v_mm, d.n + 1)
                        v.tensor_copy(vaug[d.buf][:, :, :, 0:D].rearrange("p b h d -> p (b h) d"),
                                      misc[0][:].rearrange("p (g d) -> p g d", d=D)).then_inc(v_ready, 1)
                    if u == 1 and has(i, -2):
                        dve.wait_ge(dens_in[c.buf], 32 * (c.round + 1))
                        if not isinstance(c.n, int) or c.n >= 1:
                            prev = c.plus(-1)
                            stand(dve, DVE, recips_in[prev.buf], 16 * (prev.round + 1))
                        v.reciprocal(recips, dens).then_inc(recip_ready, 1)
                    if u == 2 and has(i, 1):
                        dve.wait_ge(k_p1, d.n + 1)
                        after(dve, k_p3, d.n)
                        v.scalar_tensor_tensor(kres, misc[1][:], wsm[:, BK:BK + 1], kparts[:, 0, :],
                                               ALU.add, ALU.subtract).then_inc(k_res, 1)
                    if u == 3 and has(i, -2):
                        for g in range(2):
                            dve.wait_ge(den_mm, 2 * c.n + g + 1)
                            v.tensor_tensor(onorm[g], ounorm[g], misc[g][:], ALU.mult).then_inc(o_ready, 1)
                    if u == 3 and has(i, 2):
                        if isinstance(f.n, int) and f.n in (0, 1, 4):
                            dve.wait_ge(x_in[{0: 0, 1: 1, 4: 2}[f.n]], 16)
                        moments_of(0, f.n, seq(f.n), stats1, mom1, xn1_ready)
                    if u == 4 and has(i, -2):
                        dve.wait_ge(relu_ready, c.n + 1)
                        dve.wait_ge(enc_in[c.buf], 16 * (c.round + 1))
                        v.tensor_tensor(gated, relu_o, enc[c.buf], ALU.mult).then_inc(gated_ready, 1)
                    if u == 5 and has(i, 0):
                        neg = negmax.rearrange("p a b -> p (a b)")
                        dve.wait_ge(rowmax, 2 * UNITS * (a.n + 1))
                        v.tensor_copy(mparts[:, 0, :], neg).then_inc(m_step, 1)
                        dve.wait_ge(m_step, 4 * a.n + 1)
                        v.tensor_tensor(mres, neg, mparts[:, 0, :], ALU.subtract).then_inc(m_step, 1)
                        dve.wait_ge(m_step, 4 * a.n + 2)
                        v.tensor_copy(mparts[:, 1, :], mres).then_inc(m_step, 1)
                        dve.wait_ge(m_step, 4 * a.n + 3)
                        v.tensor_tensor(mparts[:, 2, :], mres, mparts[:, 1, :], ALU.subtract).then_inc(m_step, 1)
                    if u == 5 and has(i, 2):
                        if has(i, 1):
                            dve.wait_ge(k_mm, d.n + 1)
                        normalise(0, f.n, seq(f.n), xn1, rstd1, xn1_ready)
                    if u == 6 and has(i, 0):
                        dve.wait_ge(m_mm, a.n + 1)
                        if not isinstance(a.n, int) or a.n >= 1:
                            prev = a.plus(-1)
                            dve.wait_ge(max_in[prev.buf], 16 * (prev.round + 1))
                        v.tensor_copy(mrows[0:96, :], misc[1][:].bitcast(BF16)[0:96, 0:P]).then_inc(m_rows, 1)
                    if u == 6 and has(i, -2):
                        dve.wait_ge(ct_mm, c.n + 1)
                        v.scalar_tensor_tensor(seq(c.n), misc[0][:], wsm[:, BCT:BCT + 1], seq(c.n),
                                               ALU.add, ALU.add).then_inc(x2_ready, 1)
                        stand(dve, DVE, x2_ready, c.n + 1)
                        moments_of(1, c.n, seq(c.n), stats2, mom2, xn2_ready)
                if has(i, -2):
                    if not isinstance(c.n, int) or c.n >= 1:
                        prev = c.plus(-1)
                        dve.wait_ge(xn_stored[prev.buf], 16 * (prev.round + 1))
                        dve.wait_ge(xt_mm, c.n)
                    normalise(1, c.n, seq(c.n), xn2, rstd2, xn2_ready)
                if has(i, -3):
                    dve.wait_ge(l_mm, e.n + 1)
                    v.tensor_copy(logits[:, bass.ds(e.n, 1), :].rearrange("p a t -> p (a t)"),
                                  misc[1][:, 0:EXPERTS]).then_inc(l_ready, 1)

            attention_steps(dve, step)

            yb, gb, rb = bank[5:7], bank[2:4], bank[7]
            linked = [0]

            def link(ins):
                linked[0] += 1
                ins.then_inc(route, 1)
                dve.wait_ge(route, linked[0])

            def each(ap):
                return ap.unsqueeze(2).to_broadcast([P, SEQS, EXPERTS])

            def flat(ap):
                return ap.rearrange("p a b -> p (a b)")

            def routing_choice():
                rev = cf[:, C_REV:C_REV + EXPERTS].unsqueeze(1).to_broadcast([P, SEQS, EXPERTS])
                dve.wait_ge(l_ready, SEQS)
                link(v.tensor_reduce(pick[:, 0, :], logits[:], AX.X, ALU.max))
                v.tensor_tensor(logits[:], logits[:], each(pick[:, 0, :]), ALU.subtract).then_inc(shifted, 1)
                dve.wait_ge(exp_done, 1)
                link(v.tensor_reduce(pick[:, 0, :], logits[:], AX.X, ALU.add))
                link(v.reciprocal(pick[:, 1, :], pick[:, 0, :]))
                link(v.tensor_tensor(logits[:], logits[:], each(pick[:, 1, :]), ALU.mult))
                for k in range(2):
                    link(v.tensor_reduce(top[:, k, :], logits[:], AX.X, ALU.max))
                    link(v.tensor_tensor(tmp[:], logits[:], each(top[:, k, :]), ALU.is_equal))
                    link(v.tensor_tensor(tmp[:], tmp[:], rev, ALU.mult))
                    link(v.tensor_reduce(pick[:, k, :], tmp[:], AX.X, ALU.max))
                    link(v.tensor_tensor(hot[:, k, :, :], rev, each(pick[:, k, :]), ALU.is_equal))
                    if k == 0:
                        link(v.scalar_tensor_tensor(flat(logits[:]), flat(hot[:, 0, :, :]), -2.0,
                                                    flat(logits[:]), ALU.mult, ALU.add))
                v.tensor_tensor(member[:], hot[:, 0, :, :], hot[:, 1, :, :], ALU.add).then_inc(member_ready, 1)

            def routing_slots():
                link(v.tensor_tensor(pick[:, 0, :], top[:, 0, :], top[:, 1, :], ALU.add))
                link(v.tensor_scalar(pick[:, 0, :], pick[:, 0, :], 1e-9, None, ALU.add))
                link(v.reciprocal(pick[:, 1, :], pick[:, 0, :]))
                link(v.tensor_tensor(top[:], top[:], pick[:, 1:2, :].to_broadcast([P, 2, SEQS]), ALU.mult))
                gates = flat(top[:])
                link(v.tensor_copy(gate_parts[:, 0, :], gates))
                link(v.tensor_tensor(gate_res[:], gates, gate_parts[:, 0, :], ALU.subtract))
                link(v.tensor_copy(gate_parts[:, 1, :], gate_res[:]))
                link(v.tensor_tensor(gate_parts[:, 2, :], gate_res[:], gate_parts[:, 1, :], ALU.subtract))
                v.tensor_copy(vals[:, :, 2:5], gate_parts[:].rearrange("p g q -> p q g"))
                v.tensor_copy(vals[:, :, 0:1], cf[:, C_TILE:C_TILE + 32].unsqueeze(2))
                link(v.tensor_copy(vals[:, :, 1:2],
                                   cf[:, C_ROW1:C_ROW1 + 1].unsqueeze(1).to_broadcast([P, 2 * SEQS, 1])))
                dve.wait_ge(rank_mm, 1)
                v.tensor_copy(flat(tmp[:]), rb[:, 0:256]).then_inc(ranks_read, 1)
                dve.wait_ge(ranks_read, 1)
                dve.wait_ge(rank_mm, 2)
                v.tensor_copy(count[:, 0, :], rb[:, 0:EXPERTS]).then_inc(counts_read, 1)
                dve.wait_ge(counts_read, 1)
                link(v.tensor_scalar(count_i[:], count[:, 0, :], 127.0, None, ALU.add))
                link(v.tensor_scalar(count_i[:], count_i[:], 7, None, ALU.arith_shift_right))
                link(v.tensor_copy(count[:, 1, :], count_i[:]))
                link(v.tensor_tensor_scan(count[:, 2, :], cf[:, C_ONE:C_ONE + EXPERTS], count[:, 1, :], 0.0,
                                          ALU.mult, ALU.add))
                link(v.tensor_tensor(count[:, 3, :], count[:, 2, :], count[:, 1, :], ALU.subtract))
                link(v.tensor_scalar(count[:, 3, :], count[:, 3, :], float(P), None, ALU.mult))
                link(v.tensor_tensor(tmp[:], tmp[:],
                                     count[:, 3:4, :].to_broadcast([P, SEQS, EXPERTS]), ALU.add))
                for k in range(2):
                    link(v.tensor_tensor(logits[:], hot[:, k, :, :], tmp[:], ALU.mult))
                    link(v.tensor_reduce(small[:, 0, SEQS * k:SEQS * (k + 1)], logits[:], AX.X, ALU.add))
                link(v.tensor_copy(small_i[:, 0, :], small[:, 0, :]))
                link(v.tensor_scalar(small_i[:, 1, :], small_i[:, 0, :], 7, None, ALU.arith_shift_right))
                link(v.tensor_scalar(small_i[:, 0, :], small_i[:, 0, :], P - 1, None, ALU.bitwise_and))
                v.tensor_copy(small[:, 1, :], small_i[:, 1, :])
                link(v.tensor_copy(small[:, 2, :], small_i[:, 0, :]))
                link(v.tensor_tensor(before, cf[:, C_IOTA:C_IOTA + BLOCKS].unsqueeze(2)
                                     .to_broadcast([P, BLOCKS, EXPERTS]),
                                     count[:, 2:3, :].to_broadcast([P, BLOCKS, EXPERTS]), ALU.is_ge))
                link(v.tensor_reduce(expert_of[:], before, AX.X, ALU.add))
                link(v.tensor_scalar(expert_i[:], expert_of[:], float(EXPERTS - 1), None, ALU.min))

            def routing_chunk(trip):
                dve.wait_ge(table_mm, trip + 1)
                rows_of = small[:, 2, :][:, bass.ds(trip * 8, 8)]
                blocks_of = small[:, 1, :][:, bass.ds(trip * 8, 8)]
                v.tensor_tensor(hot_row, cf[:, C_IOTA:C_IOTA + P].unsqueeze(1).to_broadcast([P, 8, P]),
                                rows_of.unsqueeze(2).to_broadcast([P, 8, P]), ALU.is_equal)
                v.tensor_tensor(hot_block, cf[:, C_IOTA:C_IOTA + BLOCKS].unsqueeze(1).to_broadcast([P, 8, BLOCKS]),
                                blocks_of.unsqueeze(2).to_broadcast([P, 8, BLOCKS]),
                                ALU.is_equal).then_inc(hot_blocks, 1)
                dve.wait_ge(hot_blocks, trip + 1)
                v.tensor_tensor(hot_col, hot_block.unsqueeze(2).to_broadcast([P, 8, 5, BLOCKS]),
                                vals[:, bass.ds(trip * 8, 8), :].unsqueeze(3).to_broadcast([P, 8, 5, BLOCKS]),
                                ALU.mult).then_inc(hot_ready, 1)

            def routing_tables():
                dve.wait_ge(table_mm, 6)
                link(v.tensor_copy(table, rb[:, 0:TABLE]))
                part = lambda g: table[:, g * BLOCKS:(g + 1) * BLOCKS]
                link(v.scalar_tensor_tensor(slot[:, 0, :], part(0), float(P), part(1), ALU.mult, ALU.add))
                link(v.tensor_scalar(slot[:, 1, :], slot[:, 0, :], 0.0, cf[:, C_SPARE:C_SPARE + 1],
                                     ALU.is_equal, ALU.mult))
                v.tensor_scalar(gather_i[:], slot[:, 0, :], -1.0, 0.0, ALU.add, ALU.max)
                v.scalar_tensor_tensor(scatter_i[:], slot[:, 0, :], -1.0, slot[:, 1, :], ALU.add, ALU.add)
                link(v.tensor_tensor(slot[:, 2, :], part(2), part(3), ALU.add))
                v.tensor_tensor(gate_of[:], slot[:, 2, :], part(4), ALU.add).then_inc(tables_ready, 1)

            def activate(k):
                dve.wait_ge(silu_ready, k.n + 1)
                v.tensor_tensor(act_in[:, k.buf, :], act_in[:, k.buf, :], gb[k.buf][:, INNER:2 * INNER],
                                ALU.mult).then_inc(act_ready, 1)

            def result(k, shared):
                dve.wait_ge(dn_mm, k.n + 1)
                if shared or k.first in (SEQS, SEQS + 1) and isinstance(k.trip, int):
                    after(dve, y_stored[k.buf], 16 * k.round)
                else:
                    dve.wait_ge(added[k.buf], 16 * (k.round - SEQS // 2))
                if shared:
                    v.tensor_tensor(y_out[:, k.buf, :], yb[k.buf][:], seq(k.n), ALU.add).then_inc(y_ready, 1)
                else:
                    v.tensor_scalar(y_out[:, k.buf, :], yb[k.buf][:], gate_of[:, bass.ds(k.n - SEQS, 1)],
                                    None, ALU.mult).then_inc(y_ready, 1)

            def step_experts(k, shared):
                activate(k)
                result(k.plus(-1), shared)

            routing_choice()
            activate(Turn(0, 0, 2))
            dve.wait_ge(spare_stored, 16)
            step_experts(Turn(1, 0, 2), True)
            for k in range(2, 6):
                step_experts(Turn(k, 0, 2), True)
            routing_slots()
            with dve.Fori(0, 4) as trip:
                routing_chunk(trip)
                for k in range(2):
                    step_experts(Turn(6 + k, trip, 2), True)
            step_experts(Turn(14, 0, 2), True)
            routing_tables()
            step_experts(Turn(15, 0, 2), True)
            step_experts(Turn(16, 0, 2), True)
            dve.wait_ge(tables_ready, 1)
            step_experts(Turn(SEQS + 1, 0, 2), False)
            step_experts(Turn(SEQS + 2, 0, 2), False)
            with dve.Fori(0, (BLOCKS - 3) // 2) as trip:
                for k in range(2):
                    step_experts(Turn(SEQS + 3 + k, trip, 2), False)
            result(Turn(SEQS + BLOCKS - 1, 0, 2), False)


def constants():
    import numpy as np

    r, c = np.arange(P)[:, None], np.arange(P)[None, :]
    f = np.zeros((P, C_END), np.float32)
    f[:, C_ID:C_ID + P] = r == c
    for g in range(2):
        f[:, C_SEL + P * g:C_SEL + P * g + P] = r == 4 * g + c // 32
    f[:, C_IOTA:C_IOTA + P] = c
    f[:, C_REV:C_REV + EXPERTS] = EXPERTS - np.arange(EXPERTS)
    f[:, C_TILE:C_TILE + 32] = np.arange(32) % SEQS
    f[:, C_ONE:C_ONE + EXPERTS] = 1.0
    f[:, C_ROW1] = np.arange(P) + 1
    f[:, C_SPARE] = np.arange(P) + TOKENS + 1
    f[:, C_HALF] = -0.5
    b = np.zeros((P, B_END), np.float32)
    b[:, B_ID:B_ID + P] = r == c
    off = np.arange(2 * P)[None, :] - r
    b[:, B_MASK:B_MASK + 2 * P] = np.where((off >= 0) & (off <= 2 * LOCAL), 0.0, MASKED)
    b[:, B_TRI:B_TRI + P] = r < c
    b[:, B_ONES:B_ONES + P] = 1.0
    return f, b


def kernel(**inputs):
    import numpy as np
    import concourse.bacc as bacc
    from concourse.bass_utils import run_bass_kernel_spmd

    a = {k: np.asarray(v) for k, v in inputs.items()}
    w_in, b_in, w_out = a["L0_xattn_w_in"], a["L0_xattn_b_in"], a["L0_xattn_w_out"]
    w_small = np.zeros((P, W_END), np.float32)
    for i, col in enumerate((W_Q, W_K)):
        w = w_in[P * i:P * i + P].reshape(HEADS, D, P).transpose(1, 0, 2).reshape(P, P)
        w_small[:, col:col + P] = w.T
        w_small[:, W_BIAS + i] = b_in[P * i:P * i + P].reshape(HEADS, D).T.reshape(P)
    w_small[:, W_V:W_V + P] = w_in[2 * P:3 * P].T
    for h in range(HEADS):
        g, row = h // 4, 32 * (h % 4)
        w_small[row:row + D, W_O + P * g:W_O + P * g + P] = w_out[:, D * h:D * h + D].T
        w_small[row:row + D, BV0 + g] = b_in[2 * P + D * h:2 * P + D * h + D]
    w_small[:, W_CT:W_CT + P] = a["L0_xattn_w_ct"]
    w_small[:, W_R:W_R + 64] = a["L0_ffn_Wr"].reshape(EXPERTS, 4, P).transpose(2, 1, 0).reshape(P, 64)
    w_small[:, BO] = a["L0_xattn_b_out"]
    w_small[:, BCT] = a["L0_xattn_b_ct"]
    w_small[:EXPERTS, BR] = a["L0_ffn_bias"]

    gu = np.concatenate([a["L0_ffn_Wg"], a["L0_ffn_Wu"]], axis=2)
    sgu = np.concatenate([a["L0_ffn_sWg"], a["L0_ffn_sWu"]], axis=1)
    const_f, const_b = constants()
    arrays = {
        "x": a["x"], "ctx": a["ctx_2048"], "const_f": const_f, "const_b": const_b, "w_small": w_small,
        "w_gu": gu.reshape(EXPERTS, 4, P, 512).transpose(2, 0, 1, 3).reshape(P, EXPERTS, 2048),
        "w_d": a["L0_ffn_Wd"].reshape(EXPERTS, 2, P, T).transpose(0, 2, 1, 3).reshape(EXPERTS, P, 2 * T),
        "sw_gu": sgu.reshape(4, P, 512).transpose(1, 0, 2),
        "sw_d": a["L0_ffn_sWd"].reshape(2, P, T).transpose(1, 0, 2),
    }
    arrays = {k: np.ascontiguousarray(v) for k, v in arrays.items()}
    nc = bacc.Bacc("TRN2", target_bir_lowering=False, num_devices=1)
    args = [nc.dram_tensor(k, v.shape, mybir.dt.from_np(v.dtype), kind="ExternalInput").ap()
            for k, v in arrays.items()]
    out = nc.dram_tensor("out", (SEQS + 1, P, T), F32, kind="ExternalOutput").ap()
    xattn_moe_kernel(nc, *args, out)
    result = run_bass_kernel_spmd(nc, [arrays], core_ids=[0])
    return result.results[0]["out"][:SEQS]
```

```python
from contextlib import ExitStack

import concourse.bass as bass
from concourse import mybir

F32 = mybir.dt.float32
BF16 = mybir.dt.bfloat16
I32 = mybir.dt.int32
ALU = mybir.AluOpType
ACT = mybir.ActivationFunctionType
AX = mybir.AxisListType

P = 128
SEQS, T = 16, 512
HEADS, D = 8, 16
LOCAL = 64
QB = T // P
EPS = 1e-5
EXPERTS, INNER = 16, 256
TOKENS = SEQS * P
BLOCKS = 2 * TOKENS // P + EXPERTS - 1
Q_PARTS = (0, 0, 1, 0, 1, 2)
K_PARTS = (0, 1, 0, 2, 1, 0)
STACK = 6 * D
UNITS = 2 * QB
MASKED = -1e38

C_ID, C_IOTA, C_REV, C_TILE, C_ONE, C_ROW1, C_SPARE, C_HALF, C_END = 0, 128, 256, 272, 304, 320, 321, 322, 323
B_ID, B_MASK, B_TRI, B_ONES, B_SEL, B_ZERO, B_END = 0, 128, 384, 512, 640, 896, 1152
W_Q, W_K, W_V, W_O, W_CT, W_R, W_BIAS, W_END = 0, 128, 256, 384, 640, 768, 832, 840
BQ, BK, BV0, BV1, BO, BCT, BR = range(W_BIAS, W_BIAS + 7)
TABLE = 5 * BLOCKS


class Turn:

    def __init__(self, first, trip, step):
        self.first, self.trip, self.step = first, trip, step
        self.n = first if isinstance(trip, int) and trip == 0 else trip * step + first
        self.buf = first % step
        self.round = trip + first // step

    def plus(self, d):
        return Turn(self.first + d, self.trip, self.step)


def after(eng, sem, count):
    if isinstance(count, int) and count <= 0:
        return
    eng.wait_ge(sem, count)


def window(block):
    lo, hi = max(0, P * block - LOCAL), min(T, P * block + P + LOCAL)
    return lo, hi - lo, lo - (P * block - LOCAL)


def xattn_moe_kernel(nc, x, ctx_in, const_f, const_b, w_small, w_gu, w_d, sw_gu, sw_d, out):
    es = ExitStack()
    with es:
        def sb(name, shape, dt=F32):
            return es.enter_context(nc.sbuf_tensor(name, shape, dt))

        def sem(name):
            return es.enter_context(nc.semaphore(name))

        xn_rows = nc.dram_tensor("xn_rows", (TOKENS, T), F32).ap()
        out_rows = out.rearrange("a p t -> (a p) t")

        wgu = sb("wgu", [P, EXPERTS * 4 * 512])
        X = sb("X", [P, SEQS, T])
        cf = sb("cf", [P, C_END])
        cb = sb("cb", [P, B_END], BF16)
        logits = sb("logits", [P, SEQS, EXPERTS])
        swgu = sb("swgu", [P, 4, 512])
        swd = sb("swd", [P, 2, T])
        wd = sb("wd", [P, 2, 2, T])
        rows = sb("rows", [P, 2, T])
        rowsT = sb("rowsT", [P, 2, 4, P])
        act_in = sb("act_in", [P, 2, INNER])
        actT = sb("actT", [P, 2, 2, P])
        y_out = sb("y_out", [P, 2, T])

        used = [0]

        def over(shape, dt=F32):
            cols = 1
            for s in shape:
                cols *= s
            words = cols if dt is F32 else (cols + 1) // 2
            ap = wgu[:, used[0]:used[0] + words]
            used[0] += words
            assert used[0] <= EXPERTS * 4 * 512
            if dt is not F32:
                ap = ap.bitcast(dt)
            if len(shape) == 1:
                return ap
            names = " ".join("abc"[:len(shape)])
            return ap.rearrange(f"p ({names}) -> p {names}", **{"abc"[i]: s for i, s in enumerate(shape)})

        qstack = [over([HEADS, T], BF16) for _ in range(3)]
        kstack = [over([HEADS, T], BF16) for _ in range(3)]
        vaug = [over([QB, HEADS, 32]) for _ in range(3)]
        enc = [over([T]) for _ in range(3)]
        xn1 = over([T])
        qparts = over([3, T], BF16)
        kparts = over([3, T], BF16)
        qres = over([T])
        kres = over([T])
        probs = [over([4, 2 * P]) for _ in range(4)]
        ounorm = [over([T]) for _ in range(2)]
        onorm = [over([T]) for _ in range(2)]
        dens = over([HEADS * T // P])
        recips = over([HEADS * T // P])
        recip_res = over([HEADS * T // P])
        recip_parts = over([3, HEADS * T // P], BF16)
        recip_rows = over([T], BF16)
        relu_o = over([T])
        gated = over([T])
        xn2 = over([T])
        xn2T = over([4, P])
        logitT = over([P])
        negmax = over([HEADS, QB])
        mres = over([HEADS * QB])
        mparts = over([3, HEADS * QB], BF16)
        mrows = over([P], BF16)
        wsm = over([W_END])
        beff = over([1])
        cb_f = over([B_END])
        stats = over([2, 6])
        moments = over([2, 2])
        rstd = over([2])
        epsd = over([2])

        top = sb("top", [P, 2, SEQS])
        pick = sb("pick", [P, 2, SEQS])
        hot = sb("hot", [P, 2, SEQS, EXPERTS], BF16)
        tmp = sb("tmp", [P, SEQS, EXPERTS])
        member = sb("member", [P, SEQS, EXPERTS], BF16)
        count = sb("count", [P, 4, EXPERTS])
        count_i = sb("count_i", [P, EXPERTS], I32)
        small = sb("small", [P, 6, SEQS * 2])
        small_i = sb("small_i", [P, 2, SEQS * 2], I32)
        gate_parts = sb("gate_parts", [P, 3, SEQS * 2], BF16)
        gate_res = sb("gate_res", [P, SEQS * 2])
        expert_of = sb("expert_of", [P, BLOCKS])
        expert_i = sb("expert_i", [P, BLOCKS], I32)
        slot = sb("slot", [P, 4, BLOCKS])
        gather_i = sb("gather_i", [P, BLOCKS], I32)
        scatter_i = sb("scatter_i", [P, BLOCKS], I32)
        gate_of = sb("gate_of", [P, BLOCKS])
        gather_now = sb("gather_now", [P, 2], I32)
        scatter_now = sb("scatter_now", [P, 2], I32)
        vals = sb("vals", [P, 2 * SEQS, 5])
        wd_flat = wd[:].rearrange("p a b c -> p (a b c)")
        hot_row = wd_flat[:, 0:512].bitcast(BF16).rearrange("p (q r) -> p q r", q=8)
        hot_col = wd_flat[:, 512:512 + 4 * TABLE].bitcast(BF16).rearrange("p (q g b) -> p q g b", q=8, g=5)
        before = wd_flat[:, 0:BLOCKS * EXPERTS].rearrange("p (b e) -> p b e", b=BLOCKS)
        table = wd_flat[:, 1500:1500 + TABLE]
        hot_block = wd_flat[:, 1750:1750 + 4 * BLOCKS].bitcast(BF16).rearrange("p (q b) -> p q b", q=8)

        bank = [es.enter_context(nc.psum_tensor(f"bank{i}", [P, 512], F32)) for i in range(8)]
        s1, s2, oacc, misc = bank[0:2], bank[2:4], bank[4:6], bank[6:8]

        consts_in, weights_in, shared_in = sem("consts_in"), sem("weights_in"), sem("shared_in")
        x_in = [sem(f"x_in{i}") for i in range(3)]
        enc_in = [sem(f"enc_in{i}") for i in range(3)]
        stack_in = [sem(f"stack_in{i}") for i in range(3)]
        max_in = [sem(f"max_in{i}") for i in range(3)]
        xn_stored = [sem(f"xn_stored{i}") for i in range(3)]
        experts_in = sem("experts_in")
        rows_in = [sem(f"rows_in{i}") for i in range(2)]
        wd_in = [sem(f"wd_in{i}") for i in range(2)]
        y_stored = [sem(f"y_stored{i}") for i in range(2)]
        gathered = [sem(f"gathered{i}") for i in range(2)]
        added = [sem(f"added{i}") for i in range(2)]
        spare_stored = sem("spare_stored")
        setup = sem("setup")
        ones_set = sem("ones_set")
        beff_mm, beff_ready = sem("beff_mm"), sem("beff_ready")
        stats1, mom1, eps1, rstd1, xn1_ready = (sem(s) for s in ("stats1", "mom1", "eps1", "rstd1", "xn1_ready"))
        stats2, mom2, eps2, rstd2, xn2_ready = (sem(s) for s in ("stats2", "mom2", "eps2", "rstd2", "xn2_ready"))
        q_mm, k_mm, v_mm = sem("q_mm"), sem("k_mm"), sem("v_mm")
        q_p1, q_res, q_p2, q_p3 = sem("q_p1"), sem("q_res"), sem("q_p2"), sem("q_p3")
        k_p1, k_res, k_p2, k_p3 = sem("k_p1"), sem("k_res"), sem("k_p2"), sem("k_p3")
        v_ready = sem("v_ready")
        s1_ready, rowmax = sem("s1_ready"), sem("rowmax")
        m_step, m_mm, m_rows = sem("m_step"), sem("m_mm"), sem("m_rows")
        s2_ready, exp_ready, pv_done = sem("s2_ready"), sem("exp_ready"), sem("pv_done")
        o_copied = [sem(f"o_copied{i}") for i in range(2)]
        dens_in = [sem(f"dens_in{i}") for i in range(3)]
        recips_in = [sem(f"recips_in{i}") for i in range(3)]
        den_mm, recip_step, o_ready = sem("den_mm"), sem("recip_step"), sem("o_ready")
        cut_ready = sem("cut_ready")
        proj_mm, relu_ready, gated_ready = sem("proj_mm"), sem("relu_ready"), sem("gated_ready")
        ct_mm, x2_ready = sem("ct_mm"), sem("x2_ready")
        xt_mm, xt_ready, router_mm, lt_ready, l_mm, l_ready = (
            sem(s) for s in ("xt_mm", "xt_ready", "router_mm", "lt_ready", "l_mm", "l_ready"))
        t_mm, t_ready, gu_mm, silu_ready, act_ready, at_mm, at_ready, dn_mm, y_ready = (
            sem(s) for s in ("t_mm", "t_ready", "gu_mm", "silu_ready", "act_ready", "at_mm", "at_ready",
                             "dn_mm", "y_ready"))
        route, shifted, exp_done = sem("route"), sem("shifted"), sem("exp_done")
        ranks_read, counts_read = sem("ranks_read"), sem("counts_read")
        gather_set, scatter_set = sem("gather_set"), sem("scatter_set")
        member_ready, rank_mm, hot_blocks, hot_ready, table_mm, tables_ready = (
            sem(s) for s in ("member_ready", "rank_mm", "hot_blocks", "hot_ready", "table_mm", "tables_ready"))

        ident = cf[:, C_ID:C_ID + P]
        identb = cb[:, B_ID:B_ID + P]

        def mask(blk):
            lo, w, off = window(blk)
            return cb[:, B_MASK + off:B_MASK + off + w]

        STACK_DMAS = 12 * 16

        DVE, PE, POOL, SP = (sem(f"passed_{e}") for e in ("dve", "pe", "pool", "sp"))

        def stand(eng, own, sem, count):
            after(eng, sem, count)
            if not isinstance(count, int):
                eng.sem_inc(own, 1)

        def attention_steps(eng, step):
            for i in range(-2, 4):
                step(Turn(i, 0, 3))
            with eng.Fori(0, 3) as trip:
                for k in range(3):
                    step(Turn(4 + k, trip, 3))
            for i in range(13, 19):
                step(Turn(i, 0, 3))

        def rowmax_unit(i, u):
            e = i if u < UNITS - 2 else i.plus(1)
            return (e, (u + 2) % UNITS) if has(e, 0) else None

        def has(i, d):
            return not isinstance(i.n, int) or 0 <= i.n + d < SEQS

        block = es.enter_context(nc.Block())

        @block.sync
        def _(sp):
            sp.dma_start(wsm, w_small).then_inc(weights_in, 16)
            sp.dma_start(X[:, 0, :], x[0]).then_inc(x_in[0], 16)
            sp.dma_start(cf[:], const_f).then_inc(consts_in, 16)
            sp.dma_start(cb_f, const_b).then_inc(consts_in, 16)
            sp.dma_start(X[:, 1:4, :], x[1:4].rearrange("n p t -> p n t")).then_inc(x_in[1], 16)
            sp.dma_start(X[:, 4:, :], x[4:].rearrange("n p t -> p n t")).then_inc(x_in[2], 16)
            sp.dma_start(swgu[:], sw_gu).then_inc(shared_in, 16)
            sp.dma_start(swd[:], sw_d).then_inc(shared_in, 16)

            def send(stack, parts, groups, sem):
                for g in groups:
                    which = (Q_PARTS if stack is qstack else K_PARTS)[g]
                    sp.dma_start(stack[sem[1]][D * g:D * g + D, :, :], parts[:, which, :]).then_inc(sem[0], 16)

            def step(i):
                d = i.plus(1)
                def denominators(g):
                    c = i.plus(-2)
                    sp.wait_ge(o_copied[g], c.n + 1)
                    sp.dma_start(dens[64 * g:64 * g + 64, :], ounorm[g][D:P:32, :]).then_inc(dens_in[c.buf], 16)

                c = i.plus(-2)
                if has(i, -2):
                    denominators(0)
                if has(i, 1):
                    stand(sp, SP, s2_ready, 2 * UNITS * (i.n - 1))
                    to = (stack_in[d.buf], d.buf)
                    sp.wait_ge(q_p1, d.n + 1)
                    send(qstack, qparts, (0, 1, 3), to)
                if has(i, -2):
                    denominators(1)
                if has(i, 1):
                    sp.wait_ge(q_p2, d.n + 1)
                    send(qstack, qparts, (2, 4), to)
                    sp.wait_ge(q_p3, d.n + 1)
                    send(qstack, qparts, (5,), to)
                if has(i, 1):
                    sp.wait_ge(k_p1, d.n + 1)
                    send(kstack, kparts, (0, 2, 5), to)
                if has(i, -2):
                    sp.wait_ge(recip_step, 5 * (c.n + 1))
                    for p in range(3):
                        sp.dma_start(recip_rows[HEADS * p:HEADS * p + HEADS, :],
                                     recip_parts[:, p, :]).then_inc(recips_in[c.buf], 16)
                if has(i, 1):
                    sp.wait_ge(k_p2, d.n + 1)
                    send(kstack, kparts, (1, 4), to)
                    sp.wait_ge(k_p3, d.n + 1)
                    send(kstack, kparts, (3,), to)
                if has(i, -3):
                    e = i.plus(-3)
                    sp.wait_ge(xn2_ready, e.n + 1)
                    sp.dma_start(xn_rows[bass.ds(e.n * P, P), :], xn2).then_inc(xn_stored[e.buf], 16)
                if has(i, 0):
                    after(sp, gated_ready, i.n - 2)
                    sp.dma_start(enc[i.buf], ctx_in[bass.ds(i.n, 1), :, :].rearrange("a p t -> (a p) t")
                                 ).then_inc(enc_in[i.buf], 16)
                    sp.wait_ge(m_rows, i.n + 1)
                    sp.dma_start(qstack[i.buf][STACK:STACK + 3, :, :], mrows[0:96, :]).then_inc(max_in[i.buf], 16)

            attention_steps(sp, step)

            sp.wait_ge(l_ready, SEQS)
            for b in range(3):
                sp.wait_ge(xn_stored[b], 16 * len(range(b, SEQS, 3)))
            for e in range(EXPERTS):
                sp.wait_ge(t_mm, e + 1)
                sp.dma_start(wgu[:, e * 2048:(e + 1) * 2048], w_gu[:, e, :]).then_inc(experts_in, 16)

            sp.wait_ge(tables_ready, 1)

            def load_wd(k):
                stand(sp, SP, dn_mm, k.n - 1)
                e = sp.value_load(expert_i[0:1, bass.ds(k.n - SEQS, 1)], min_val=0, max_val=EXPERTS - 1)
                sp.dma_start(wd[:, k.buf, :, :].rearrange("p c n -> p (c n)"),
                             w_d[bass.ds(e, 1), :, :].rearrange("a p n -> (a p) n")).then_inc(wd_in[k.buf], 16)

            with sp.Fori(0, BLOCKS // 2) as trip:
                for k in range(2):
                    load_wd(Turn(SEQS + k, trip, 2))
            load_wd(Turn(SEQS + BLOCKS - 1, 0, 2))

        @block.gpsimd
        def _(pool):
            pool.wait_ge(consts_in, 32)

            def inverse_deviation(which, n, mom, eps, out_sem):
                stand(pool, POOL, mom, n + 1)
                nc.gpsimd.tensor_scalar(epsd[:, which:which + 1], moments[:, which, 1:2], EPS, None,
                                        ALU.add).then_inc(eps, 1)
                pool.wait_ge(eps, n + 1)
                nc.gpsimd.tensor_tensor(rstd[:, which:which + 1], epsd[:, which:which + 1],
                                        cf[:, C_HALF:C_HALF + 1], ALU.pow).then_inc(out_sem, 1)

            def third_part(n, res, to, p2_sem, p3_sem):
                stand(pool, POOL, p2_sem, n + 1)
                nc.gpsimd.tensor_tensor(to[:, 2, :], res, to[:, 1, :], ALU.subtract).then_inc(p3_sem, 1)

            def split_reciprocals(c):
                v = nc.gpsimd
                stand(pool, POOL, recip_step, 5 * c.n + 1)
                v.tensor_copy(recip_parts[:, 0, :], recips).then_inc(recip_step, 1)
                pool.wait_ge(recip_step, 5 * c.n + 2)
                v.tensor_tensor(recip_res, recips, recip_parts[:, 0, :], ALU.subtract).then_inc(recip_step, 1)
                stand(pool, POOL, recip_step, 5 * c.n + 3)
                v.tensor_copy(recip_parts[:, 1, :], recip_res).then_inc(recip_step, 1)
                pool.wait_ge(recip_step, 5 * c.n + 4)
                v.tensor_tensor(recip_parts[:, 2, :], recip_res, recip_parts[:, 1, :],
                                ALU.subtract).then_inc(recip_step, 1)

            def split_max(a):
                v = nc.gpsimd
                neg = negmax.rearrange("p a b -> p (a b)")
                stand(pool, POOL, m_mm, a.n)
                stand(pool, POOL, rowmax, 2 * UNITS * (a.n + 1))
                v.tensor_copy(mparts[:, 0, :], neg).then_inc(m_step, 1)
                pool.wait_ge(m_step, 4 * a.n + 1)
                v.tensor_tensor(mres, neg, mparts[:, 0, :], ALU.subtract).then_inc(m_step, 1)
                stand(pool, POOL, m_step, 4 * a.n + 2)
                v.tensor_copy(mparts[:, 1, :], mres).then_inc(m_step, 1)
                pool.wait_ge(m_step, 4 * a.n + 3)
                v.tensor_tensor(mparts[:, 2, :], mres, mparts[:, 1, :], ALU.subtract).then_inc(m_step, 1)

            def cut_band(b, u):
                blk = u // 2
                _, w, off = window(blk)
                stand(pool, POOL, exp_ready, 2 * UNITS * b.n + 2 * u + 2)
                before, behind = probs[u % 4][:, :, 0:P - off], probs[u % 4][:, :, P - off:w]
                nc.gpsimd.affine_select(out=before, in_=before, compare_op=ALU.is_ge, fill=0.0, base=off,
                                        pattern=[[0, 4], [1, P - off]], channel_multiplier=-1)
                nc.gpsimd.affine_select(out=behind, in_=behind, compare_op=ALU.is_ge, fill=0.0, base=0,
                                        pattern=[[0, 4], [-1, w - P + off]],
                                        channel_multiplier=1).then_inc(cut_ready, 1)

            def step(i):
                for u in range(UNITS):
                    if u == 2 and has(i, -2):
                        split_reciprocals(i.plus(-2))
                    if u == 3 and has(i, 1):
                        third_part(i.n + 1, kres, kparts, k_p2, k_p3)
                    if has(i, -1):
                        cut_band(i.plus(-1), u)
                    if u == 1 and has(i, 1):
                        third_part(i.n + 1, qres, qparts, q_p2, q_p3)
                    if u == 1 and has(i, -3):
                        inverse_deviation(1, i.n - 3, mom2, eps2, rstd2)
                    if u == 4 and has(i, 2):
                        inverse_deviation(0, i.n + 2, mom1, eps1, rstd1)
                    if u == 5 and has(i, 0):
                        split_max(i)
                if isinstance(i.n, int) and i.n <= 0:
                    pool.wait_ge(rstd1, i.n + 3)
                    after(pool, m_step, 4 * (i.n + 1))
                    nc.gpsimd.memset(kstack[i.n + 2][STACK:STACK + 3, :, :], 1.0).then_inc(ones_set, 1)
                    pool.wait_ge(ones_set, i.n + 3)

            attention_steps(pool, step)

            pool.wait_ge(tables_ready, 1)

            def gather(k):
                stand(pool, POOL, gathered[k.buf], 16 * (k.round - SEQS // 2))
                nc.gpsimd.tensor_copy(gather_now[:, k.buf:k.buf + 1],
                                      gather_i[:, bass.ds(k.n - SEQS, 1)]).then_inc(gather_set, 1)
                pool.wait_ge(gather_set, k.n - SEQS + 1)
                stand(pool, POOL, t_mm, k.n - 1)
                nc.gpsimd.indirect_dma_start(
                    rows[:, k.buf, :], None, xn_rows[:, :],
                    bass.IndirectOffsetOnAxis(ap=gather_now[:, k.buf:k.buf + 1], axis=0),
                    bounds_check=TOKENS - 1, oob_is_err=True).then_inc(gathered[k.buf], 16)

            def add_rows(k):
                for b in range(2):
                    stand(pool, POOL, added[b], 16 * ((k.round if b or not k.buf else k.round + 1) - SEQS // 2))
                nc.gpsimd.tensor_copy(scatter_now[:, k.buf:k.buf + 1],
                                      scatter_i[:, bass.ds(k.n - SEQS, 1)]).then_inc(scatter_set, 1)
                stand(pool, POOL, scatter_set, k.n - SEQS + 1)
                stand(pool, POOL, y_ready, k.n + 1)
                nc.gpsimd.indirect_dma_start(
                    out_rows[:, :], bass.IndirectOffsetOnAxis(ap=scatter_now[:, k.buf:k.buf + 1], axis=0),
                    y_out[:, k.buf, :], None, bounds_check=TOKENS + P - 1, oob_is_err=True,
                    compute_op=ALU.add).then_inc(added[k.buf], 16)

            AHEAD = 4
            for k in range(AHEAD):
                gather(Turn(SEQS + k, 0, 2))
            pool.wait_ge(spare_stored, 16)
            for b in range(2):
                pool.wait_ge(y_stored[b], 16 * (SEQS // 2))
            for k in range(2):
                add_rows(Turn(SEQS + k, 0, 2))
                gather(Turn(SEQS + AHEAD + k, 0, 2))
            with pool.Fori(0, (BLOCKS - AHEAD) // 2 - 1) as trip:
                for k in range(2):
                    add_rows(Turn(SEQS + 2 + k, trip, 2))
                    gather(Turn(SEQS + 2 + AHEAD + k, trip, 2))
            for k in range((BLOCKS - AHEAD) // 2 * 2, BLOCKS):
                add_rows(Turn(SEQS + k, 0, 2))
                if k + AHEAD < BLOCKS:
                    gather(Turn(SEQS + AHEAD + k, 0, 2))
            for b in range(2):
                pool.wait_ge(added[b], 16 * len(range(b, BLOCKS, 2)))

        @block.tensor
        def _(pe):
            mm = nc.tensor.matmul

            pe.wait_ge(weights_in, 16)
            for g in range(2):
                last = mm(misc[0][:, 0:1], wsm[:, W_O + P * g:W_O + P * g + P], wsm[:, BV0 + g:BV0 + g + 1],
                          start=(g == 0), stop=(g == 1))
            last.then_inc(beff_mm, 1)
            pe.wait_ge(consts_in, 32)
            pe.wait_ge(setup, 5)

            def step(i):
                b, c, d, e = i.plus(-1), i.plus(-2), i.plus(1), i.plus(-3)
                for u in range(UNITS):
                    if rowmax_unit(i, u):
                        a, au = rowmax_unit(i, u)
                        blk, hg = au // 2, au % 2
                        lo, w, _ = window(blk)
                        if au == 0:
                            pe.wait_ge(stack_in[a.buf], STACK_DMAS * (a.round + 1))
                        for half in range(2):
                            r = 2 * UNITS * a.n + 2 * au + half
                            after(pe, rowmax, r - 1)
                            for j in range(2):
                                h = 4 * hg + 2 * half + j
                                o = s1[half][:, 256 * j:256 * j + w]
                                mm(o, qstack[a.buf][0:STACK, h, P * blk:P * blk + P],
                                   kstack[a.buf][0:STACK, h, lo:lo + w], start=True, stop=False)
                                last = mm(o, identb, mask(blk), start=False, stop=True)
                            last.then_inc(s1_ready, 1)
                    if has(i, -1):
                        blk, hg = u // 2, u % 2
                        lo, w, _ = window(blk)
                        if u == 0 and isinstance(b.n, int) and b.n < 3:
                            pe.wait_ge(ones_set, b.n + 1)
                        if u == 0:
                            pe.wait_ge(max_in[b.buf], 16 * (b.round + 1))
                        for half in range(2):
                            r = 2 * UNITS * b.n + 2 * u + half
                            after(pe, exp_ready, r - 1)
                            for j in range(2):
                                h = 4 * hg + 2 * half + j
                                o = s2[half][:, 256 * j:256 * j + w]
                                last = mm(o, kstack[b.buf][0:STACK + 3, h, P * blk:P * blk + P],
                                          qstack[b.buf][0:STACK + 3, h, lo:lo + w], start=True, stop=True)
                            last.then_inc(s2_ready, 1)
                    if u < 2 and has(i, -2):
                        attend_values(c, UNITS - 2 + u)
                    if u >= 2 and has(i, -1):
                        attend_values(b, u - 2)
                    between(i, u)

            def between(i, u):
                a, b, c, d, e = i, i.plus(-1), i.plus(-2), i.plus(1), i.plus(-3)
                if u == 0 and has(i, 1):
                    pe.wait_ge(xn1_ready, d.n + 1)
                    after(pe, k_res, d.n)
                    after(pe, m_rows, d.n - 1)
                    after(pe, l_ready, d.n - 4)
                    mm(misc[1][:], wsm[:, W_Q:W_Q + P], xn1, start=True, stop=True).then_inc(q_mm, 1)
                if u == 1 and has(i, 1):
                    pe.wait_ge(q_res, d.n + 1)
                    mm(misc[1][:], wsm[:, W_K:W_K + P], xn1, start=True, stop=True).then_inc(k_mm, 1)
                if u == 2 and has(i, 1):
                    after(pe, v_ready, d.n)
                    after(pe, x2_ready, d.n - 3)
                    if isinstance(d.n, int) and d.n == 0:
                        pe.wait_ge(beff_ready, 1)
                    for k in range(QB):
                        last = mm(misc[0][:, P * k:P * k + P], xn1[:, P * k:P * k + P], wsm[:, W_V:W_V + P],
                                  start=True, stop=True)
                    last.then_inc(v_mm, 1)
                if u == 3 and has(i, -3):
                    pe.wait_ge(xn2_ready, e.n + 1)
                    if has(i, 1):
                        pe.wait_ge(k_res, d.n + 1)
                    after(pe, l_ready, e.n)
                    for k in range(4):
                        last = nc.tensor.transpose(misc[1][:, P * k:P * k + P], xn2[:, P * k:P * k + P], ident)
                    last.then_inc(xt_mm, 1)
                if u == 4 and has(i, -3):
                    pe.wait_ge(xt_ready, e.n + 1)
                    pe.wait_ge(x2_ready, e.n + 1)
                    if has(i, 1):
                        pe.wait_ge(v_ready, d.n + 1)
                    for k in range(4):
                        last = mm(misc[0][0:EXPERTS, 0:P], wsm[:, W_R + 16 * k:W_R + 16 * k + 16], xn2T[:, k, :],
                                  start=(k == 0), stop=(k == 3))
                    last.then_inc(router_mm, 1)
                if u == 5 and has(i, -2):
                    pe.wait_ge(recips_in[c.buf], 48 * (c.round + 1))
                    if has(i, -3):
                        pe.wait_ge(lt_ready, e.n + 1)
                    elif has(i, 1):
                        pe.wait_ge(v_ready, d.n + 1)
                        pe.wait_ge(k_res, d.n + 1)
                    for g in range(2):
                        mm(misc[g][:], cb[0:3 * HEADS, B_SEL + P * g:B_SEL + P * g + P], recip_rows[0:3 * HEADS, :],
                           start=True, stop=True).then_inc(den_mm, 1)
                if u == 6 and has(i, -2):
                    pe.wait_ge(o_ready, 2 * c.n + 2)
                    for g in range(2):
                        last = mm(misc[0][:], wsm[:, W_O + P * g:W_O + P * g + P], onorm[g],
                                  start=(g == 0), stop=(g == 1))
                    last.then_inc(proj_mm, 1)
                if u == 6 and has(i, 0):
                    if has(i, -2):
                        pe.wait_ge(o_ready, 2 * c.n + 2)
                    elif has(i, 1):
                        pe.wait_ge(k_res, d.n + 1)
                    pe.wait_ge(m_step, 4 * (a.n + 1))
                    nc.tensor.transpose(misc[1][:].bitcast(BF16)[0:96, 0:P],
                                        mparts.rearrange("p a b -> p (a b)"), identb).then_inc(m_mm, 1)
                if u == 7 and has(i, -3):
                    if has(i, 0):
                        pe.wait_ge(m_rows, a.n + 1)
                    stand(pe, PE, lt_ready, e.n + 1)
                    nc.tensor.transpose(misc[1][:, 0:EXPERTS], logitT[0:EXPERTS, :],
                                        cf[0:EXPERTS, C_ID:C_ID + EXPERTS]).then_inc(l_mm, 1)
                if u == 7 and has(i, -2):
                    pe.wait_ge(gated_ready, c.n + 1)
                    mm(misc[0][:], wsm[:, W_CT:W_CT + P], gated, start=True, stop=True).then_inc(ct_mm, 1)

            def attend_values(b, u):
                blk, hg = u // 2, u % 2
                lo, w, _ = window(blk)
                pe.wait_ge(cut_ready, UNITS * b.n + u + 1)
                if u == 0:
                    pe.wait_ge(v_ready, b.n + 1)
                if blk == 0:
                    after(pe, o_copied[hg], b.n)
                for j in range(4):
                    last = mm(oacc[hg][32 * j:32 * j + 32, lo:lo + w], vaug[b.buf][:, blk, 4 * hg + j, :],
                              probs[u % 4][:, j, 0:w], start=(blk == 0), stop=(blk == QB - 1),
                              skip_group_check=True)
                last.then_inc(pv_done, 1)

            attention_steps(pe, step)

            tb, gb, ab, yb, rb = bank[0:2], bank[2:4], bank[4], bank[5:7], bank[7]
            pe.wait_ge(l_ready, SEQS)

            def turn_rows(k, shared):
                if shared:
                    pe.wait_ge(rows_in[k.buf], 16 * (k.round + 1))
                else:
                    pe.wait_ge(gathered[k.buf], 16 * (k.round - SEQS // 2 + 1))
                after(pe, t_ready, k.n - 1)
                for c in range(4):
                    last = nc.tensor.transpose(tb[k.buf][:, P * c:P * c + P], rows[:, k.buf, P * c:P * c + P], ident)
                last.then_inc(t_mm, 1)

            def gate_up(k, shared, between=None):
                pe.wait_ge(t_ready, k.n + 1)
                after(pe, act_ready, k.n - 1)
                if not shared:
                    e = pe.value_load(expert_i[0:1, bass.ds(k.n - SEQS, 1)], min_val=0, max_val=EXPERTS - 1)
                for c in range(4):
                    w = swgu[:, c, :] if shared else wgu[:, bass.ds(e * 2048 + 512 * c, 512)]
                    last = mm(gb[k.buf][:], rowsT[:, k.buf, c, :], w, start=(c == 0), stop=(c == 3))
                    if c == 2 and between:
                        turn_act(between)
                last.then_inc(gu_mm, 1)

            def turn_act(k):
                pe.wait_ge(act_ready, k.n + 1)
                after(pe, at_ready, k.n - 1)
                for c in range(2):
                    o = INNER * k.buf + P * c
                    last = nc.tensor.transpose(ab[:, o:o + P], act_in[:, k.buf, P * c:P * c + P], ident)
                last.then_inc(at_mm, 1)

            def down(k, shared):
                pe.wait_ge(at_ready, k.n + 1)
                after(pe, y_ready, k.n - 1)
                if not shared:
                    pe.wait_ge(wd_in[k.buf], 16 * (k.round - SEQS // 2 + 1))
                for c in range(2):
                    w = swd[:, c, :] if shared else wd[:, k.buf, c, :]
                    last = mm(yb[k.buf][:], actT[:, k.buf, c, :], w, start=(c == 0), stop=(c == 1))
                last.then_inc(dn_mm, 1)

            def ranks():
                pe.wait_ge(member_ready, 1)
                tri, ones = cb[:, B_TRI:B_TRI + P], cb[:, B_ONES:B_ONES + P]
                m = member[:].rearrange("p n e -> p (n e)")
                mm(rb[:, 0:256], tri, m, start=True, stop=False)
                for t in range(SEQS - 1):
                    later = SEQS - 1 - t
                    last = mm(rb[:, 16 * (t + 1):256].rearrange("p (n e) -> p n e", e=EXPERTS), ones,
                              member[:, t:t + 1, :].to_broadcast([P, later, EXPERTS]),
                              start=False, stop=(later == 1))
                last.then_inc(rank_mm, 1)
                pe.wait_ge(ranks_read, 1)
                for t in range(SEQS):
                    last = mm(rb[:, 0:EXPERTS], ones, member[:, t, :], start=(t == 0), stop=(t == SEQS - 1))
                last.then_inc(rank_mm, 1)
                pe.wait_ge(counts_read, 1)
                mm(rb[:, 0:TABLE], ones, cb[:, B_ZERO:B_ZERO + TABLE], start=True,
                   stop=False).then_inc(table_mm, 1)

            def chunk(trip):
                pe.wait_ge(hot_ready, trip + 1)
                for q in range(8):
                    last = mm(rb[:, 0:TABLE], hot_row[:, q, :], hot_col[:, q, :, :].rearrange("p g b -> p (g b)"),
                              start=False, stop=False)
                last.then_inc(table_mm, 1)

            def tables():
                mm(rb[:, 0:TABLE], cb[:, B_ONES:B_ONES + P], cb[:, B_ZERO:B_ZERO + TABLE], start=False,
                   stop=True).then_inc(table_mm, 1)

            pe.wait_ge(shared_in, 32)
            turn_rows(Turn(0, 0, 2), True)

            def pe_step(k, shared):
                if not shared and k.first == SEQS:
                    pe.wait_ge(experts_in, 16 * EXPERTS)
                prev = k.plus(-1)
                prev_shared = shared or (k.first == SEQS and isinstance(k.trip, int))
                gate_up(k, shared, prev)
                if not (isinstance(k.n, int) and k.n == SEQS + BLOCKS - 1):
                    turn_rows(k.plus(1), shared and not (isinstance(k.n, int) and k.n == SEQS - 1))
                down(prev, prev_shared)

            gate_up(Turn(0, 0, 2), True)
            turn_rows(Turn(1, 0, 2), True)
            pe_step(Turn(1, 0, 2), True)
            for k in range(2, 6):
                pe_step(Turn(k, 0, 2), True)
            ranks()
            with pe.Fori(0, 4) as trip:
                for k in range(2):
                    pe_step(Turn(6 + k, trip, 2), True)
                chunk(trip)
            tables()
            pe_step(Turn(14, 0, 2), True)
            pe_step(Turn(15, 0, 2), True)
            pe_step(Turn(16, 0, 2), False)
            pe_step(Turn(17, 0, 2), False)
            with pe.Fori(0, (BLOCKS - 3) // 2) as trip:
                for k in range(2):
                    pe_step(Turn(SEQS + 2 + k, trip, 2), False)
            pe_step(Turn(SEQS + BLOCKS - 1, 0, 2), False)
            turn_act(Turn(SEQS + BLOCKS - 1, 0, 2))
            down(Turn(SEQS + BLOCKS - 1, 0, 2), False)

        @block.scalar
        def _(act):
            act.wait_ge(weights_in, 16)
            act.wait_ge(beff_mm, 1)
            nc.scalar.activation(beff, misc[0][:, 0:1], ACT.Identity, bias=wsm[:, BO:BO + 1]).then_inc(beff_ready, 1)
            act.wait_ge(beff_ready, 1)

            def copy_out(c, hg):
                act.wait_ge(pv_done, UNITS * c.n + UNITS - 1 + hg)
                after(act, o_ready, 2 * c.n)
                nc.scalar.copy(ounorm[hg], oacc[hg][:]).then_inc(o_copied[hg], 1)

            def step(i):
                b, c, d, e = i.plus(-1), i.plus(-2), i.plus(1), i.plus(-3)
                for u in range(UNITS):
                    if has(i, -1):
                        blk = u // 2
                        _, w, _ = window(blk)
                        after(act, pv_done, UNITS * b.n + u - 3)
                        for half in range(2):
                            act.wait_ge(s2_ready, 2 * UNITS * b.n + 2 * u + half + 1)
                            nc.scalar.activation(
                                probs[u % 4][:, 2 * half:2 * half + 2, 0:w],
                                s2[half][:].rearrange("p (j c) -> p j c", j=2)[:, :, 0:w],
                                ACT.Exp, scale=D ** -0.5).then_inc(exp_ready, 1)
                    if u < 2 and has(i, -2):
                        copy_out(c, u)
                    if u == 0 and has(i, 1):
                        act.wait_ge(q_mm, d.n + 1)
                        first_part_free(d)
                        nc.scalar.activation(qparts[:, 0, :], misc[1][:], ACT.Identity,
                                             bias=wsm[:, BQ:BQ + 1]).then_inc(q_p1, 1)
                    if u == 1 and has(i, 1):
                        act.wait_ge(q_res, d.n + 1)
                        nc.scalar.copy(qparts[:, 1, :], qres).then_inc(q_p2, 1)
                        act.wait_ge(k_mm, d.n + 1)
                        nc.scalar.activation(kparts[:, 0, :], misc[1][:], ACT.Identity,
                                             bias=wsm[:, BK:BK + 1]).then_inc(k_p1, 1)
                    if u == 2 and has(i, 1):
                        act.wait_ge(k_res, d.n + 1)
                        nc.scalar.copy(kparts[:, 1, :], kres).then_inc(k_p2, 1)
                        act.wait_ge(v_mm, d.n + 1)
                        nc.scalar.copy(vaug[d.buf][:, :, :, 0:D].rearrange("p b h d -> p (b h) d"),
                                       misc[0][:].rearrange("p (g d) -> p g d", d=D)).then_inc(v_ready, 1)
                    if u == 3 and has(i, -3):
                        act.wait_ge(xt_mm, e.n + 1)
                        nc.scalar.copy(xn2T.rearrange("p a b -> p (a b)"), misc[1][:]).then_inc(xt_ready, 1)
                    if u == 4 and has(i, -3):
                        act.wait_ge(router_mm, e.n + 1)
                        nc.scalar.activation(logitT[0:EXPERTS, :], misc[0][0:EXPERTS, 0:P], ACT.Identity,
                                             bias=wsm[0:EXPERTS, BR:BR + 1]).then_inc(lt_ready, 1)
                    if u == 6 and has(i, -2):
                        act.wait_ge(proj_mm, c.n + 1)
                        after(act, gated_ready, c.n)
                        nc.scalar.activation(relu_o, misc[0][:], ACT.Relu, bias=beff).then_inc(relu_ready, 1)

            def first_part_free(d):
                prev = d.plus(-1)
                if not isinstance(d.n, int) or d.n >= 1:
                    act.wait_ge(stack_in[prev.buf], STACK_DMAS * (prev.round + 1))

            attention_steps(act, step)

            tb, gb, ab = bank[0:2], bank[2:4], bank[4]
            act.wait_ge(setup, 5)
            act.dma_start(out_rows[TOKENS:TOKENS + P, :], y_out[:, 1, :]).then_inc(spare_stored, 16)
            for b in range(3):
                act.wait_ge(xn_stored[b], 16 * len(range(b, SEQS, 3)))

            def load_rows(k):
                after(act, t_mm, k.n - 1)
                act.dma_start(rows[:, k.buf, :], xn_rows[bass.ds(k.n * P, P), :]).then_inc(rows_in[k.buf], 16)

            def rows_copy(k):
                act.wait_ge(t_mm, k.n + 1)
                after(act, gu_mm, k.n - 1)
                nc.scalar.copy(rowsT[:, k.buf, :, :].rearrange("p a b -> p (a b)"), tb[k.buf][:]).then_inc(t_ready, 1)

            def act_copy(k):
                act.wait_ge(at_mm, k.n + 1)
                after(act, dn_mm, k.n - 1)
                nc.scalar.copy(actT[:, k.buf, :, :].rearrange("p a b -> p (a b)"),
                               ab[:, INNER * k.buf:INNER * k.buf + INNER]).then_inc(at_ready, 1)

            def silu(k):
                act.wait_ge(gu_mm, k.n + 1)
                after(act, at_mm, k.n - 1)
                nc.scalar.activation(act_in[:, k.buf, :], gb[k.buf][:, 0:INNER], ACT.Silu).then_inc(silu_ready, 1)

            def store_shared(k):
                act.wait_ge(y_ready, k.n + 1)
                act.dma_start(out_rows[bass.ds(k.n * P, P), :], y_out[:, k.buf, :]).then_inc(y_stored[k.buf], 16)

            load_rows(Turn(0, 0, 2))
            load_rows(Turn(1, 0, 2))
            act.wait_ge(shifted, 1)
            nc.scalar.activation(logits[:], logits[:], ACT.Exp).then_inc(exp_done, 1)
            rows_copy(Turn(0, 0, 2))

            def step_experts(k, load, store):
                act_copy(k.plus(-1))
                rows_copy(k.plus(1))
                if load:
                    load_rows(k.plus(2))
                silu(k)
                if store:
                    store_shared(k.plus(-1))

            rows_copy(Turn(1, 0, 2))
            load_rows(Turn(2, 0, 2))
            silu(Turn(0, 0, 2))
            step_experts(Turn(1, 0, 2), True, True)
            for k in range(2, 4):
                step_experts(Turn(k, 0, 2), True, True)
            with act.Fori(0, 5) as trip:
                for k in range(2):
                    step_experts(Turn(4 + k, trip, 2), True, True)
            for k in range(14, 17):
                step_experts(Turn(k, 0, 2), False, True)
            with act.Fori(0, (BLOCKS - 3) // 2) as trip:
                for k in range(2):
                    step_experts(Turn(SEQS + 1 + k, trip, 2), False, False)
            step_experts(Turn(SEQS + BLOCKS - 2, 0, 2), False, False)
            last = Turn(SEQS + BLOCKS - 1, 0, 2)
            act_copy(last.plus(-1))
            silu(last)
            act_copy(last)

        @block.vector
        def _(dve):
            v = nc.vector
            for b in range(3):
                v.memset(vaug[b][:, :, :, D:2 * D], 1.0).then_inc(setup, 1)
            v.memset(y_out[:, 1, :], 0.0).then_inc(setup, 1)
            dve.wait_ge(consts_in, 32)
            v.tensor_copy(cb[:], cb_f).then_inc(setup, 1)
            dve.wait_ge(weights_in, 16)

            def normalise(which, n, src, dst, rstd_sem, ready):
                dve.wait_ge(rstd_sem, n + 1)
                v.tensor_scalar(dst, src, moments[:, which, 0:1], rstd[:, which:which + 1],
                                ALU.subtract, ALU.mult).then_inc(ready, 1)

            def moments_of(which, n, src, st, mom, before):
                stand(dve, DVE, before, n)
                v.bn_stats(stats[:, which, :], src).then_inc(st, 1)
                stand(dve, DVE, st, n + 1)
                v.bn_aggr(moments[:, which, :], stats[:, which, :]).then_inc(mom, 1)

            def seq(n):
                return X[:, bass.ds(n, 1), :].rearrange("p a t -> p (a t)")

            def maximum(s, su, half):
                blk, hg = su // 2, su % 2
                _, w, _ = window(blk)
                h = 4 * hg + 2 * half
                dve.wait_ge(s1_ready, 2 * UNITS * s.n + 2 * su + half + 1)
                v.tensor_reduce(negmax[:, h:h + 2, blk:blk + 1],
                                s1[half][:].rearrange("p (j c) -> p j c", j=2)[:, :, 0:w],
                                AX.X, ALU.max, negate=True).then_inc(rowmax, 1)

            def reciprocals(c):
                dve.wait_ge(dens_in[c.buf], 32 * (c.round + 1))
                if not isinstance(c.n, int) or c.n >= 1:
                    prev = c.plus(-1)
                    stand(dve, DVE, recips_in[prev.buf], 48 * (prev.round + 1))
                v.reciprocal(recips, dens).then_inc(recip_step, 1)

            def step(i):
                a, c, d, e, f = i, i.plus(-2), i.plus(1), i.plus(-3), i.plus(2)
                for u in range(UNITS):
                    if u == 0 and has(i, -3):
                        dve.wait_ge(ct_mm, e.n + 1)
                        v.scalar_tensor_tensor(seq(e.n), misc[0][:], wsm[:, BCT:BCT + 1], seq(e.n),
                                               ALU.add, ALU.add).then_inc(x2_ready, 1)
                    if u == UNITS - 2 and has(i, 0):
                        dve.wait_ge(m_step, 4 * a.n + 2)
                    if u == 7 and has(i, -2):
                        dve.wait_ge(relu_ready, c.n + 1)
                        dve.wait_ge(enc_in[c.buf], 16 * (c.round + 1))
                        v.tensor_tensor(gated, relu_o, enc[c.buf], ALU.mult).then_inc(gated_ready, 1)
                    if rowmax_unit(i, u):
                        maximum(*rowmax_unit(i, u), 0)
                    if rowmax_unit(i, u):
                        maximum(*rowmax_unit(i, u), 1)
                    if u == 0 and has(i, 1):
                        dve.wait_ge(q_p1, d.n + 1)
                        after(dve, q_p3, d.n)
                        v.scalar_tensor_tensor(qres, misc[1][:], wsm[:, BQ:BQ + 1], qparts[:, 0, :],
                                               ALU.add, ALU.subtract).then_inc(q_res, 1)
                    if u == 1 and has(i, -3):
                        stand(dve, DVE, x2_ready, e.n + 1)
                        moments_of(1, e.n, seq(e.n), stats2, mom2, xn2_ready)
                    if u == 2 and has(i, -2):
                        reciprocals(c)
                    if u == 2 and has(i, 1):
                        dve.wait_ge(k_p1, d.n + 1)
                        after(dve, k_p3, d.n)
                        v.scalar_tensor_tensor(kres, misc[1][:], wsm[:, BK:BK + 1], kparts[:, 0, :],
                                               ALU.add, ALU.subtract).then_inc(k_res, 1)
                    if u == 2 and has(i, -3):
                        if not isinstance(e.n, int) or e.n >= 1:
                            prev = e.plus(-1)
                            dve.wait_ge(xn_stored[prev.buf], 16 * (prev.round + 1))
                            dve.wait_ge(xt_mm, e.n)
                        normalise(1, e.n, seq(e.n), xn2, rstd2, xn2_ready)
                    if u == 3 and has(i, 2):
                        if isinstance(f.n, int) and f.n in (0, 1, 4):
                            dve.wait_ge(x_in[{0: 0, 1: 1, 4: 2}[f.n]], 16)
                        moments_of(0, f.n, seq(f.n), stats1, mom1, xn1_ready)
                    if u == 5 and has(i, -2):
                        for g in range(2):
                            dve.wait_ge(den_mm, 2 * c.n + g + 1)
                            v.tensor_tensor(onorm[g], ounorm[g], misc[g][:], ALU.mult).then_inc(o_ready, 1)
                    if u == 5 and has(i, 2):
                        if has(i, 1):
                            dve.wait_ge(v_mm, d.n + 1)
                        normalise(0, f.n, seq(f.n), xn1, rstd1, xn1_ready)
                    if u == 6 and has(i, 0):
                        dve.wait_ge(m_mm, a.n + 1)
                        if not isinstance(a.n, int) or a.n >= 1:
                            prev = a.plus(-1)
                            dve.wait_ge(max_in[prev.buf], 16 * (prev.round + 1))
                        v.tensor_copy(mrows[0:96, :], misc[1][:].bitcast(BF16)[0:96, 0:P]).then_inc(m_rows, 1)
                if has(i, -3):
                    dve.wait_ge(l_mm, e.n + 1)
                    v.tensor_copy(logits[:, bass.ds(e.n, 1), :].rearrange("p a t -> p (a t)"),
                                  misc[1][:, 0:EXPERTS]).then_inc(l_ready, 1)

            attention_steps(dve, step)

            yb, gb, rb = bank[5:7], bank[2:4], bank[7]
            linked = [0]

            def link(ins):
                linked[0] += 1
                ins.then_inc(route, 1)
                dve.wait_ge(route, linked[0])

            def each(ap):
                return ap.unsqueeze(2).to_broadcast([P, SEQS, EXPERTS])

            def flat(ap):
                return ap.rearrange("p a b -> p (a b)")

            def routing_choice():
                rev = cf[:, C_REV:C_REV + EXPERTS].unsqueeze(1).to_broadcast([P, SEQS, EXPERTS])
                dve.wait_ge(l_ready, SEQS)
                link(v.tensor_reduce(pick[:, 0, :], logits[:], AX.X, ALU.max))
                v.tensor_tensor(logits[:], logits[:], each(pick[:, 0, :]), ALU.subtract).then_inc(shifted, 1)
                dve.wait_ge(exp_done, 1)
                link(v.tensor_reduce(pick[:, 0, :], logits[:], AX.X, ALU.add))
                link(v.reciprocal(pick[:, 1, :], pick[:, 0, :]))
                link(v.tensor_tensor(logits[:], logits[:], each(pick[:, 1, :]), ALU.mult))
                for k in range(2):
                    link(v.tensor_reduce(top[:, k, :], logits[:], AX.X, ALU.max))
                    link(v.tensor_tensor(tmp[:], logits[:], each(top[:, k, :]), ALU.is_equal))
                    link(v.tensor_tensor(tmp[:], tmp[:], rev, ALU.mult))
                    link(v.tensor_reduce(pick[:, k, :], tmp[:], AX.X, ALU.max))
                    link(v.tensor_tensor(hot[:, k, :, :], rev, each(pick[:, k, :]), ALU.is_equal))
                    if k == 0:
                        link(v.scalar_tensor_tensor(flat(logits[:]), flat(hot[:, 0, :, :]), -2.0,
                                                    flat(logits[:]), ALU.mult, ALU.add))
                v.tensor_tensor(member[:], hot[:, 0, :, :], hot[:, 1, :, :], ALU.add).then_inc(member_ready, 1)

            def routing_slots():
                link(v.tensor_tensor(pick[:, 0, :], top[:, 0, :], top[:, 1, :], ALU.add))
                link(v.tensor_scalar(pick[:, 0, :], pick[:, 0, :], 1e-9, None, ALU.add))
                link(v.reciprocal(pick[:, 1, :], pick[:, 0, :]))
                link(v.tensor_tensor(top[:], top[:], pick[:, 1:2, :].to_broadcast([P, 2, SEQS]), ALU.mult))
                gates = flat(top[:])
                link(v.tensor_copy(gate_parts[:, 0, :], gates))
                link(v.tensor_tensor(gate_res[:], gates, gate_parts[:, 0, :], ALU.subtract))
                link(v.tensor_copy(gate_parts[:, 1, :], gate_res[:]))
                link(v.tensor_tensor(gate_parts[:, 2, :], gate_res[:], gate_parts[:, 1, :], ALU.subtract))
                v.tensor_copy(vals[:, :, 2:5], gate_parts[:].rearrange("p g q -> p q g"))
                v.tensor_copy(vals[:, :, 0:1], cf[:, C_TILE:C_TILE + 32].unsqueeze(2))
                link(v.tensor_copy(vals[:, :, 1:2],
                                   cf[:, C_ROW1:C_ROW1 + 1].unsqueeze(1).to_broadcast([P, 2 * SEQS, 1])))
                dve.wait_ge(rank_mm, 1)
                v.tensor_copy(flat(tmp[:]), rb[:, 0:256]).then_inc(ranks_read, 1)
                dve.wait_ge(ranks_read, 1)
                dve.wait_ge(rank_mm, 2)
                v.tensor_copy(count[:, 0, :], rb[:, 0:EXPERTS]).then_inc(counts_read, 1)
                dve.wait_ge(counts_read, 1)
                link(v.tensor_scalar(count_i[:], count[:, 0, :], 127.0, None, ALU.add))
                link(v.tensor_scalar(count_i[:], count_i[:], 7, None, ALU.arith_shift_right))
                link(v.tensor_copy(count[:, 1, :], count_i[:]))
                link(v.tensor_tensor_scan(count[:, 2, :], cf[:, C_ONE:C_ONE + EXPERTS], count[:, 1, :], 0.0,
                                          ALU.mult, ALU.add))
                link(v.tensor_tensor(count[:, 3, :], count[:, 2, :], count[:, 1, :], ALU.subtract))
                link(v.tensor_scalar(count[:, 3, :], count[:, 3, :], float(P), None, ALU.mult))
                link(v.tensor_tensor(tmp[:], tmp[:],
                                     count[:, 3:4, :].to_broadcast([P, SEQS, EXPERTS]), ALU.add))
                for k in range(2):
                    link(v.tensor_tensor(logits[:], hot[:, k, :, :], tmp[:], ALU.mult))
                    link(v.tensor_reduce(small[:, 0, SEQS * k:SEQS * (k + 1)], logits[:], AX.X, ALU.add))
                link(v.tensor_copy(small_i[:, 0, :], small[:, 0, :]))
                link(v.tensor_scalar(small_i[:, 1, :], small_i[:, 0, :], 7, None, ALU.arith_shift_right))
                link(v.tensor_scalar(small_i[:, 0, :], small_i[:, 0, :], P - 1, None, ALU.bitwise_and))
                v.tensor_copy(small[:, 1, :], small_i[:, 1, :])
                link(v.tensor_copy(small[:, 2, :], small_i[:, 0, :]))
                link(v.tensor_tensor(before, cf[:, C_IOTA:C_IOTA + BLOCKS].unsqueeze(2)
                                     .to_broadcast([P, BLOCKS, EXPERTS]),
                                     count[:, 2:3, :].to_broadcast([P, BLOCKS, EXPERTS]), ALU.is_ge))
                link(v.tensor_reduce(expert_of[:], before, AX.X, ALU.add))
                link(v.tensor_scalar(expert_i[:], expert_of[:], float(EXPERTS - 1), None, ALU.min))

            def routing_chunk(trip):
                dve.wait_ge(table_mm, trip + 1)
                rows_of = small[:, 2, :][:, bass.ds(trip * 8, 8)]
                blocks_of = small[:, 1, :][:, bass.ds(trip * 8, 8)]
                v.tensor_tensor(hot_row, cf[:, C_IOTA:C_IOTA + P].unsqueeze(1).to_broadcast([P, 8, P]),
                                rows_of.unsqueeze(2).to_broadcast([P, 8, P]), ALU.is_equal)
                v.tensor_tensor(hot_block, cf[:, C_IOTA:C_IOTA + BLOCKS].unsqueeze(1).to_broadcast([P, 8, BLOCKS]),
                                blocks_of.unsqueeze(2).to_broadcast([P, 8, BLOCKS]),
                                ALU.is_equal).then_inc(hot_blocks, 1)
                dve.wait_ge(hot_blocks, trip + 1)
                v.tensor_tensor(hot_col, hot_block.unsqueeze(2).to_broadcast([P, 8, 5, BLOCKS]),
                                vals[:, bass.ds(trip * 8, 8), :].unsqueeze(3).to_broadcast([P, 8, 5, BLOCKS]),
                                ALU.mult).then_inc(hot_ready, 1)

            def routing_tables():
                dve.wait_ge(table_mm, 6)
                link(v.tensor_copy(table, rb[:, 0:TABLE]))
                part = lambda g: table[:, g * BLOCKS:(g + 1) * BLOCKS]
                link(v.scalar_tensor_tensor(slot[:, 0, :], part(0), float(P), part(1), ALU.mult, ALU.add))
                link(v.tensor_scalar(slot[:, 1, :], slot[:, 0, :], 0.0, cf[:, C_SPARE:C_SPARE + 1],
                                     ALU.is_equal, ALU.mult))
                v.tensor_scalar(gather_i[:], slot[:, 0, :], -1.0, 0.0, ALU.add, ALU.max)
                v.scalar_tensor_tensor(scatter_i[:], slot[:, 0, :], -1.0, slot[:, 1, :], ALU.add, ALU.add)
                link(v.tensor_tensor(slot[:, 2, :], part(2), part(3), ALU.add))
                v.tensor_tensor(gate_of[:], slot[:, 2, :], part(4), ALU.add).then_inc(tables_ready, 1)

            def activate(k):
                dve.wait_ge(silu_ready, k.n + 1)
                v.tensor_tensor(act_in[:, k.buf, :], act_in[:, k.buf, :], gb[k.buf][:, INNER:2 * INNER],
                                ALU.mult).then_inc(act_ready, 1)

            def result(k, shared):
                dve.wait_ge(dn_mm, k.n + 1)
                if shared or k.first in (SEQS, SEQS + 1) and isinstance(k.trip, int):
                    after(dve, y_stored[k.buf], 16 * k.round)
                else:
                    dve.wait_ge(added[k.buf], 16 * (k.round - SEQS // 2))
                if shared:
                    v.tensor_tensor(y_out[:, k.buf, :], yb[k.buf][:], seq(k.n), ALU.add).then_inc(y_ready, 1)
                else:
                    v.tensor_scalar(y_out[:, k.buf, :], yb[k.buf][:], gate_of[:, bass.ds(k.n - SEQS, 1)],
                                    None, ALU.mult).then_inc(y_ready, 1)

            def step_experts(k, shared):
                activate(k)
                result(k.plus(-1), shared)

            routing_choice()
            activate(Turn(0, 0, 2))
            dve.wait_ge(spare_stored, 16)
            step_experts(Turn(1, 0, 2), True)
            for k in range(2, 6):
                step_experts(Turn(k, 0, 2), True)
            routing_slots()
            with dve.Fori(0, 4) as trip:
                routing_chunk(trip)
                for k in range(2):
                    step_experts(Turn(6 + k, trip, 2), True)
            step_experts(Turn(14, 0, 2), True)
            routing_tables()
            step_experts(Turn(15, 0, 2), True)
            step_experts(Turn(16, 0, 2), True)
            dve.wait_ge(tables_ready, 1)
            step_experts(Turn(SEQS + 1, 0, 2), False)
            step_experts(Turn(SEQS + 2, 0, 2), False)
            with dve.Fori(0, (BLOCKS - 3) // 2) as trip:
                for k in range(2):
                    step_experts(Turn(SEQS + 3 + k, trip, 2), False)
            result(Turn(SEQS + BLOCKS - 1, 0, 2), False)


def constants():
    import numpy as np

    r, c = np.arange(P)[:, None], np.arange(P)[None, :]
    f = np.zeros((P, C_END), np.float32)
    f[:, C_ID:C_ID + P] = r == c
    f[:, C_IOTA:C_IOTA + P] = c
    f[:, C_REV:C_REV + EXPERTS] = EXPERTS - np.arange(EXPERTS)
    f[:, C_TILE:C_TILE + 32] = np.arange(32) % SEQS
    f[:, C_ONE:C_ONE + EXPERTS] = 1.0
    f[:, C_ROW1] = np.arange(P) + 1
    f[:, C_SPARE] = np.arange(P) + TOKENS + 1
    f[:, C_HALF] = -0.5
    b = np.zeros((P, B_END), np.float32)
    b[:, B_ID:B_ID + P] = r == c
    off = np.arange(2 * P)[None, :] - r
    b[:, B_MASK:B_MASK + 2 * P] = np.where((off >= 0) & (off <= 2 * LOCAL), 0.0, MASKED)
    b[:, B_TRI:B_TRI + P] = r < c
    for g in range(2):
        b[:3 * HEADS, B_SEL + P * g:B_SEL + P * g + P] = (r % HEADS == 4 * g + c // 32)[:3 * HEADS]
    b[:, B_ONES:B_ONES + P] = 1.0
    return f, b


def kernel(**inputs):
    import numpy as np
    import concourse.bacc as bacc
    from concourse.bass_utils import run_bass_kernel_spmd

    a = {k: np.asarray(v) for k, v in inputs.items()}
    w_in, b_in, w_out = a["L0_xattn_w_in"], a["L0_xattn_b_in"], a["L0_xattn_w_out"]
    w_small = np.zeros((P, W_END), np.float32)
    for i, col in enumerate((W_Q, W_K)):
        w = w_in[P * i:P * i + P].reshape(HEADS, D, P).transpose(1, 0, 2).reshape(P, P)
        w_small[:, col:col + P] = w.T
        w_small[:, W_BIAS + i] = b_in[P * i:P * i + P].reshape(HEADS, D).T.reshape(P)
    w_small[:, W_V:W_V + P] = w_in[2 * P:3 * P].T
    for h in range(HEADS):
        g, row = h // 4, 32 * (h % 4)
        w_small[row:row + D, W_O + P * g:W_O + P * g + P] = w_out[:, D * h:D * h + D].T
        w_small[row:row + D, BV0 + g] = b_in[2 * P + D * h:2 * P + D * h + D]
    w_small[:, W_CT:W_CT + P] = a["L0_xattn_w_ct"]
    w_small[:, W_R:W_R + 64] = a["L0_ffn_Wr"].reshape(EXPERTS, 4, P).transpose(2, 1, 0).reshape(P, 64)
    w_small[:, BO] = a["L0_xattn_b_out"]
    w_small[:, BCT] = a["L0_xattn_b_ct"]
    w_small[:EXPERTS, BR] = a["L0_ffn_bias"]

    gu = np.concatenate([a["L0_ffn_Wg"], a["L0_ffn_Wu"]], axis=2)
    sgu = np.concatenate([a["L0_ffn_sWg"], a["L0_ffn_sWu"]], axis=1)
    const_f, const_b = constants()
    arrays = {
        "x": a["x"], "ctx": a["ctx_2048"], "const_f": const_f, "const_b": const_b, "w_small": w_small,
        "w_gu": gu.reshape(EXPERTS, 4, P, 512).transpose(2, 0, 1, 3).reshape(P, EXPERTS, 2048),
        "w_d": a["L0_ffn_Wd"].reshape(EXPERTS, 2, P, T).transpose(0, 2, 1, 3).reshape(EXPERTS, P, 2 * T),
        "sw_gu": sgu.reshape(4, P, 512).transpose(1, 0, 2),
        "sw_d": a["L0_ffn_sWd"].reshape(2, P, T).transpose(1, 0, 2),
    }
    arrays = {k: np.ascontiguousarray(v) for k, v in arrays.items()}
    nc = bacc.Bacc("TRN2", target_bir_lowering=False, num_devices=1)
    args = [nc.dram_tensor(k, v.shape, mybir.dt.from_np(v.dtype), kind="ExternalInput").ap()
            for k, v in arrays.items()]
    out = nc.dram_tensor("out", (SEQS + 1, P, T), F32, kind="ExternalOutput").ap()
    xattn_moe_kernel(nc, *args, out)
    result = run_bass_kernel_spmd(nc, [arrays], core_ids=[0])
    return result.results[0]["out"][:SEQS]
```

```python
from contextlib import ExitStack

import concourse.bass as bass
from concourse import mybir

F32 = mybir.dt.float32
BF16 = mybir.dt.bfloat16
FR = mybir.dt.float32r
I32 = mybir.dt.int32
ALU = mybir.AluOpType
ACT = mybir.ActivationFunctionType
AX = mybir.AxisListType

P = 128
SEQS, T = 16, 512
HEADS, D = 8, 16
LOCAL = 64
QB = T // P
EPS = 1e-5
EXPERTS, INNER = 16, 256
TOKENS = SEQS * P
BLOCKS = 2 * TOKENS // P + EXPERTS - 1
Q_PARTS = (0, 0, 1, 0, 1, 2)
K_PARTS = (0, 1, 0, 2, 1, 0)
STACK = 6 * D
UNITS = 2 * QB
MASKED = -1e38

C_ID, C_IOTA, C_REV, C_TILE, C_ONE, C_ROW1, C_SPARE, C_HALF, C_END = 0, 128, 256, 272, 304, 320, 321, 322, 323
B_ID, B_MASK, B_TRI, B_ONES, B_SEL, B_ZERO, B_END = 0, 128, 384, 512, 640, 896, 1152
W_Q, W_K, W_V, W_O, W_CT, W_R, W_BIAS, W_END = 0, 128, 256, 384, 640, 768, 832, 840
BQ, BK, BV0, BV1, BO, BCT, BR = range(W_BIAS, W_BIAS + 7)
TABLE = 5 * BLOCKS


class Turn:

    def __init__(self, first, trip, step):
        self.first, self.trip, self.step = first, trip, step
        self.n = first if isinstance(trip, int) and trip == 0 else trip * step + first
        self.buf = first % step
        self.round = trip + first // step

    def plus(self, d):
        return Turn(self.first + d, self.trip, self.step)


def after(eng, sem, count):
    if isinstance(count, int) and count <= 0:
        return
    eng.wait_ge(sem, count)


def window(block):
    lo, hi = max(0, P * block - LOCAL), min(T, P * block + P + LOCAL)
    return lo, hi - lo, lo - (P * block - LOCAL)


def xattn_moe_kernel(nc, x, ctx_in, const_f, const_b, w_small, w_gu, w_d, sw_gu, sw_d, out):
    es = ExitStack()
    with es:
        def sb(name, shape, dt=F32):
            return es.enter_context(nc.sbuf_tensor(name, shape, dt))

        def sem(name):
            return es.enter_context(nc.semaphore(name))

        xn_rows = nc.dram_tensor("xn_rows", (TOKENS, T), F32).ap()
        out_rows = out.rearrange("a p t -> (a p) t")

        first = ExitStack()

        def sb_first(name, shape):
            return first.enter_context(nc.sbuf_tensor(name, shape, F32))

        X = sb_first("X", [P, SEQS, T])
        swgu = sb_first("swgu", [P, 4, 512])
        wd = sb_first("wd", [P, 2, 2, T])
        rowsT = sb_first("rowsT", [P, 2, 4, P])
        actT = sb_first("actT", [P, 2, 2, P])
        first.close()
        gu_parts = sb("gu_parts", [P, 2, 2, 2048], FR)
        wd_high = sb("wd_high", [P, 2, 2, T], FR)
        wd_low = sb("wd_low", [P, 2, 2, T], FR)
        rows_parts = sb("rows_parts", [P, 2, 4, P], FR)
        act_parts = sb("act_parts", [P, 2, 2, P], FR)
        wgu = sb("wgu", [P, EXPERTS * 4 * 512])
        cf = sb("cf", [P, C_END])
        cb = sb("cb", [P, B_END], BF16)
        logits = sb("logits", [P, SEQS, EXPERTS])
        swd = sb("swd", [P, 2, T])
        rows = sb("rows", [P, 2, T])
        act_in = sb("act_in", [P, 2, INNER])
        y_out = sb("y_out", [P, 2, T])

        used = [0]

        def over(shape, dt=F32):
            cols = 1
            for s in shape:
                cols *= s
            words = cols if dt is F32 else (cols + 1) // 2
            ap = wgu[:, used[0]:used[0] + words]
            used[0] += words
            assert used[0] <= EXPERTS * 4 * 512
            if dt is not F32:
                ap = ap.bitcast(dt)
            if len(shape) == 1:
                return ap
            names = " ".join("abc"[:len(shape)])
            return ap.rearrange(f"p ({names}) -> p {names}", **{"abc"[i]: s for i, s in enumerate(shape)})

        qstack = [over([HEADS, T], BF16) for _ in range(3)]
        kstack = [over([HEADS, T], BF16) for _ in range(3)]
        vaug = [over([QB, HEADS, 32]) for _ in range(3)]
        enc = [over([T]) for _ in range(3)]
        xn1 = over([T])
        qparts = over([3, T], BF16)
        kparts = over([3, T], BF16)
        qres = over([T])
        kres = over([T])
        probs = [over([4, 2 * P]) for _ in range(4)]
        ounorm = [over([T]) for _ in range(2)]
        onorm = [over([T]) for _ in range(2)]
        dens = over([HEADS * T // P])
        recips = over([HEADS * T // P])
        recip_res = over([HEADS * T // P])
        recip_parts = over([3, HEADS * T // P], BF16)
        recip_rows = over([T], BF16)
        relu_o = over([T])
        gated = over([T])
        xn2 = over([T])
        xn2T = over([4, P])
        logitT = over([P])
        negmax = over([HEADS, QB])
        mres = over([HEADS * QB])
        mparts = over([3, HEADS * QB], BF16)
        mrows = over([P], BF16)
        wsm = over([W_END])
        beff = over([1])
        cb_f = over([B_END])
        stats = over([2, 6])
        moments = over([2, 2])
        rstd = over([2])
        epsd = over([2])

        top = sb("top", [P, 2, SEQS])
        pick = sb("pick", [P, 2, SEQS])
        hot = sb("hot", [P, 2, SEQS, EXPERTS], BF16)
        tmp = sb("tmp", [P, SEQS, EXPERTS])
        member = sb("member", [P, SEQS, EXPERTS], BF16)
        count = sb("count", [P, 4, EXPERTS])
        count_i = sb("count_i", [P, EXPERTS], I32)
        small = sb("small", [P, 6, SEQS * 2])
        small_i = sb("small_i", [P, 2, SEQS * 2], I32)
        gate_parts = sb("gate_parts", [P, 3, SEQS * 2], BF16)
        gate_res = sb("gate_res", [P, SEQS * 2])
        expert_of = sb("expert_of", [P, BLOCKS])
        expert_i = sb("expert_i", [P, BLOCKS], I32)
        slot = sb("slot", [P, 4, BLOCKS])
        gather_i = sb("gather_i", [P, BLOCKS], I32)
        scatter_i = sb("scatter_i", [P, BLOCKS], I32)
        gate_of = sb("gate_of", [P, BLOCKS])
        gather_now = sb("gather_now", [P, 2], I32)
        scatter_now = sb("scatter_now", [P, 2], I32)
        vals = sb("vals", [P, 2 * SEQS, 5])
        wd_flat = wd[:].rearrange("p a b c -> p (a b c)")
        hot_row = wd_flat[:, 0:512].bitcast(BF16).rearrange("p (q r) -> p q r", q=8)
        hot_col = wd_flat[:, 512:512 + 4 * TABLE].bitcast(BF16).rearrange("p (q g b) -> p q g b", q=8, g=5)
        before = wd_flat[:, 0:BLOCKS * EXPERTS].rearrange("p (b e) -> p b e", b=BLOCKS)
        table = wd_flat[:, 1500:1500 + TABLE]
        hot_block = wd_flat[:, 1750:1750 + 4 * BLOCKS].bitcast(BF16).rearrange("p (q b) -> p q b", q=8)

        bank = [es.enter_context(nc.psum_tensor(f"bank{i}", [P, 512], F32)) for i in range(8)]
        s1, s2, oacc, misc = bank[0:2], bank[2:4], bank[4:6], bank[6:8]

        consts_in, weights_in, shared_in = sem("consts_in"), sem("weights_in"), sem("shared_in")
        x_in = [sem(f"x_in{i}") for i in range(3)]
        enc_in = [sem(f"enc_in{i}") for i in range(3)]
        stack_in = [sem(f"stack_in{i}") for i in range(3)]
        max_in = [sem(f"max_in{i}") for i in range(3)]
        xn_stored = [sem(f"xn_stored{i}") for i in range(3)]
        experts_in = sem("experts_in")
        rows_in = [sem(f"rows_in{i}") for i in range(2)]
        wd_in = [sem(f"wd_in{i}") for i in range(2)]
        y_stored = [sem(f"y_stored{i}") for i in range(2)]
        gathered = [sem(f"gathered{i}") for i in range(2)]
        added = [sem(f"added{i}") for i in range(2)]
        spare_stored = sem("spare_stored")
        setup = sem("setup")
        ones_set = sem("ones_set")
        beff_mm, beff_ready = sem("beff_mm"), sem("beff_ready")
        stats1, mom1, eps1, rstd1, xn1_ready = (sem(s) for s in ("stats1", "mom1", "eps1", "rstd1", "xn1_ready"))
        stats2, mom2, eps2, rstd2, xn2_ready = (sem(s) for s in ("stats2", "mom2", "eps2", "rstd2", "xn2_ready"))
        q_mm, k_mm, v_mm = sem("q_mm"), sem("k_mm"), sem("v_mm")
        q_p1, q_res, q_p2, q_p3 = sem("q_p1"), sem("q_res"), sem("q_p2"), sem("q_p3")
        k_p1, k_res, k_p2, k_p3 = sem("k_p1"), sem("k_res"), sem("k_p2"), sem("k_p3")
        v_ready = sem("v_ready")
        s1_ready, rowmax = sem("s1_ready"), sem("rowmax")
        m_step, m_mm, m_rows = sem("m_step"), sem("m_mm"), sem("m_rows")
        s2_ready, exp_ready, pv_done = sem("s2_ready"), sem("exp_ready"), sem("pv_done")
        o_copied = [sem(f"o_copied{i}") for i in range(2)]
        dens_in = [sem(f"dens_in{i}") for i in range(3)]
        recips_in = [sem(f"recips_in{i}") for i in range(3)]
        den_mm, recip_step, o_ready = sem("den_mm"), sem("recip_step"), sem("o_ready")
        cut_ready = sem("cut_ready")
        proj_mm, relu_ready, gated_ready = sem("proj_mm"), sem("relu_ready"), sem("gated_ready")
        ct_mm, x2_ready = sem("ct_mm"), sem("x2_ready")
        xt_mm, xt_ready, router_mm, lt_ready, l_mm, l_ready = (
            sem(s) for s in ("xt_mm", "xt_ready", "router_mm", "lt_ready", "l_mm", "l_ready"))
        t_mm, t_ready, gu_mm, silu_ready, act_ready, at_mm, at_ready, dn_mm, y_ready = (
            sem(s) for s in ("t_mm", "t_ready", "gu_mm", "silu_ready", "act_ready", "at_mm", "at_ready",
                             "dn_mm", "y_ready"))
        route, shifted, exp_done = sem("route"), sem("shifted"), sem("exp_done")
        ranks_read, counts_read = sem("ranks_read"), sem("counts_read")
        gu_high, gu_low, rows_low, act_low = (sem(s) for s in ("gu_high", "gu_low", "rows_low", "act_low"))
        wd_split, wd_low0, wd_low1 = sem("wd_split"), sem("wd_low0"), sem("wd_low1")
        gather_set, scatter_set = sem("gather_set"), sem("scatter_set")
        member_ready, rank_mm, hot_blocks, hot_ready, table_mm, tables_ready = (
            sem(s) for s in ("member_ready", "rank_mm", "hot_blocks", "hot_ready", "table_mm", "tables_ready"))

        ident = cf[:, C_ID:C_ID + P]
        identb = cb[:, B_ID:B_ID + P]

        def mask(blk):
            lo, w, off = window(blk)
            return cb[:, B_MASK + off:B_MASK + off + w]

        STACK_DMAS = 12 * 16

        DVE, PE, POOL, SP, SCALAR = (sem(f"passed_{e}") for e in ("dve", "pe", "pool", "sp", "scalar"))

        def stand(eng, own, sem, count):
            after(eng, sem, count)
            if not isinstance(count, int):
                eng.sem_inc(own, 1)

        def attention_steps(eng, step):
            for i in range(-2, 4):
                step(Turn(i, 0, 3))
            with eng.Fori(0, 3) as trip:
                for k in range(3):
                    step(Turn(4 + k, trip, 3))
            for i in range(13, 19):
                step(Turn(i, 0, 3))

        def rowmax_unit(i, u):
            e = i if u < UNITS - 2 else i.plus(1)
            return (e, (u + 2) % UNITS) if has(e, 0) else None

        def has(i, d):
            return not isinstance(i.n, int) or 0 <= i.n + d < SEQS

        block = es.enter_context(nc.Block())

        @block.sync
        def _(sp):
            sp.dma_start(wsm, w_small).then_inc(weights_in, 16)
            sp.dma_start(X[:, 0, :], x[0]).then_inc(x_in[0], 16)
            sp.dma_start(cf[:], const_f).then_inc(consts_in, 16)
            sp.dma_start(cb_f, const_b).then_inc(consts_in, 16)
            sp.dma_start(X[:, 1:4, :], x[1:4].rearrange("n p t -> p n t")).then_inc(x_in[1], 16)
            sp.dma_start(X[:, 4:, :], x[4:].rearrange("n p t -> p n t")).then_inc(x_in[2], 16)
            sp.dma_start(swgu[:], sw_gu).then_inc(shared_in, 16)
            sp.dma_start(swd[:], sw_d).then_inc(shared_in, 16)

            def send(stack, parts, groups, sem):
                for g in groups:
                    which = (Q_PARTS if stack is qstack else K_PARTS)[g]
                    sp.dma_start(stack[sem[1]][D * g:D * g + D, :, :], parts[:, which, :]).then_inc(sem[0], 16)

            def load_expert(e):
                sp.dma_start(wgu[:, e * 2048:(e + 1) * 2048], w_gu[:, e, :]).then_inc(experts_in, 16)

            def step(i):
                d = i.plus(1)

                def denominators(g):
                    c = i.plus(-2)
                    sp.wait_ge(o_copied[g], c.n + 1)
                    sp.dma_start(dens[64 * g:64 * g + 64, :], ounorm[g][D:P:32, :]).then_inc(dens_in[c.buf], 16)

                c = i.plus(-2)
                if has(i, -2):
                    denominators(0)
                if has(i, 1):
                    stand(sp, SP, s2_ready, 2 * UNITS * (i.n - 1))
                    to = (stack_in[d.buf], d.buf)
                    sp.wait_ge(q_p1, d.n + 1)
                    send(qstack, qparts, (0, 1, 3), to)
                if has(i, -2):
                    denominators(1)
                if has(i, 1):
                    sp.wait_ge(q_p2, d.n + 1)
                    send(qstack, qparts, (2, 4), to)
                    sp.wait_ge(q_p3, d.n + 1)
                    send(qstack, qparts, (5,), to)
                if has(i, 1):
                    sp.wait_ge(k_p1, d.n + 1)
                    send(kstack, kparts, (0, 2, 5), to)
                if has(i, -2):
                    sp.wait_ge(recip_step, 5 * (c.n + 1))
                    for p in range(3):
                        sp.dma_start(recip_rows[HEADS * p:HEADS * p + HEADS, :],
                                     recip_parts[:, p, :]).then_inc(recips_in[c.buf], 16)
                if has(i, 1):
                    sp.wait_ge(k_p2, d.n + 1)
                    send(kstack, kparts, (1, 4), to)
                    sp.wait_ge(k_p3, d.n + 1)
                    send(kstack, kparts, (3,), to)
                if has(i, -3):
                    e = i.plus(-3)
                    sp.wait_ge(xn2_ready, e.n + 1)
                    sp.dma_start(xn_rows[bass.ds(e.n * P, P), :], xn2).then_inc(xn_stored[e.buf], 16)
                if has(i, 0):
                    after(sp, gated_ready, i.n - 2)
                    sp.dma_start(enc[i.buf], ctx_in[bass.ds(i.n, 1), :, :].rearrange("a p t -> (a p) t")
                                 ).then_inc(enc_in[i.buf], 16)
                    sp.wait_ge(m_rows, i.n + 1)
                    sp.dma_start(qstack[i.buf][STACK:STACK + 3, :, :], mrows[0:96, :]).then_inc(max_in[i.buf], 16)

                for n, end in ((SEQS - 3, SEQS - 1), (SEQS - 2, SEQS), (SEQS - 1, SEQS + 1)):
                    if isinstance(i.n, int) and i.n == end:
                        sp.wait_ge(s2_ready, 2 * UNITS * (n + 1))
                        load_expert(n % 3)
                        load_expert(3 + n % 3)

            attention_steps(sp, step)

            sp.wait_ge(l_ready, SEQS)
            for b in range(3):
                sp.wait_ge(xn_stored[b], 16 * len(range(b, SEQS, 3)))
            for e in range(6, EXPERTS):
                sp.wait_ge(silu_ready, e - 5)
                load_expert(e)

            sp.wait_ge(tables_ready, 1)

            def load_wd(k):
                stand(sp, SP, dn_mm, k.n - 1)
                e = sp.value_load(expert_i[0:1, bass.ds(k.n - SEQS, 1)], min_val=0, max_val=EXPERTS - 1)
                sp.dma_start(wd[:, k.buf, :, :].rearrange("p c n -> p (c n)"),
                             w_d[bass.ds(e, 1), :, :].rearrange("a p n -> (a p) n")).then_inc(wd_in[k.buf], 16)

            with sp.Fori(0, BLOCKS // 2) as trip:
                for k in range(2):
                    load_wd(Turn(SEQS + k, trip, 2))
            load_wd(Turn(SEQS + BLOCKS - 1, 0, 2))

        @block.gpsimd
        def _(pool):
            pool.wait_ge(consts_in, 32)

            def inverse_deviation(which, n, mom, eps, out_sem):
                stand(pool, POOL, mom, n + 1)
                nc.gpsimd.tensor_scalar(epsd[:, which:which + 1], moments[:, which, 1:2], EPS, None,
                                        ALU.add).then_inc(eps, 1)
                pool.wait_ge(eps, n + 1)
                nc.gpsimd.tensor_tensor(rstd[:, which:which + 1], epsd[:, which:which + 1],
                                        cf[:, C_HALF:C_HALF + 1], ALU.pow).then_inc(out_sem, 1)

            def third_part(n, res, to, p2_sem, p3_sem):
                stand(pool, POOL, p2_sem, n + 1)
                nc.gpsimd.tensor_tensor(to[:, 2, :], res, to[:, 1, :], ALU.subtract).then_inc(p3_sem, 1)

            def split_reciprocals(c):
                v = nc.gpsimd
                stand(pool, POOL, recip_step, 5 * c.n + 1)
                v.tensor_copy(recip_parts[:, 0, :], recips).then_inc(recip_step, 1)
                pool.wait_ge(recip_step, 5 * c.n + 2)
                v.tensor_tensor(recip_res, recips, recip_parts[:, 0, :], ALU.subtract).then_inc(recip_step, 1)
                stand(pool, POOL, recip_step, 5 * c.n + 3)
                v.tensor_copy(recip_parts[:, 1, :], recip_res).then_inc(recip_step, 1)
                pool.wait_ge(recip_step, 5 * c.n + 4)
                v.tensor_tensor(recip_parts[:, 2, :], recip_res, recip_parts[:, 1, :],
                                ALU.subtract).then_inc(recip_step, 1)

            def split_max(a):
                v = nc.gpsimd
                neg = negmax.rearrange("p a b -> p (a b)")
                stand(pool, POOL, m_mm, a.n)
                stand(pool, POOL, rowmax, 2 * UNITS * (a.n + 1))
                v.tensor_copy(mparts[:, 0, :], neg).then_inc(m_step, 1)
                pool.wait_ge(m_step, 4 * a.n + 1)
                v.tensor_tensor(mres, neg, mparts[:, 0, :], ALU.subtract).then_inc(m_step, 1)
                stand(pool, POOL, m_step, 4 * a.n + 2)
                v.tensor_copy(mparts[:, 1, :], mres).then_inc(m_step, 1)
                pool.wait_ge(m_step, 4 * a.n + 3)
                v.tensor_tensor(mparts[:, 2, :], mres, mparts[:, 1, :], ALU.subtract).then_inc(m_step, 1)

            def cut_band(b, u):
                blk = u // 2
                _, w, off = window(blk)
                stand(pool, POOL, exp_ready, 2 * UNITS * b.n + 2 * u + 2)
                before, behind = probs[u % 4][:, :, 0:P - off], probs[u % 4][:, :, P - off:w]
                nc.gpsimd.affine_select(out=before, in_=before, compare_op=ALU.is_ge, fill=0.0, base=off,
                                        pattern=[[0, 4], [1, P - off]], channel_multiplier=-1)
                nc.gpsimd.affine_select(out=behind, in_=behind, compare_op=ALU.is_ge, fill=0.0, base=0,
                                        pattern=[[0, 4], [-1, w - P + off]],
                                        channel_multiplier=1).then_inc(cut_ready, 1)

            def step(i):
                for u in range(UNITS):
                    if u == 2 and has(i, -2):
                        split_reciprocals(i.plus(-2))
                    if u == 3 and has(i, 1):
                        third_part(i.n + 1, kres, kparts, k_p2, k_p3)
                    if has(i, -1):
                        cut_band(i.plus(-1), u)
                    if u == 1 and has(i, 1):
                        third_part(i.n + 1, qres, qparts, q_p2, q_p3)
                    if u == 1 and has(i, -3):
                        inverse_deviation(1, i.n - 3, mom2, eps2, rstd2)
                    if u == 4 and has(i, 2):
                        inverse_deviation(0, i.n + 2, mom1, eps1, rstd1)
                    if u == 5 and has(i, 0):
                        split_max(i)
                if isinstance(i.n, int) and i.n <= 0:
                    pool.wait_ge(rstd1, i.n + 3)
                    after(pool, m_step, 4 * (i.n + 1))
                    nc.gpsimd.memset(kstack[i.n + 2][STACK:STACK + 3, :, :], 1.0).then_inc(ones_set, 1)
                    pool.wait_ge(ones_set, i.n + 3)

            attention_steps(pool, step)

            pool.wait_ge(tables_ready, 1)

            def gather(k):
                stand(pool, POOL, gathered[k.buf], 16 * (k.round - SEQS // 2))
                nc.gpsimd.tensor_copy(gather_now[:, k.buf:k.buf + 1],
                                      gather_i[:, bass.ds(k.n - SEQS, 1)]).then_inc(gather_set, 1)
                pool.wait_ge(gather_set, k.n - SEQS + 1)
                stand(pool, POOL, t_mm, k.n - 1)
                nc.gpsimd.indirect_dma_start(
                    rows[:, k.buf, :], None, xn_rows[:, :],
                    bass.IndirectOffsetOnAxis(ap=gather_now[:, k.buf:k.buf + 1], axis=0),
                    bounds_check=TOKENS - 1, oob_is_err=True).then_inc(gathered[k.buf], 16)

            def add_rows(k):
                for b in range(2):
                    stand(pool, POOL, added[b], 16 * ((k.round if b or not k.buf else k.round + 1) - SEQS // 2))
                nc.gpsimd.tensor_copy(scatter_now[:, k.buf:k.buf + 1],
                                      scatter_i[:, bass.ds(k.n - SEQS, 1)]).then_inc(scatter_set, 1)
                stand(pool, POOL, scatter_set, k.n - SEQS + 1)
                stand(pool, POOL, y_ready, k.n + 1)
                nc.gpsimd.indirect_dma_start(
                    out_rows[:, :], bass.IndirectOffsetOnAxis(ap=scatter_now[:, k.buf:k.buf + 1], axis=0),
                    y_out[:, k.buf, :], None, bounds_check=TOKENS + P - 1, oob_is_err=True,
                    compute_op=ALU.add).then_inc(added[k.buf], 16)

            def low_down(k):
                stand(pool, POOL, wd_split, k.n - SEQS + 1)
                nc.gpsimd.tensor_tensor(wd_low[:, k.buf, 1, :], wd[:, k.buf, 1, :], wd_high[:, k.buf, 1, :],
                                        ALU.subtract).then_inc(wd_low1, 1)

            AHEAD = 4
            for k in range(AHEAD):
                gather(Turn(SEQS + k, 0, 2))
            pool.wait_ge(spare_stored, 16)
            for b in range(2):
                pool.wait_ge(y_stored[b], 16 * (SEQS // 2))
            low_down(Turn(SEQS, 0, 2))
            for k in range(2):
                low_down(Turn(SEQS + k + 1, 0, 2))
                add_rows(Turn(SEQS + k, 0, 2))
                gather(Turn(SEQS + AHEAD + k, 0, 2))
            with pool.Fori(0, (BLOCKS - AHEAD) // 2 - 1) as trip:
                for k in range(2):
                    low_down(Turn(SEQS + 3 + k, trip, 2))
                    add_rows(Turn(SEQS + 2 + k, trip, 2))
                    gather(Turn(SEQS + 2 + AHEAD + k, trip, 2))
            for k in range((BLOCKS - AHEAD) // 2 * 2, BLOCKS):
                if k + 1 < BLOCKS:
                    low_down(Turn(SEQS + k + 1, 0, 2))
                add_rows(Turn(SEQS + k, 0, 2))
                if k + AHEAD < BLOCKS:
                    gather(Turn(SEQS + AHEAD + k, 0, 2))
            for b in range(2):
                pool.wait_ge(added[b], 16 * len(range(b, BLOCKS, 2)))

        @block.tensor
        def _(pe):
            mm = nc.tensor.matmul

            pe.wait_ge(weights_in, 16)
            for g in range(2):
                last = mm(misc[0][:, 0:1], wsm[:, W_O + P * g:W_O + P * g + P], wsm[:, BV0 + g:BV0 + g + 1],
                          start=(g == 0), stop=(g == 1))
            last.then_inc(beff_mm, 1)
            pe.wait_ge(consts_in, 32)
            pe.wait_ge(setup, 5)

            def step(i):
                b, c, d, e = i.plus(-1), i.plus(-2), i.plus(1), i.plus(-3)
                for u in range(UNITS):
                    if rowmax_unit(i, u):
                        a, au = rowmax_unit(i, u)
                        blk, hg = au // 2, au % 2
                        lo, w, _ = window(blk)
                        if au == 0:
                            pe.wait_ge(stack_in[a.buf], STACK_DMAS * (a.round + 1))
                        for half in range(2):
                            r = 2 * UNITS * a.n + 2 * au + half
                            after(pe, rowmax, r - 1)
                            for j in range(2):
                                h = 4 * hg + 2 * half + j
                                o = s1[half][:, 256 * j:256 * j + w]
                                mm(o, qstack[a.buf][0:STACK, h, P * blk:P * blk + P],
                                   kstack[a.buf][0:STACK, h, lo:lo + w], start=True, stop=False)
                                last = mm(o, identb, mask(blk), start=False, stop=True)
                            last.then_inc(s1_ready, 1)
                    if has(i, -1):
                        blk, hg = u // 2, u % 2
                        lo, w, _ = window(blk)
                        if u == 0 and isinstance(b.n, int) and b.n < 3:
                            pe.wait_ge(ones_set, b.n + 1)
                        if u == 0:
                            pe.wait_ge(max_in[b.buf], 16 * (b.round + 1))
                        for half in range(2):
                            r = 2 * UNITS * b.n + 2 * u + half
                            after(pe, exp_ready, r - 1)
                            for j in range(2):
                                h = 4 * hg + 2 * half + j
                                o = s2[half][:, 256 * j:256 * j + w]
                                last = mm(o, kstack[b.buf][0:STACK + 3, h, P * blk:P * blk + P],
                                          qstack[b.buf][0:STACK + 3, h, lo:lo + w], start=True, stop=True)
                            last.then_inc(s2_ready, 1)
                    if u < 2 and has(i, -2):
                        attend_values(c, UNITS - 2 + u)
                    if u >= 2 and has(i, -1):
                        attend_values(b, u - 2)
                    between(i, u)
                if isinstance(i.n, int) and i.n == SEQS:
                    turn_rows(Turn(0, 0, 2), True)
                if isinstance(i.n, int) and i.n == SEQS + 1:
                    pe.wait_ge(shared_in, 32)
                    gate_up(Turn(0, 0, 2), True)
                    turn_rows(Turn(1, 0, 2), True)

            def between(i, u):
                a, b, c, d, e = i, i.plus(-1), i.plus(-2), i.plus(1), i.plus(-3)
                if u == 0 and has(i, 1):
                    pe.wait_ge(xn1_ready, d.n + 1)
                    after(pe, k_res, d.n)
                    after(pe, m_rows, d.n - 1)
                    after(pe, l_ready, d.n - 4)
                    mm(misc[1][:], wsm[:, W_Q:W_Q + P], xn1, start=True, stop=True).then_inc(q_mm, 1)
                if u == 1 and has(i, 1):
                    pe.wait_ge(q_res, d.n + 1)
                    mm(misc[1][:], wsm[:, W_K:W_K + P], xn1, start=True, stop=True).then_inc(k_mm, 1)
                if u == 2 and has(i, 1):
                    after(pe, v_ready, d.n)
                    after(pe, x2_ready, d.n - 3)
                    if isinstance(d.n, int) and d.n == 0:
                        pe.wait_ge(beff_ready, 1)
                    for k in range(QB):
                        last = mm(misc[0][:, P * k:P * k + P], xn1[:, P * k:P * k + P], wsm[:, W_V:W_V + P],
                                  start=True, stop=True)
                    last.then_inc(v_mm, 1)
                if u == 3 and has(i, -3):
                    pe.wait_ge(xn2_ready, e.n + 1)
                    if has(i, 1):
                        pe.wait_ge(k_res, d.n + 1)
                    after(pe, l_ready, e.n)
                    for k in range(4):
                        last = nc.tensor.transpose(misc[1][:, P * k:P * k + P], xn2[:, P * k:P * k + P], ident)
                    last.then_inc(xt_mm, 1)
                if u == 4 and has(i, -3):
                    pe.wait_ge(xt_ready, e.n + 1)
                    pe.wait_ge(x2_ready, e.n + 1)
                    if has(i, 1):
                        pe.wait_ge(v_ready, d.n + 1)
                    for k in range(4):
                        last = mm(misc[0][0:EXPERTS, 0:P], wsm[:, W_R + 16 * k:W_R + 16 * k + 16], xn2T[:, k, :],
                                  start=(k == 0), stop=(k == 3))
                    last.then_inc(router_mm, 1)
                if u == 5 and has(i, -2):
                    pe.wait_ge(recips_in[c.buf], 48 * (c.round + 1))
                    if has(i, -3):
                        pe.wait_ge(lt_ready, e.n + 1)
                    elif has(i, 1):
                        pe.wait_ge(v_ready, d.n + 1)
                        pe.wait_ge(k_res, d.n + 1)
                    for g in range(2):
                        mm(misc[g][:], cb[0:3 * HEADS, B_SEL + P * g:B_SEL + P * g + P], recip_rows[0:3 * HEADS, :],
                           start=True, stop=True).then_inc(den_mm, 1)
                if u == 6 and has(i, -2):
                    pe.wait_ge(o_ready, 2 * c.n + 2)
                    for g in range(2):
                        last = mm(misc[0][:], wsm[:, W_O + P * g:W_O + P * g + P], onorm[g],
                                  start=(g == 0), stop=(g == 1))
                    last.then_inc(proj_mm, 1)
                if u == 6 and has(i, 0):
                    if has(i, -2):
                        pe.wait_ge(o_ready, 2 * c.n + 2)
                    elif has(i, 1):
                        pe.wait_ge(k_res, d.n + 1)
                    pe.wait_ge(m_step, 4 * (a.n + 1))
                    nc.tensor.transpose(misc[1][:].bitcast(BF16)[0:96, 0:P],
                                        mparts.rearrange("p a b -> p (a b)"), identb).then_inc(m_mm, 1)
                if u == 7 and has(i, -3):
                    if has(i, 0):
                        pe.wait_ge(m_rows, a.n + 1)
                    stand(pe, PE, lt_ready, e.n + 1)
                    nc.tensor.transpose(misc[1][:, 0:EXPERTS], logitT[0:EXPERTS, :],
                                        cf[0:EXPERTS, C_ID:C_ID + EXPERTS]).then_inc(l_mm, 1)
                if u == 7 and has(i, -2):
                    pe.wait_ge(gated_ready, c.n + 1)
                    mm(misc[0][:], wsm[:, W_CT:W_CT + P], gated, start=True, stop=True).then_inc(ct_mm, 1)

            def attend_values(b, u):
                blk, hg = u // 2, u % 2
                lo, w, _ = window(blk)
                pe.wait_ge(cut_ready, UNITS * b.n + u + 1)
                if u == 0:
                    pe.wait_ge(v_ready, b.n + 1)
                if blk == 0:
                    after(pe, o_copied[hg], b.n)
                for j in range(4):
                    last = mm(oacc[hg][32 * j:32 * j + 32, lo:lo + w], vaug[b.buf][:, blk, 4 * hg + j, :],
                              probs[u % 4][:, j, 0:w], start=(blk == 0), stop=(blk == QB - 1),
                              skip_group_check=True)
                last.then_inc(pv_done, 1)

            tb, gb, ab, yb, rb = bank[0:2], bank[2:4], bank[4], bank[5:7], bank[7]

            def turn_rows(k, shared):
                if shared:
                    pe.wait_ge(rows_in[k.buf], 16 * (k.round + 1))
                else:
                    pe.wait_ge(gathered[k.buf], 16 * (k.round - SEQS // 2 + 1))
                after(pe, t_ready, k.n - 1)
                for c in range(4):
                    last = nc.tensor.transpose(tb[k.buf][:, P * c:P * c + P], rows[:, k.buf, P * c:P * c + P], ident)
                last.then_inc(t_mm, 1)

            def gate_up(k, shared, between=None):
                pe.wait_ge(t_ready, k.n + 1)
                after(pe, act_ready, k.n - 1)
                o = gb[k.buf][:]
                if shared:
                    for c in range(4):
                        last = mm(o, rowsT[:, k.buf, c, :], swgu[:, c, :], start=(c == 0), stop=(c == 3))
                        if c == 2 and between:
                            turn_act(between)
                else:
                    pe.wait_ge(gu_high, 2 * (k.n - SEQS + 1))
                    for i, (r, w) in enumerate(((0, 0), (0, 1), (1, 0))):
                        if i == 1:
                            pe.wait_ge(gu_low, 2 * (k.n - SEQS + 1))
                        if i == 2:
                            pe.wait_ge(rows_low, k.n - SEQS + 1)
                        for c in range(4):
                            last = mm(o, rows_parts[:, r, c, :], gu_parts[:, k.buf, w, 512 * c:512 * c + 512],
                                      start=(i == c == 0), stop=(i == 2 and c == 3))
                            if i == 2 and c == 0 and between:
                                turn_act(between)
                last.then_inc(gu_mm, 1)

            def turn_act(k):
                pe.wait_ge(act_ready, k.n + 1)
                after(pe, at_ready, k.n - 1)
                for c in range(2):
                    o = INNER * k.buf + P * c
                    last = nc.tensor.transpose(ab[:, o:o + P], act_in[:, k.buf, P * c:P * c + P], ident)
                last.then_inc(at_mm, 1)

            def down(k, shared):
                pe.wait_ge(at_ready, k.n + 1)
                after(pe, y_ready, k.n - 1)
                o = yb[k.buf][:]
                if shared:
                    for c in range(2):
                        last = mm(o, actT[:, k.buf, c, :], swd[:, c, :], start=(c == 0), stop=(c == 1))
                else:
                    pe.wait_ge(wd_split, k.n - SEQS + 1)
                    for i, (a, w) in enumerate(((0, 0), (0, 1), (1, 0))):
                        if i == 1:
                            pe.wait_ge(wd_low0, k.n - SEQS + 1)
                            pe.wait_ge(wd_low1, k.n - SEQS + 1)
                        if i == 2:
                            pe.wait_ge(act_low, k.n - SEQS + 1)
                        for c in range(2):
                            last = mm(o, act_parts[:, a, c, :], (wd_low if w else wd_high)[:, k.buf, c, :],
                                      start=(i == c == 0), stop=(i == 2 and c == 1))
                last.then_inc(dn_mm, 1)

            def ranks():
                pe.wait_ge(member_ready, 1)
                tri, ones = cb[:, B_TRI:B_TRI + P], cb[:, B_ONES:B_ONES + P]
                m = member[:].rearrange("p n e -> p (n e)")
                mm(rb[:, 0:256], tri, m, start=True, stop=False)
                for t in range(SEQS - 1):
                    later = SEQS - 1 - t
                    last = mm(rb[:, 16 * (t + 1):256].rearrange("p (n e) -> p n e", e=EXPERTS), ones,
                              member[:, t:t + 1, :].to_broadcast([P, later, EXPERTS]),
                              start=False, stop=(later == 1))
                last.then_inc(rank_mm, 1)

            def counts():
                ones = cb[:, B_ONES:B_ONES + P]
                pe.wait_ge(ranks_read, 1)
                for t in range(SEQS):
                    last = mm(rb[:, 0:EXPERTS], ones, member[:, t, :], start=(t == 0), stop=(t == SEQS - 1))
                last.then_inc(rank_mm, 1)
                pe.wait_ge(counts_read, 1)
                mm(rb[:, 0:TABLE], ones, cb[:, B_ZERO:B_ZERO + TABLE], start=True,
                   stop=False).then_inc(table_mm, 1)

            def chunk(trip):
                pe.wait_ge(hot_ready, trip + 1)
                for q in range(8):
                    last = mm(rb[:, 0:TABLE], hot_row[:, q, :], hot_col[:, q, :, :].rearrange("p g b -> p (g b)"),
                              start=False, stop=False)
                last.then_inc(table_mm, 1)

            def tables():
                mm(rb[:, 0:TABLE], cb[:, B_ONES:B_ONES + P], cb[:, B_ZERO:B_ZERO + TABLE], start=False,
                   stop=True).then_inc(table_mm, 1)

            attention_steps(pe, step)
            pe.wait_ge(l_ready, SEQS)

            def pe_step(k, shared):
                prev = k.plus(-1)
                prev_shared = shared or (k.first == SEQS and isinstance(k.trip, int))
                gate_up(k, shared, prev)
                if not (isinstance(k.n, int) and k.n == SEQS + BLOCKS - 1):
                    turn_rows(k.plus(1), shared and not (isinstance(k.n, int) and k.n == SEQS - 1))
                down(prev, prev_shared)

            pe_step(Turn(1, 0, 2), True)
            for k in range(2, 5):
                pe_step(Turn(k, 0, 2), True)
            ranks()
            pe_step(Turn(5, 0, 2), True)
            counts()
            for k in range(6, 8):
                pe_step(Turn(k, 0, 2), True)
            with pe.Fori(0, 2) as trip:
                for k in range(2):
                    pe_step(Turn(8 + k, trip, 2), True)
                    chunk(Turn(k, trip, 2).n)
            tables()
            for k in range(12, 14):
                pe_step(Turn(k, 0, 2), True)
            pe_step(Turn(14, 0, 2), True)
            pe_step(Turn(15, 0, 2), True)
            pe_step(Turn(16, 0, 2), False)
            pe_step(Turn(17, 0, 2), False)
            with pe.Fori(0, (BLOCKS - 3) // 2) as trip:
                for k in range(2):
                    pe_step(Turn(SEQS + 2 + k, trip, 2), False)
            pe_step(Turn(SEQS + BLOCKS - 1, 0, 2), False)
            turn_act(Turn(SEQS + BLOCKS - 1, 0, 2))
            down(Turn(SEQS + BLOCKS - 1, 0, 2), False)

        @block.scalar
        def _(act):
            act.wait_ge(weights_in, 16)
            act.wait_ge(beff_mm, 1)
            nc.scalar.activation(beff, misc[0][:, 0:1], ACT.Identity, bias=wsm[:, BO:BO + 1]).then_inc(beff_ready, 1)
            act.wait_ge(beff_ready, 1)

            def copy_out(c, hg):
                act.wait_ge(pv_done, UNITS * c.n + UNITS - 1 + hg)
                after(act, o_ready, 2 * c.n)
                nc.scalar.copy(ounorm[hg], oacc[hg][:]).then_inc(o_copied[hg], 1)

            def step(i):
                b, c, d, e = i.plus(-1), i.plus(-2), i.plus(1), i.plus(-3)
                for u in range(UNITS):
                    if has(i, -1):
                        blk = u // 2
                        _, w, _ = window(blk)
                        after(act, pv_done, UNITS * b.n + u - 3)
                        for half in range(2):
                            act.wait_ge(s2_ready, 2 * UNITS * b.n + 2 * u + half + 1)
                            nc.scalar.activation(
                                probs[u % 4][:, 2 * half:2 * half + 2, 0:w],
                                s2[half][:].rearrange("p (j c) -> p j c", j=2)[:, :, 0:w],
                                ACT.Exp, scale=D ** -0.5).then_inc(exp_ready, 1)
                    if u < 2 and has(i, -2):
                        copy_out(c, u)
                    if u == 1 and isinstance(i.n, int) and i.n == SEQS:
                        for k in range(2):
                            act.wait_ge(xn_stored[k], 16)
                            load_rows(Turn(k, 0, 2))
                    if u == 1 and isinstance(i.n, int) and i.n == SEQS + 1:
                        rows_copy(Turn(0, 0, 2))
                    if u == 0 and has(i, 1):
                        act.wait_ge(q_mm, d.n + 1)
                        first_part_free(d)
                        nc.scalar.activation(qparts[:, 0, :], misc[1][:], ACT.Identity,
                                             bias=wsm[:, BQ:BQ + 1]).then_inc(q_p1, 1)
                    if u == 1 and has(i, 1):
                        act.wait_ge(q_res, d.n + 1)
                        nc.scalar.copy(qparts[:, 1, :], qres).then_inc(q_p2, 1)
                        act.wait_ge(k_mm, d.n + 1)
                        nc.scalar.activation(kparts[:, 0, :], misc[1][:], ACT.Identity,
                                             bias=wsm[:, BK:BK + 1]).then_inc(k_p1, 1)
                    if u == 2 and has(i, 1):
                        act.wait_ge(k_res, d.n + 1)
                        nc.scalar.copy(kparts[:, 1, :], kres).then_inc(k_p2, 1)
                        act.wait_ge(v_mm, d.n + 1)
                        nc.scalar.copy(vaug[d.buf][:, :, :, 0:D].rearrange("p b h d -> p (b h) d"),
                                       misc[0][:].rearrange("p (g d) -> p g d", d=D)).then_inc(v_ready, 1)
                    if u == 3 and has(i, -3):
                        act.wait_ge(xt_mm, e.n + 1)
                        nc.scalar.copy(xn2T.rearrange("p a b -> p (a b)"), misc[1][:]).then_inc(xt_ready, 1)
                    if u == 4 and has(i, -3):
                        act.wait_ge(router_mm, e.n + 1)
                        nc.scalar.activation(logitT[0:EXPERTS, :], misc[0][0:EXPERTS, 0:P], ACT.Identity,
                                             bias=wsm[0:EXPERTS, BR:BR + 1]).then_inc(lt_ready, 1)
                        if isinstance(i.n, int) and i.n == SEQS + 2:
                            rows_copy(Turn(1, 0, 2))
                    if u == 6 and has(i, -2):
                        act.wait_ge(proj_mm, c.n + 1)
                        after(act, gated_ready, c.n)
                        nc.scalar.activation(relu_o, misc[0][:], ACT.Relu, bias=beff).then_inc(relu_ready, 1)

            def first_part_free(d):
                prev = d.plus(-1)
                if not isinstance(d.n, int) or d.n >= 1:
                    act.wait_ge(stack_in[prev.buf], STACK_DMAS * (prev.round + 1))

            tb, gb, ab, yb = bank[0:2], bank[2:4], bank[4], bank[5:7]
            act.wait_ge(setup, 5)
            act.dma_start(out_rows[TOKENS:TOKENS + P, :], y_out[:, 1, :]).then_inc(spare_stored, 16)
            def load_rows(k):
                after(act, t_mm, k.n - 1)
                act.dma_start(rows[:, k.buf, :], xn_rows[bass.ds(k.n * P, P), :]).then_inc(rows_in[k.buf], 16)

            def rows_copy(k, shared=True):
                act.wait_ge(t_mm, k.n + 1)
                after(act, gu_mm, k.n - 1 if shared else k.n)
                to = rowsT[:, k.buf, :, :] if shared else rows_parts[:, 0, :, :]
                nc.scalar.copy(to.rearrange("p a b -> p (a b)"), tb[k.buf][:]).then_inc(t_ready, 1)

            def act_copy(k, shared=True):
                act.wait_ge(at_mm, k.n + 1)
                after(act, dn_mm, k.n - 1 if shared else k.n)
                to = actT[:, k.buf, :, :] if shared else act_parts[:, 0, :, :]
                nc.scalar.copy(to.rearrange("p a b -> p (a b)"),
                               ab[:, INNER * k.buf:INNER * k.buf + INNER]).then_inc(at_ready, 1)

            def high_down(k):
                act.wait_ge(wd_in[k.buf], 16 * (k.round - SEQS // 2 + 1))
                nc.scalar.copy(wd_high[:, k.buf, :, :].rearrange("p c n -> p (c n)"),
                               wd[:, k.buf, :, :].rearrange("p c n -> p (c n)")).then_inc(wd_split, 1)

            def high_gate_up(k):
                e = act.value_load(expert_i[0:1, bass.ds(k.n - SEQS, 1)], min_val=0, max_val=EXPERTS - 1)
                for half in range(2):
                    nc.scalar.copy(gu_parts[:, k.buf, 0, 1024 * half:1024 * half + 1024],
                                   wgu[:, bass.ds(e * 2048 + 1024 * half, 1024)]).then_inc(gu_high, 1)

            def result(k):
                stand(act, SCALAR, dn_mm, k.n + 1)
                if k.first in (SEQS, SEQS + 1) and isinstance(k.trip, int):
                    act.wait_ge(y_stored[k.buf], 16 * k.round)
                else:
                    stand(act, SCALAR, added[k.buf], 16 * (k.round - SEQS // 2))
                nc.scalar.activation(y_out[:, k.buf, :], yb[k.buf][:], ACT.Copy,
                                     scale=gate_of[:, bass.ds(k.n - SEQS, 1)]).then_inc(y_ready, 1)

            def silu(k):
                act.wait_ge(gu_mm, k.n + 1)
                after(act, at_mm, k.n - 1)
                nc.scalar.activation(act_in[:, k.buf, :], gb[k.buf][:, 0:INNER], ACT.Silu).then_inc(silu_ready, 1)

            def store_shared(k):
                act.wait_ge(y_ready, k.n + 1)
                act.dma_start(out_rows[bass.ds(k.n * P, P), :], y_out[:, k.buf, :]).then_inc(y_stored[k.buf], 16)

            attention_steps(act, step)
            act.wait_ge(shifted, 1)
            nc.scalar.activation(logits[:], logits[:], ACT.Exp).then_inc(exp_done, 1)

            def step_experts(k, load, store):
                act_copy(k.plus(-1))
                rows_copy(k.plus(1))
                if load:
                    load_rows(k.plus(2))
                silu(k)
                if store:
                    store_shared(k.plus(-1))

            for b in range(3):
                act.wait_ge(xn_stored[b], 16 * len(range(b, SEQS, 3)))
            load_rows(Turn(2, 0, 2))
            silu(Turn(0, 0, 2))
            step_experts(Turn(1, 0, 2), True, True)
            for k in range(2, 4):
                step_experts(Turn(k, 0, 2), True, True)
            with act.Fori(0, 5) as trip:
                for k in range(2):
                    step_experts(Turn(4 + k, trip, 2), True, True)
            step_experts(Turn(14, 0, 2), False, True)

            def step_routed(k, last=False):
                silu(k)
                if not last:
                    rows_copy(k.plus(1), False)
                high_down(k)
                if k.first == SEQS:
                    store_shared(k.plus(-1))
                if not (isinstance(k.n, int) and k.n + 2 >= SEQS + BLOCKS):
                    high_gate_up(k.plus(2))
                if k.first != SEQS:
                    result(k.plus(-1))
                act_copy(k, False)

            act.wait_ge(tables_ready, 1)
            act.wait_ge(experts_in, 16 * EXPERTS)
            high_gate_up(Turn(SEQS, 0, 2))
            act_copy(Turn(14, 0, 2))
            rows_copy(Turn(SEQS, 0, 2), False)
            silu(Turn(15, 0, 2))
            store_shared(Turn(14, 0, 2))
            high_gate_up(Turn(SEQS + 1, 0, 2))
            act_copy(Turn(15, 0, 2))
            step_routed(Turn(SEQS, 0, 2))
            step_routed(Turn(SEQS + 1, 0, 2))
            step_routed(Turn(SEQS + 2, 0, 2))
            with act.Fori(0, (BLOCKS - 5) // 2) as trip:
                for k in range(2):
                    step_routed(Turn(SEQS + 3 + k, trip, 2))
            step_routed(Turn(SEQS + BLOCKS - 2, 0, 2))
            step_routed(Turn(SEQS + BLOCKS - 1, 0, 2), True)
            result(Turn(SEQS + BLOCKS - 1, 0, 2))

        @block.vector
        def _(dve):
            v = nc.vector
            for b in range(3):
                v.memset(vaug[b][:, :, :, D:2 * D], 1.0).then_inc(setup, 1)
            v.memset(y_out[:, 1, :], 0.0).then_inc(setup, 1)
            dve.wait_ge(consts_in, 32)
            v.tensor_copy(cb[:], cb_f).then_inc(setup, 1)
            dve.wait_ge(weights_in, 16)

            def normalise(which, n, src, dst, rstd_sem, ready):
                dve.wait_ge(rstd_sem, n + 1)
                v.tensor_scalar(dst, src, moments[:, which, 0:1], rstd[:, which:which + 1],
                                ALU.subtract, ALU.mult).then_inc(ready, 1)

            def moments_of(which, n, src, st, mom, before):
                stand(dve, DVE, before, n)
                v.bn_stats(stats[:, which, :], src).then_inc(st, 1)
                stand(dve, DVE, st, n + 1)
                v.bn_aggr(moments[:, which, :], stats[:, which, :]).then_inc(mom, 1)

            def seq(n):
                return X[:, bass.ds(n, 1), :].rearrange("p a t -> p (a t)")

            def maximum(s, su, half):
                blk, hg = su // 2, su % 2
                _, w, _ = window(blk)
                h = 4 * hg + 2 * half
                dve.wait_ge(s1_ready, 2 * UNITS * s.n + 2 * su + half + 1)
                v.tensor_reduce(negmax[:, h:h + 2, blk:blk + 1],
                                s1[half][:].rearrange("p (j c) -> p j c", j=2)[:, :, 0:w],
                                AX.X, ALU.max, negate=True).then_inc(rowmax, 1)

            def reciprocals(c):
                dve.wait_ge(dens_in[c.buf], 32 * (c.round + 1))
                if not isinstance(c.n, int) or c.n >= 1:
                    prev = c.plus(-1)
                    stand(dve, DVE, recips_in[prev.buf], 48 * (prev.round + 1))
                v.reciprocal(recips, dens).then_inc(recip_step, 1)

            def step(i):
                a, c, d, e, f = i, i.plus(-2), i.plus(1), i.plus(-3), i.plus(2)
                for u in range(UNITS):
                    if u == 0 and has(i, -3):
                        dve.wait_ge(ct_mm, e.n + 1)
                        v.scalar_tensor_tensor(seq(e.n), misc[0][:], wsm[:, BCT:BCT + 1], seq(e.n),
                                               ALU.add, ALU.add).then_inc(x2_ready, 1)
                    if u == UNITS - 2 and has(i, 0):
                        dve.wait_ge(m_step, 4 * a.n + 2)
                    if u == 7 and has(i, -2):
                        dve.wait_ge(relu_ready, c.n + 1)
                        dve.wait_ge(enc_in[c.buf], 16 * (c.round + 1))
                        v.tensor_tensor(gated, relu_o, enc[c.buf], ALU.mult).then_inc(gated_ready, 1)
                    if rowmax_unit(i, u):
                        maximum(*rowmax_unit(i, u), 0)
                    if rowmax_unit(i, u):
                        maximum(*rowmax_unit(i, u), 1)
                    if u == 0 and has(i, 1):
                        dve.wait_ge(q_p1, d.n + 1)
                        after(dve, q_p3, d.n)
                        v.scalar_tensor_tensor(qres, misc[1][:], wsm[:, BQ:BQ + 1], qparts[:, 0, :],
                                               ALU.add, ALU.subtract).then_inc(q_res, 1)
                    if u == 1 and has(i, -3):
                        stand(dve, DVE, x2_ready, e.n + 1)
                        moments_of(1, e.n, seq(e.n), stats2, mom2, xn2_ready)
                    if u == 2 and has(i, -2):
                        reciprocals(c)
                    if u == 2 and has(i, 1):
                        dve.wait_ge(k_p1, d.n + 1)
                        after(dve, k_p3, d.n)
                        v.scalar_tensor_tensor(kres, misc[1][:], wsm[:, BK:BK + 1], kparts[:, 0, :],
                                               ALU.add, ALU.subtract).then_inc(k_res, 1)
                    if u == 2 and has(i, -3):
                        if not isinstance(e.n, int) or e.n >= 1:
                            prev = e.plus(-1)
                            dve.wait_ge(xn_stored[prev.buf], 16 * (prev.round + 1))
                            dve.wait_ge(xt_mm, e.n)
                        normalise(1, e.n, seq(e.n), xn2, rstd2, xn2_ready)
                    if u == 3 and has(i, 2):
                        if isinstance(f.n, int) and f.n in (0, 1, 4):
                            dve.wait_ge(x_in[{0: 0, 1: 1, 4: 2}[f.n]], 16)
                        moments_of(0, f.n, seq(f.n), stats1, mom1, xn1_ready)
                    if u == 5 and has(i, -2):
                        for g in range(2):
                            dve.wait_ge(den_mm, 2 * c.n + g + 1)
                            v.tensor_tensor(onorm[g], ounorm[g], misc[g][:], ALU.mult).then_inc(o_ready, 1)
                    if u == 5 and has(i, 2):
                        if has(i, 1):
                            dve.wait_ge(v_mm, d.n + 1)
                        normalise(0, f.n, seq(f.n), xn1, rstd1, xn1_ready)
                    if u == 6 and has(i, 0):
                        dve.wait_ge(m_mm, a.n + 1)
                        if not isinstance(a.n, int) or a.n >= 1:
                            prev = a.plus(-1)
                            dve.wait_ge(max_in[prev.buf], 16 * (prev.round + 1))
                        v.tensor_copy(mrows[0:96, :], misc[1][:].bitcast(BF16)[0:96, 0:P]).then_inc(m_rows, 1)
                if has(i, -3):
                    dve.wait_ge(l_mm, e.n + 1)
                    v.tensor_copy(logits[:, bass.ds(e.n, 1), :].rearrange("p a t -> p (a t)"),
                                  misc[1][:, 0:EXPERTS]).then_inc(l_ready, 1)

            attention_steps(dve, step)

            tb, gb, ab, yb, rb = bank[0:2], bank[2:4], bank[4], bank[5:7], bank[7]
            linked = [0]

            def link(ins):
                linked[0] += 1
                ins.then_inc(route, 1)
                dve.wait_ge(route, linked[0])

            def each(ap):
                return ap.unsqueeze(2).to_broadcast([P, SEQS, EXPERTS])

            def flat(ap):
                return ap.rearrange("p a b -> p (a b)")

            def routing_choice():
                rev = cf[:, C_REV:C_REV + EXPERTS].unsqueeze(1).to_broadcast([P, SEQS, EXPERTS])
                dve.wait_ge(l_ready, SEQS)
                link(v.tensor_reduce(pick[:, 0, :], logits[:], AX.X, ALU.max))
                v.tensor_tensor(logits[:], logits[:], each(pick[:, 0, :]), ALU.subtract).then_inc(shifted, 1)
                dve.wait_ge(exp_done, 1)
                link(v.tensor_reduce(pick[:, 0, :], logits[:], AX.X, ALU.add))
                link(v.reciprocal(pick[:, 1, :], pick[:, 0, :]))
                link(v.tensor_tensor(logits[:], logits[:], each(pick[:, 1, :]), ALU.mult))
                for k in range(2):
                    link(v.tensor_reduce(top[:, k, :], logits[:], AX.X, ALU.max))
                    link(v.tensor_tensor(tmp[:], logits[:], each(top[:, k, :]), ALU.is_equal))
                    link(v.tensor_tensor(tmp[:], tmp[:], rev, ALU.mult))
                    link(v.tensor_reduce(pick[:, k, :], tmp[:], AX.X, ALU.max))
                    link(v.tensor_tensor(hot[:, k, :, :], rev, each(pick[:, k, :]), ALU.is_equal))
                    if k == 0:
                        activate(Turn(0, 0, 2))
                    if k == 0:
                        link(v.scalar_tensor_tensor(flat(logits[:]), flat(hot[:, 0, :, :]), -2.0,
                                                    flat(logits[:]), ALU.mult, ALU.add))
                v.tensor_tensor(member[:], hot[:, 0, :, :], hot[:, 1, :, :], ALU.add).then_inc(member_ready, 1)

            def copy_ranks():
                dve.wait_ge(rank_mm, 1)
                v.tensor_copy(flat(tmp[:]), rb[:, 0:256]).then_inc(ranks_read, 1)

            def copy_counts():
                dve.wait_ge(ranks_read, 1)
                dve.wait_ge(rank_mm, 2)
                v.tensor_copy(count[:, 0, :], rb[:, 0:EXPERTS]).then_inc(counts_read, 1)

            def routing_gates():
                link(v.tensor_tensor(pick[:, 0, :], top[:, 0, :], top[:, 1, :], ALU.add))
                link(v.tensor_scalar(pick[:, 0, :], pick[:, 0, :], 1e-9, None, ALU.add))
                link(v.reciprocal(pick[:, 1, :], pick[:, 0, :]))
                link(v.tensor_tensor(top[:], top[:], pick[:, 1:2, :].to_broadcast([P, 2, SEQS]), ALU.mult))
                gates = flat(top[:])
                link(v.tensor_copy(gate_parts[:, 0, :], gates))
                link(v.tensor_tensor(gate_res[:], gates, gate_parts[:, 0, :], ALU.subtract))
                link(v.tensor_copy(gate_parts[:, 1, :], gate_res[:]))
                link(v.tensor_tensor(gate_parts[:, 2, :], gate_res[:], gate_parts[:, 1, :], ALU.subtract))
                v.tensor_copy(vals[:, :, 2:5], gate_parts[:].rearrange("p g q -> p q g"))
                v.tensor_copy(vals[:, :, 0:1], cf[:, C_TILE:C_TILE + 32].unsqueeze(2))
                link(v.tensor_copy(vals[:, :, 1:2],
                                   cf[:, C_ROW1:C_ROW1 + 1].unsqueeze(1).to_broadcast([P, 2 * SEQS, 1])))

            def routing_slots():
                dve.wait_ge(counts_read, 1)
                link(v.tensor_scalar(count_i[:], count[:, 0, :], 127.0, None, ALU.add))
                link(v.tensor_scalar(count_i[:], count_i[:], 7, None, ALU.arith_shift_right))
                link(v.tensor_copy(count[:, 1, :], count_i[:]))
                link(v.tensor_tensor_scan(count[:, 2, :], cf[:, C_ONE:C_ONE + EXPERTS], count[:, 1, :], 0.0,
                                          ALU.mult, ALU.add))
                link(v.tensor_tensor(count[:, 3, :], count[:, 2, :], count[:, 1, :], ALU.subtract))
                link(v.tensor_scalar(count[:, 3, :], count[:, 3, :], float(P), None, ALU.mult))
                link(v.tensor_tensor(tmp[:], tmp[:],
                                     count[:, 3:4, :].to_broadcast([P, SEQS, EXPERTS]), ALU.add))
                for k in range(2):
                    link(v.tensor_tensor(logits[:], hot[:, k, :, :], tmp[:], ALU.mult))
                    link(v.tensor_reduce(small[:, 0, SEQS * k:SEQS * (k + 1)], logits[:], AX.X, ALU.add))
                link(v.tensor_copy(small_i[:, 0, :], small[:, 0, :]))
                link(v.tensor_scalar(small_i[:, 1, :], small_i[:, 0, :], 7, None, ALU.arith_shift_right))
                link(v.tensor_scalar(small_i[:, 0, :], small_i[:, 0, :], P - 1, None, ALU.bitwise_and))
                v.tensor_copy(small[:, 1, :], small_i[:, 1, :])
                link(v.tensor_copy(small[:, 2, :], small_i[:, 0, :]))

            def routing_blocks():
                link(v.tensor_tensor(before, cf[:, C_IOTA:C_IOTA + BLOCKS].unsqueeze(2)
                                     .to_broadcast([P, BLOCKS, EXPERTS]),
                                     count[:, 2:3, :].to_broadcast([P, BLOCKS, EXPERTS]), ALU.is_ge))
                link(v.tensor_reduce(expert_of[:], before, AX.X, ALU.add))
                link(v.tensor_scalar(expert_i[:], expert_of[:], float(EXPERTS - 1), None, ALU.min))

            def routing_chunk(trip):
                dve.wait_ge(table_mm, trip + 1)
                rows_of = small[:, 2, :][:, bass.ds(trip * 8, 8)]
                blocks_of = small[:, 1, :][:, bass.ds(trip * 8, 8)]
                v.tensor_tensor(hot_row, cf[:, C_IOTA:C_IOTA + P].unsqueeze(1).to_broadcast([P, 8, P]),
                                rows_of.unsqueeze(2).to_broadcast([P, 8, P]), ALU.is_equal)
                v.tensor_tensor(hot_block, cf[:, C_IOTA:C_IOTA + BLOCKS].unsqueeze(1).to_broadcast([P, 8, BLOCKS]),
                                blocks_of.unsqueeze(2).to_broadcast([P, 8, BLOCKS]),
                                ALU.is_equal).then_inc(hot_blocks, 1)
                dve.wait_ge(hot_blocks, trip + 1)
                v.tensor_tensor(hot_col, hot_block.unsqueeze(2).to_broadcast([P, 8, 5, BLOCKS]),
                                vals[:, bass.ds(trip * 8, 8), :].unsqueeze(3).to_broadcast([P, 8, 5, BLOCKS]),
                                ALU.mult).then_inc(hot_ready, 1)

            def routing_tables():
                dve.wait_ge(table_mm, 6)
                link(v.tensor_copy(table, rb[:, 0:TABLE]))
                part = lambda g: table[:, g * BLOCKS:(g + 1) * BLOCKS]
                link(v.scalar_tensor_tensor(slot[:, 0, :], part(0), float(P), part(1), ALU.mult, ALU.add))
                link(v.tensor_scalar(slot[:, 1, :], slot[:, 0, :], 0.0, cf[:, C_SPARE:C_SPARE + 1],
                                     ALU.is_equal, ALU.mult))
                v.tensor_scalar(gather_i[:], slot[:, 0, :], -1.0, 0.0, ALU.add, ALU.max)
                v.scalar_tensor_tensor(scatter_i[:], slot[:, 0, :], -1.0, slot[:, 1, :], ALU.add, ALU.add)
                link(v.tensor_tensor(slot[:, 2, :], part(2), part(3), ALU.add))
                v.tensor_tensor(gate_of[:], slot[:, 2, :], part(4), ALU.add).then_inc(tables_ready, 1)

            def activate(k):
                dve.wait_ge(silu_ready, k.n + 1)
                v.tensor_tensor(act_in[:, k.buf, :], act_in[:, k.buf, :], gb[k.buf][:, INNER:2 * INNER],
                                ALU.mult).then_inc(act_ready, 1)

            def result(k):
                dve.wait_ge(dn_mm, k.n + 1)
                after(dve, y_stored[k.buf], 16 * k.round)
                v.tensor_tensor(y_out[:, k.buf, :], yb[k.buf][:], seq(k.n), ALU.add).then_inc(y_ready, 1)

            def low_rows(k):
                dve.wait_ge(t_ready, k.n + 1)
                dve.wait_ge(gu_mm, k.n)
                v.tensor_tensor(rows_parts[:, 1, :, :].rearrange("p a b -> p (a b)"), tb[k.buf][:],
                                rows_parts[:, 0, :, :].rearrange("p a b -> p (a b)"),
                                ALU.subtract).then_inc(rows_low, 1)

            def low_act(k):
                dve.wait_ge(at_ready, k.n + 1)
                dve.wait_ge(dn_mm, k.n)
                v.tensor_tensor(act_parts[:, 1, :, :].rearrange("p a b -> p (a b)"),
                                ab[:, INNER * k.buf:INNER * k.buf + INNER],
                                act_parts[:, 0, :, :].rearrange("p a b -> p (a b)"),
                                ALU.subtract).then_inc(act_low, 1)

            def low_down(k):
                dve.wait_ge(wd_split, k.n - SEQS + 1)
                v.tensor_tensor(wd_low[:, k.buf, 0, :], wd[:, k.buf, 0, :], wd_high[:, k.buf, 0, :],
                                ALU.subtract).then_inc(wd_low0, 1)

            def low_gate_up(k, halves=(0, 1)):
                e = dve.value_load(expert_i[0:1, bass.ds(k.n - SEQS, 1)], min_val=0, max_val=EXPERTS - 1)
                for half in halves:
                    dve.wait_ge(gu_high, 2 * (k.n - SEQS) + half + 1)
                    cols = slice(1024 * half, 1024 * half + 1024)
                    v.tensor_tensor(gu_parts[:, k.buf, 1, cols], wgu[:, bass.ds(e * 2048 + 1024 * half, 1024)],
                                    gu_parts[:, k.buf, 0, cols], ALU.subtract).then_inc(gu_low, 1)

            def step_routed(k, last=False):
                activate(k)
                if not last:
                    low_rows(k.plus(1))
                if k.first == SEQS:
                    result(k.plus(-1))
                low_down(k)
                if k.first == SEQS:
                    dve.wait_ge(y_ready, SEQS)
                    low_gate_up(k.plus(1), (1,))
                if not (isinstance(k.n, int) and k.n + 2 >= SEQS + BLOCKS):
                    low_gate_up(k.plus(2))
                low_act(k)

            def step_experts(k):
                activate(k)
                result(k.plus(-1))

            routing_choice()
            dve.wait_ge(spare_stored, 16)
            for k in range(1, 5):
                step_experts(Turn(k, 0, 2))
            copy_ranks()
            step_experts(Turn(5, 0, 2))
            copy_counts()
            routing_gates()
            step_experts(Turn(6, 0, 2))
            routing_slots()
            step_experts(Turn(7, 0, 2))
            routing_blocks()
            with dve.Fori(0, 2) as trip:
                for k in range(2):
                    routing_chunk(Turn(k, trip, 2).n)
                    step_experts(Turn(8 + k, trip, 2))
            routing_tables()
            for k in range(12, 14):
                step_experts(Turn(k, 0, 2))
            step_experts(Turn(14, 0, 2))
            dve.wait_ge(tables_ready, 1)
            low_gate_up(Turn(SEQS, 0, 2))
            step_experts(Turn(15, 0, 2))
            low_rows(Turn(SEQS, 0, 2))
            dve.wait_ge(y_ready, SEQS - 2)
            low_gate_up(Turn(SEQS + 1, 0, 2), (0,))
            for k in range(3):
                step_routed(Turn(SEQS + k, 0, 2))
            with dve.Fori(0, (BLOCKS - 5) // 2) as trip:
                for k in range(2):
                    step_routed(Turn(SEQS + 3 + k, trip, 2))
            step_routed(Turn(SEQS + BLOCKS - 2, 0, 2))
            step_routed(Turn(SEQS + BLOCKS - 1, 0, 2), True)


def constants():
    import numpy as np

    r, c = np.arange(P)[:, None], np.arange(P)[None, :]
    f = np.zeros((P, C_END), np.float32)
    f[:, C_ID:C_ID + P] = r == c
    f[:, C_IOTA:C_IOTA + P] = c
    f[:, C_REV:C_REV + EXPERTS] = EXPERTS - np.arange(EXPERTS)
    f[:, C_TILE:C_TILE + 32] = np.arange(32) % SEQS
    f[:, C_ONE:C_ONE + EXPERTS] = 1.0
    f[:, C_ROW1] = np.arange(P) + 1
    f[:, C_SPARE] = np.arange(P) + TOKENS + 1
    f[:, C_HALF] = -0.5
    b = np.zeros((P, B_END), np.float32)
    b[:, B_ID:B_ID + P] = r == c
    off = np.arange(2 * P)[None, :] - r
    b[:, B_MASK:B_MASK + 2 * P] = np.where((off >= 0) & (off <= 2 * LOCAL), 0.0, MASKED)
    b[:, B_TRI:B_TRI + P] = r < c
    for g in range(2):
        b[:3 * HEADS, B_SEL + P * g:B_SEL + P * g + P] = (r % HEADS == 4 * g + c // 32)[:3 * HEADS]
    b[:, B_ONES:B_ONES + P] = 1.0
    return f, b


def kernel(**inputs):
    import numpy as np
    import concourse.bacc as bacc
    from concourse.bass_utils import run_bass_kernel_spmd

    a = {k: np.asarray(v) for k, v in inputs.items()}
    w_in, b_in, w_out = a["L0_xattn_w_in"], a["L0_xattn_b_in"], a["L0_xattn_w_out"]
    w_small = np.zeros((P, W_END), np.float32)
    for i, col in enumerate((W_Q, W_K)):
        w = w_in[P * i:P * i + P].reshape(HEADS, D, P).transpose(1, 0, 2).reshape(P, P)
        w_small[:, col:col + P] = w.T
        w_small[:, W_BIAS + i] = b_in[P * i:P * i + P].reshape(HEADS, D).T.reshape(P)
    w_small[:, W_V:W_V + P] = w_in[2 * P:3 * P].T
    for h in range(HEADS):
        g, row = h // 4, 32 * (h % 4)
        w_small[row:row + D, W_O + P * g:W_O + P * g + P] = w_out[:, D * h:D * h + D].T
        w_small[row:row + D, BV0 + g] = b_in[2 * P + D * h:2 * P + D * h + D]
    w_small[:, W_CT:W_CT + P] = a["L0_xattn_w_ct"]
    w_small[:, W_R:W_R + 64] = a["L0_ffn_Wr"].reshape(EXPERTS, 4, P).transpose(2, 1, 0).reshape(P, 64)
    w_small[:, BO] = a["L0_xattn_b_out"]
    w_small[:, BCT] = a["L0_xattn_b_ct"]
    w_small[:EXPERTS, BR] = a["L0_ffn_bias"]

    gu = np.concatenate([a["L0_ffn_Wg"], a["L0_ffn_Wu"]], axis=2)
    sgu = np.concatenate([a["L0_ffn_sWg"], a["L0_ffn_sWu"]], axis=1)
    const_f, const_b = constants()
    arrays = {
        "x": a["x"], "ctx": a["ctx_2048"], "const_f": const_f, "const_b": const_b, "w_small": w_small,
        "w_gu": gu.reshape(EXPERTS, 4, P, 512).transpose(2, 0, 1, 3).reshape(P, EXPERTS, 2048),
        "w_d": a["L0_ffn_Wd"].reshape(EXPERTS, 2, P, T).transpose(0, 2, 1, 3).reshape(EXPERTS, P, 2 * T),
        "sw_gu": sgu.reshape(4, P, 512).transpose(1, 0, 2),
        "sw_d": a["L0_ffn_sWd"].reshape(2, P, T).transpose(1, 0, 2),
    }
    arrays = {k: np.ascontiguousarray(v) for k, v in arrays.items()}
    nc = bacc.Bacc("TRN2", target_bir_lowering=False, num_devices=1)
    args = [nc.dram_tensor(k, v.shape, mybir.dt.from_np(v.dtype), kind="ExternalInput").ap()
            for k, v in arrays.items()]
    out = nc.dram_tensor("out", (SEQS + 1, P, T), F32, kind="ExternalOutput").ap()
    xattn_moe_kernel(nc, *args, out)
    result = run_bass_kernel_spmd(nc, [arrays], core_ids=[0])
    return result.results[0]["out"][:SEQS]
```
